# Optimizing a Trainium2 kernel written in Bass

```python
import numpy as np
import jax
import jax.numpy as jnp

def _softmax(x, axis=-1):
    return jax.nn.softmax(x, axis=axis)

def _gelu(x):
    return jax.nn.gelu(x, approximate=True)

def _silu(x):
    return jax.nn.silu(x)

def _sigmoid(x):
    return jax.nn.sigmoid(x)

def _layernorm(x, axis=-1, eps=1e-05):
    m = jnp.mean(x, axis=axis, keepdims=True)
    v = jnp.var(x, axis=axis, keepdims=True)
    return (x - m) / jnp.sqrt(v + eps)

def _scatter_add(tgt, idx, src, axis=0):
    return tgt.at[idx].add(src)

def _segment_sum(src, seg, n):
    return jax.ops.segment_sum(src, seg, n)
kernel_name = 'mk_audio_tower_d1_tok_audfeat1024_r4_6f4d16'

def setup_inputs(seed: int=0):
    np.random.seed(seed)
    _w = jnp.asarray

    def _rec_inputs():
        import jax
        import jax.numpy as jnp
        _rk = jax.random.key(seed)
        x = -0.000125008 + 0.999885 * jax.random.normal(jax.random.fold_in(_rk, 1), (8, 750, 256), jnp.float32)
        return x
    x = _rec_inputs()

    def _L0_tok_setup():
        import jax, jax.numpy as jnp
        import numpy as np
        D_MODEL = 256
        STRIDE = 2
        KERNEL = 2
        INIT_STD = 0.02
        EPS = 1e-05
        key = jax.random.key(seed)
        k1, k2 = jax.random.split(key)
        hidden_states = jax.random.normal(k1, (4, 2048, D_MODEL), dtype=jnp.float32)
        conv_w = INIT_STD * jax.random.normal(k2, (D_MODEL, D_MODEL, KERNEL), dtype=jnp.float32)
        conv_b = jnp.zeros((D_MODEL,), dtype=jnp.float32)
        ln_gamma = jnp.ones((D_MODEL,), dtype=jnp.float32)
        ln_beta = jnp.zeros((D_MODEL,), dtype=jnp.float32)
        return {'hidden_states': hidden_states, 'conv_w': conv_w, 'conv_b': conv_b, 'ln_gamma': ln_gamma, 'ln_beta': ln_beta}
    _L0_tok_all = _L0_tok_setup()
    _L0_tok_in = {k: v for k, v in _L0_tok_all.items() if k in ('conv_w', 'conv_b', 'ln_gamma', 'ln_beta')}
    del _L0_tok_all

    def _L0_attn_setup():
        import jax, jax.numpy as jnp
        import numpy as np
        B, S, HID = (2, 512, 256)
        NH, NKV, D = (16, 4, 64)
        SCALE = 1.0 / np.sqrt(D).astype(np.float32)
        SOFTCAP = 30.0
        WINDOW = 256
        NEG = -1e+30
        key = jax.random.key(seed)
        kx, kq, kk, kv, ko = jax.random.split(key, 5)
        std = 0.02
        return {'x': jax.random.normal(kx, (B, S, HID), jnp.float32), 'Wq': jax.random.normal(kq, (NH * D, HID), jnp.float32) * std, 'Wk': jax.random.normal(kk, (NKV * D, HID), jnp.float32) * std, 'Wv': jax.random.normal(kv, (NKV * D, HID), jnp.float32) * std, 'Wo': jax.random.normal(ko, (HID, NH * D), jnp.float32) * std}
    _L0_attn_all = _L0_attn_setup()
    _L0_attn_in = {k: v for k, v in _L0_attn_all.items() if k in ('Wq', 'Wk', 'Wv', 'Wo')}
    del _L0_attn_all

    def _L0_ffn_setup():
        import jax, jax.numpy as jnp
        import numpy as np
        B, S, D = (2, 256, 256)
        E, H, K, G = (8, 512, 2, 64)
        key = jax.random.key(seed)
        ks = jax.random.split(key, 5)
        return {'x': jax.random.normal(ks[0], (B, S, D), jnp.float32), 'wg1': jax.random.normal(ks[1], (D, G), jnp.float32) * 0.02, 'bg1': jnp.zeros((G,), jnp.float32), 'wg2': jax.random.normal(ks[2], (G, E), jnp.float32) * 0.02, 'w_in': jax.random.uniform(ks[3], (E, D, H), jnp.float32, -1.0 / D, 1.0 / D), 'w_out': jax.random.uniform(ks[4], (E, H, D), jnp.float32, -1.0 / H, 1.0 / H)}
    _L0_ffn_all = _L0_ffn_setup()
    _L0_ffn_in = {k: v for k, v in _L0_ffn_all.items() if k in ('wg1', 'bg1', 'wg2', 'w_in', 'w_out')}
    del _L0_ffn_all
    return {'x': x, 'L0_tok_conv_w': _L0_tok_in['conv_w'], 'L0_tok_conv_b': _L0_tok_in['conv_b'], 'L0_tok_ln_gamma': _L0_tok_in['ln_gamma'], 'L0_tok_ln_beta': _L0_tok_in['ln_beta'], 'L0_attn_Wq': _L0_attn_in['Wq'], 'L0_attn_Wk': _L0_attn_in['Wk'], 'L0_attn_Wv': _L0_attn_in['Wv'], 'L0_attn_Wo': _L0_attn_in['Wo'], 'L0_ffn_wg1': _L0_ffn_in['wg1'], 'L0_ffn_bg1': _L0_ffn_in['bg1'], 'L0_ffn_wg2': _L0_ffn_in['wg2'], 'L0_ffn_w_in': _L0_ffn_in['w_in'], 'L0_ffn_w_out': _L0_ffn_in['w_out']}

def reference(x, L0_tok_conv_w, L0_tok_conv_b, L0_tok_ln_gamma, L0_tok_ln_beta, L0_attn_Wq, L0_attn_Wk, L0_attn_Wv, L0_attn_Wo, L0_ffn_wg1, L0_ffn_bg1, L0_ffn_wg2, L0_ffn_w_in, L0_ffn_w_out):
    import jax
    import jax.numpy as jnp

    def _L0_tok_ref(hidden_states, conv_w, conv_b, ln_gamma, ln_beta):
        import jax, jax.numpy as jnp
        import numpy as np
        D_MODEL = 256
        STRIDE = 2
        KERNEL = 2
        INIT_STD = 0.02
        EPS = 1e-05
        B, L, D = hidden_states.shape
        pad_len = -L % STRIDE
        if pad_len:
            hidden_states = jnp.pad(hidden_states, ((0, 0), (0, pad_len), (0, 0)))
            L = L + pad_len
        xb = hidden_states.reshape(B, L // STRIDE, STRIDE, D)
        x = jnp.einsum('btki,oik->bto', xb, conv_w) + conv_b
        x = x + xb.mean(axis=2)
        mu = x.mean(axis=-1, keepdims=True)
        var = jnp.mean(jnp.square(x - mu), axis=-1, keepdims=True)
        x = (x - mu) * jax.lax.rsqrt(var + EPS) * ln_gamma + ln_beta
        return x

    def _L0_attn_ref(x, Wq, Wk, Wv, Wo):
        import jax, jax.numpy as jnp
        import numpy as np
        B, S, HID = (2, 512, 256)
        NH, NKV, D = (16, 4, 64)
        SCALE = 1.0 / np.sqrt(D).astype(np.float32)
        SOFTCAP = 30.0
        WINDOW = 256
        NEG = -1e+30
        b, s, _ = x.shape
        n_rep = NH // NKV
        q = (x @ Wq.T).reshape(b, s, NH, D)
        k = (x @ Wk.T).reshape(b, s, NKV, D)
        v = (x @ Wv.T).reshape(b, s, NKV, D)
        k = jnp.repeat(k, n_rep, axis=2)
        v = jnp.repeat(v, n_rep, axis=2)
        scores = jnp.einsum('bqhd,bkhd->bhqk', q, k) * SCALE
        scores = SOFTCAP * jnp.tanh(scores / SOFTCAP)
        i = jnp.arange(s)[:, None]
        j = jnp.arange(s)[None, :]
        mask = (j <= i) & (j > i - WINDOW)
        scores = jnp.where(mask, scores, NEG)
        p = jax.nn.softmax(scores, axis=-1)
        o = jnp.einsum('bhqk,bkhd->bqhd', p, v).reshape(b, s, NH * D)
        return o @ Wo.T

    def _L0_ffn_ref(x, wg1, bg1, wg2, w_in, w_out):
        import jax, jax.numpy as jnp
        import numpy as np
        B, S, D = (2, 256, 256)
        E, H, K, G = (8, 512, 2, 64)
        b, s, d = x.shape
        xt = x.reshape(-1, d)
        n = xt.shape[0]
        g = jax.nn.gelu(xt @ wg1 + bg1, approximate=False)
        logits = g @ wg2
        probs = jax.nn.softmax(logits, axis=-1)
        top_vals, top_idx = jax.lax.top_k(probs, K)
        gates = jnp.zeros_like(probs).at[jnp.arange(n)[:, None], top_idx].set(top_vals)
        h = jax.nn.gelu(jnp.einsum('nd,edh->enh', xt, w_in), approximate=False)
        o = jnp.einsum('enh,ehd->end', h, w_out)
        y = jnp.einsum('ne,end->nd', gates, o)
        return y.reshape(b, s, d)
    h = _L0_tok_ref(x, L0_tok_conv_w, L0_tok_conv_b, L0_tok_ln_gamma, L0_tok_ln_beta)
    h = h + _L0_attn_ref(_layernorm(h, axis=-1), L0_attn_Wq, L0_attn_Wk, L0_attn_Wv, L0_attn_Wo)
    h = h + _L0_ffn_ref(_layernorm(h, axis=-1), L0_ffn_wg1, L0_ffn_bg1, L0_ffn_wg2, L0_ffn_w_in, L0_ffn_w_out)
    return h

_drawn_inputs = setup_inputs


def setup_inputs(seed=0):
    import zlib

    import numpy as np

    out = dict(_drawn_inputs(seed))
    spreads = {'L0_tok_conv_b': (0.0, 0.1),
     'L0_tok_ln_gamma': (1.0, 0.2),
     'L0_tok_ln_beta': (0.0, 0.1),
     'L0_ffn_bg1': (0.0, 2.0)}
    factors = {'L0_attn_Wq': 8.0,
     'L0_attn_Wk': 8.0,
     'L0_ffn_wg1': 27.039,
     'L0_ffn_wg2': 21.711,
     'L0_ffn_w_in': 8.0,
     'L0_ffn_w_out': 8.0}
    for name, (base, spread) in spreads.items():
        noise = np.random.default_rng([zlib.crc32(name.encode()), seed]).standard_normal(out[name].shape)
        drawn = base * np.exp(spread * noise) if base else spread * noise
        out[name] = jnp.asarray(drawn.astype(out[name].dtype))
    for name, factor in factors.items():
        out[name] = (out[name] * factor).astype(out[name].dtype)
    return out
```

```python
import concourse.bass as bass
from concourse import mybir
from contextlib import ExitStack

F32 = mybir.dt.float32
F32R = mybir.dt.float32r
I32 = mybir.dt.int32
U32 = mybir.dt.uint32
ALU = mybir.AluOpType
ACT = mybir.ActivationFunctionType
AX = mybir.AxisListType

BATCHES, FRAMES, DM = 8, 750, 256
SEQ = FRAMES // 2
P = 128
TT = -(-SEQ // P)
LAST = SEQ - (TT - 1) * P
QW = SEQ + SEQ % 2
TOK = BATCHES * SEQ
HEADS, KV, HD = 16, 4, 64
PAIRS = HEADS // 2
WINDOW = 256
SOFTCAP = 30.0
SCALE = HD ** -0.5
EPS = 1e-5
EXPERTS, HID, TOPK, GATE = 8, 512, 2, 64
CAP = TOK + P
ROW = DM + 2
FT = (TOK * TOPK + EXPERTS * (P - 1)) // P
NOWHERE = EXPERTS * CAP
OFF = 1 << 20
UNROLL = 6
assert FT % UNROLL == 0 and TT == 3 and SEQ <= WINDOW + P

W0, W1, W2 = QW, QW - P, QW - 2 * P
REG = W0 + W2
assert REG == 2 * W1 and REG <= 512
LAG = 2
NP_ = 4

QKV = [f"q{j}" for j in range(PAIRS)] + ["k0", "k1", "v0", "v1", "v2"]
WO = ["w0", "w1", "w2"]
XT = ["xt0", "xt1", "xt2"]
CV = ["cv0", "cv1", "cv2"]
X2T = ["x2t0", "x2t1"]
XNT = ["xnt0", "xnt1"]
RK = ["tri", "tot"]


def jobs_of(back, front, attention=True):
    out = list(QKV) if attention else []
    out += WO if back else []
    out += XT + CV if front else []
    out += X2T + ["g", "l"] if back else []
    out += RK if back else []
    out += XNT if front else []
    return out


PER_TURN = len(jobs_of(True, True))
assert PER_TURN % 3 == 0
PROLOGUE = XT + CV + XNT
FIRST_JOB = PER_TURN - len(PROLOGUE) - len(jobs_of(False, True))


class Turn:

    def __init__(self, b):
        self.b = b
        self.attention = not (isinstance(b, int) and b in (-1, BATCHES))
        self.back = not (isinstance(b, int) and b <= 0)
        self.front = not (isinstance(b, int) and b >= BATCHES - 1)
        if isinstance(b, int) and b == -1:
            names, self.base = PROLOGUE, FIRST_JOB
        elif isinstance(b, int) and b == 0:
            names, self.base = jobs_of(False, True), FIRST_JOB + len(PROLOGUE)
        elif isinstance(b, int) and b == BATCHES:
            names, self.base = jobs_of(True, False, False), PER_TURN * (BATCHES - 1) + len(jobs_of(True, False))
        else:
            names, self.base = jobs_of(True, self.front), b * PER_TURN
        start = 0 if not isinstance(self.base, int) else self.base % 3
        self.local = {name: k for k, name in enumerate(names)}
        self.bank_start = start

    def bank(self, name):
        return (self.bank_start + self.local[name]) % 3

    def before(self, name):
        return self.base + (self.local[name] - FIRST_JOB)

    def upto(self, name):
        return self.base + (self.local[name] - FIRST_JOB + 1)


def turns(engine_loop, body):
    body(Turn(0))
    with engine_loop(1, BATCHES - 1) as b:
        body(Turn(b))
    body(Turn(BATCHES - 1))


def front_done(b):
    return Turn(b).base - FIRST_JOB


class Link:

    def __init__(self, sem, engine):
        self.sem, self.engine, self.n = sem, engine, 0

    def __call__(self, instruction):
        instruction.then_inc(self.sem, 1)
        self.n = self.n + 1
        self.engine.wait_ge(self.sem, self.n)


def build(nc, x, conv_w, conv_b, gamma, beta, wq, wk, wv, wo, wg1, bg1, wg2, w_in, w_out, xs, ys, out):
    ctx = ExitStack()
    with ctx:
        def sem(name):
            return ctx.enter_context(nc.semaphore(name))

        def sb(stack, name, shape, dt=F32):
            return stack.enter_context(nc.sbuf_tensor(name, shape, dt))

        keep = ctx
        h_all = sb(keep, "h_all", [P, BATCHES * TT * DM])
        payload = sb(keep, "payload", [P, TOPK, TT, ROW])
        x2t = sb(keep, "x2t", [P, 2, TT * P])
        gate_t = sb(keep, "gate_t", [GATE, TT * P])
        wg1_sb = sb(keep, "wg1_sb", [P, 2, GATE])
        bg1_sb = sb(keep, "bg1_sb", [GATE, 1])
        wg2_sb = sb(keep, "wg2_sb", [GATE, EXPERTS])
        ident = sb(keep, "ident", [P, P])
        before_m = sb(keep, "before_m", [P, P])
        ones_m = sb(keep, "ones_m", [P, P])
        stats3 = sb(keep, "stats3", [P, TT, 6])
        mv3 = sb(keep, "mv3", [P, TT, 2])
        ve3 = sb(keep, "ve3", [P, TT])
        rstd3 = sb(keep, "rstd3", [P, TT])
        minus_half = sb(keep, "minus_half", [P, TT])
        mx = sb(keep, "mx", [P, TT, 1])
        shifted = sb(keep, "shifted", [P, TT, EXPERTS])
        expd = sb(keep, "expd", [P, TT, EXPERTS])
        denom = sb(keep, "denom", [P, TT, 1])
        rdenom = sb(keep, "rdenom", [P, TT, 1])
        probs = sb(keep, "probs", [P, TT, EXPERTS])
        top8 = sb(keep, "top8", [P, TT, 8])
        idx8 = sb(keep, "idx8", [P, TT, 8], U32)
        idxf = sb(keep, "idxf", [P, TT, TOPK])
        iota8 = sb(keep, "iota8", [P, TT, EXPERTS])
        hot0 = sb(keep, "hot0", [P, TT, EXPERTS])
        hot1 = sb(keep, "hot1", [P, TT, EXPERTS])
        hots = sb(keep, "hots", [P, TT, EXPERTS])
        chosen = sb(keep, "chosen", [P, TT, EXPERTS])
        valid8 = sb(keep, "valid8", [P, TT, EXPERTS])
        beyond = sb(keep, "beyond", [P, TT, TOPK])
        carry = sb(keep, "carry", [P, TT + 1, EXPERTS])
        carry0 = sb(keep, "carry0", [P, EXPERTS])
        rank = sb(keep, "rank", [P, TT, EXPERTS])
        pick0 = sb(keep, "pick0", [P, TT, EXPERTS])
        pick1 = sb(keep, "pick1", [P, TT, EXPERTS])
        slotf = sb(keep, "slotf", [P, TT, TOPK])
        slotg = sb(keep, "slotg", [P, TT, TOPK])
        slot = sb(keep, "slot", [P, TT, TOPK], I32)
        place = sb(keep, "place", [P, TT, TOPK])
        padf = sb(keep, "padf", [P, EXPERTS])
        padi = sb(keep, "padi", [P, EXPERTS], I32)
        iota_p = sb(keep, "iota_p", [P, 1])
        cntf = sb(keep, "cntf", [P, EXPERTS])
        cnti = sb(keep, "cnti", [P, EXPERTS], I32)
        cnts = sb(keep, "cnts", [P, EXPERTS], I32)
        tilesf = sb(keep, "tilesf", [P, EXPERTS])
        ends = sb(keep, "ends", [P, EXPERTS])
        lag_rows = sb(keep, "lag_rows", [P, EXPERTS])
        iota_j = sb(keep, "iota_j", [1, FT])
        tile_j = sb(keep, "tile_j", [1, FT])
        total1 = sb(keep, "total1", [1, 1])
        over = sb(keep, "over", [1, FT, EXPERTS])
        overw = sb(keep, "overw", [1, FT, EXPERTS])
        expf = sb(keep, "expf", [1, FT])
        rowf = sb(keep, "rowf", [1, FT])
        rowg = sb(keep, "rowg", [1, FT])
        past = sb(keep, "past", [1, FT])
        rowh = sb(keep, "rowh", [1, FT])
        table = sb(keep, "table", [1, 2, FT], I32)
        pad_rows = sb(keep, "pad_rows", [P, ROW])
        tick_dve = sb(keep, "tick_dve", [1, 1])
        tick_pool = sb(keep, "tick_pool", [1, 1])
        eps_c = sb(keep, "eps_c", [P, TT])

        early = ExitStack()
        x_sb = sb(early, "x_sb", [P, TT, 2 * DM])
        xsum = sb(early, "xsum", [P, TT, DM])
        bias2 = sb(early, "bias2", [P, DM])
        gamma_b = sb(early, "gamma_b", [P, DM])
        beta_b = sb(early, "beta_b", [P, DM])
        xth = sb(early, "xth", [P, TT, 2 * DM], F32R)
        xtl = sb(early, "xtl", [P, TT, 2 * DM], F32R)
        y_sb = sb(early, "y_sb", [P, TT, DM])
        xn = sb(early, "xn", [P, TT, DM])
        stats = sb(early, "stats", [P, TT, 6])
        mv1 = sb(early, "mv1", [P, TT, 2])
        ve1 = sb(early, "ve1", [P, TT])
        rstd1 = sb(early, "rstd1", [P, TT])
        mv2 = sb(early, "mv2", [P, TT, 2])
        ve2 = sb(early, "ve2", [P, TT])
        rstd2 = sb(early, "rstd2", [P, TT])
        xnh = sb(early, "xnh", [P, 2, TT * P], F32R)
        xnl = sb(early, "xnl", [P, 2, TT * P], F32R)
        qh = sb(early, "qh", [P, PAIRS, QW], F32R)
        ql = sb(early, "ql", [P, PAIRS, QW], F32R)
        kh = sb(early, "kh", [P, KV, TT * P], F32R)
        kl = sb(early, "kl", [P, KV, TT * P], F32R)
        vo = sb(early, "vo", [P, TT, KV, P])
        prob = sb(early, "prob", [P, NP_, 3 * REG])
        recip = sb(early, "recip", [P, QW])
        ot = sb(early, "ot", [P, PAIRS, QW])
        cwh = sb(early, "cwh", [P, 4, DM], F32R)
        cwl = sb(early, "cwl", [P, 4, DM], F32R)
        wqh = sb(early, "wqh", [P, 2, HEADS * HD], F32R)
        wql = sb(early, "wql", [P, 2, HEADS * HD], F32R)
        wkvh = sb(early, "wkvh", [P, 2, 2, KV * HD], F32R)
        wkvl = sb(early, "wkvl", [P, 2, 2, KV * HD], F32R)
        wo_sb = sb(early, "wo_sb", [P, PAIRS, DM])
        causal = sb(early, "causal", [P, P])
        win_causal = sb(early, "win_causal", [P, 2 * W2])
        early.close()

        late = ExitStack()
        wih = sb(late, "wih", [P, EXPERTS * 2 * HID], F32R)
        wil = sb(late, "wil", [P, EXPERTS * 2 * HID], F32R)
        woh = sb(late, "woh", [P, EXPERTS * 4 * DM], F32R)
        wol = sb(late, "wol", [P, EXPERTS * 4 * DM], F32R)
        raw = sb(late, "raw", [P, 2, 2 * HID])
        xt_rows = sb(late, "xt_rows", [P, UNROLL, ROW])
        fxh = sb(late, "fxh", [P, 2, 2 * P], F32R)
        fxl = sb(late, "fxl", [P, 2, 2 * P], F32R)
        act_h = sb(late, "act_h", [P, 2, HID])
        fhh = sb(late, "fhh", [P, 2, HID], F32R)
        fhl = sb(late, "fhl", [P, 2, HID], F32R)
        y_rows = sb(late, "y_rows", [P, 3, DM])
        late.close()
        final = ExitStack()
        fin_in = sb(final, "fin_in", [P, 2, TT, 2 * DM])
        fin_out = sb(final, "fin_out", [P, 2, TT, DM])
        final.close()

        ps = ctx.enter_context(nc.psum_tensor("ps", [P, 8, 512], F32))
        S_BANK, O_BANK, G_BANK = 0, 3, 5

        weights_in = [sem(f"weights_in{i}") for i in range(3)]
        consts_in = sem("consts_in")
        x_in = sem("x_in")
        x_summed = sem("x_summed")
        consts = sem("consts")
        split_hi = sem("split_hi")
        split_lo = sem("split_lo")
        filled = sem("filled")
        drained = sem("drained")
        hi_done = sem("hi_done")
        scores = sem("scores")
        capped = sem("capped")
        exped = sem("exped")
        masked = sem("masked")
        pv_done = sem("pv_done")
        normed = sem("normed")
        xsum_ready = sem("xsum_ready")
        var_ready = [sem(f"var_ready{i}") for i in range(3)]
        rstd_ready = [sem(f"rstd_ready{i}") for i in range(3)]
        z_ready = sem("z_ready")
        h1_ready = sem("h1_ready")
        xn_ready = sem("xn_ready")
        xn2_ready = sem("xn2_ready")
        copy_ready = sem("copy_ready")
        x2t_ready = sem("x2t_ready")
        gate_ready = sem("gate_ready")
        shift_ready = sem("shift_ready")
        expd_ready = sem("expd_ready")
        chosen_ready = sem("chosen_ready")
        slots_ready = sem("slots_ready")
        scattered = sem("scattered")
        dve_link = sem("dve_link")
        pool_link = sem("pool_link")
        pad_ready = sem("pad_ready")
        ticked = sem("ticked")
        pad_done = sem("pad_done")
        table_ready = sem("table_ready")
        raw_in = [sem(f"raw_in{i}") for i in range(2)]
        exp_hi = sem("exp_hi")
        exp_lo = sem("exp_lo")
        rows_in = [sem(f"rows_in{i}") for i in range(UNROLL)]
        fx_filled = sem("fx_filled")
        fx_hi = sem("fx_hi")
        fx_lo = sem("fx_lo")
        fh_filled = sem("fh_filled")
        gelued = sem("gelued")
        ft_filled = sem("ft_filled")
        ft_hi = sem("ft_hi")
        ft_lo = sem("ft_lo")
        fy_filled = sem("fy_filled")
        fy_done = sem("fy_done")
        y_out = [sem(f"y_out{i}") for i in range(3)]
        fin_loaded = [sem(f"fin_loaded{i}") for i in range(2)]
        fin_clear = sem("fin_clear")
        fin_ready = sem("fin_ready")
        fin_stored = [sem(f"fin_stored{i}") for i in range(2)]

        block = ctx.enter_context(nc.Block())

        def general(turn, name, width=512):
            return ps[:, G_BANK + turn.bank(name), 0:width]

        def h_tile(b, t):
            return h_all[:, bass.ds((b * TT + t) * DM, DM)]

        def h_batch(b):
            return h_all[:, bass.ds(b * (TT * DM), TT * DM)].rearrange("p (t d) -> p t d", t=TT)

        stage = prob[:, :, :].rearrange("p n c -> p (n c)")
        ST_CONV, ST_Q = 0, 4 * DM
        ST_KV = ST_Q + 2 * HEADS * HD

        @block.sync
        def _(sp):
            def load_x(b):
                sp.dma_start(x_sb[:, 0:TT - 1, :],
                             x[bass.ds(b, 1), 0:(TT - 1) * P, :].rearrange("a (t p) f -> p (a t) f", p=P)
                             ).then_inc(x_in, 16)
                sp.dma_start(x_sb[0:LAST, TT - 1, :],
                             x[bass.ds(b, 1), (TT - 1) * P:SEQ, :].rearrange("a p f -> p (a f)")).then_inc(x_in, 16)

            sp.wait_ge(consts, 1)
            load_x(0)
            sp.dma_start(stage[:, ST_CONV:ST_Q].rearrange("p (c o) -> p c o", c=4),
                         conv_w.rearrange("(c p) o -> p c o", p=P)).then_inc(weights_in[0], 16)
            sp.dma_start(stage[:, ST_Q:ST_KV].rearrange("p (c o) -> p c o", c=2),
                         wq.rearrange("(c p) o -> p c o", p=P)).then_inc(weights_in[1], 16)
            for i, w in enumerate((wk, wv)):
                at = ST_KV + i * 2 * KV * HD
                sp.dma_start(stage[:, at:at + 2 * KV * HD].rearrange("p (c o) -> p c o", c=2),
                             w.rearrange("(c p) o -> p c o", p=P)).then_inc(weights_in[1], 16)
            sp.dma_start(wo_sb[:, :, :], wo.rearrange("(c p) o -> p c o", p=P)).then_inc(weights_in[2], 16)
            sp.dma_start(wg1_sb[:, :, :], wg1.rearrange("(c p) o -> p c o", p=P)).then_inc(weights_in[2], 16)
            sp.dma_start(wg2_sb[:, :], wg2).then_inc(weights_in[2], 16)
            sp.dma_start(bg1_sb[:, :], bg1.rearrange("(g a) -> g a", a=1)).then_inc(weights_in[2], 16)

            def next_x(b):
                sp.wait_ge(drained, Turn(b - 2).upto(XT[-1]))
                sp.wait_ge(x_summed, b)
                load_x(b)

            next_x(1)
            next_x(2)
            with sp.Fori(3, BATCHES) as b:
                next_x(b)

            last = Turn(BATCHES)
            sp.wait_ge(filled, last.upto("w2"))
            sp.wait_ge(drained, last.upto("w2"))
            for e in range(EXPERTS):
                for half, w in enumerate((w_in, w_out)):
                    if e >= 1:
                        sp.wait_ge(exp_lo, 2 * (e - 1) + half + 1)
                    c = 2 if half == 0 else 4
                    sp.dma_start(raw[:, half, :].rearrange("p (c o) -> p c o", c=c),
                                 w[e, :, :].rearrange("(c p) o -> p c o", p=P)).then_inc(raw_in[half], 16)

            sp.wait_ge(table_ready, 1)
            sp.wait_ge(pad_done, 16 * (EXPERTS + 1))
            sp.wait_ge(scattered, 16 * TOPK * TT * BATCHES)

            def load_rows(j, u, reuse):
                row = sp.value_load(table[0:1, 1, bass.ds(j, 1)], min_val=0, max_val=NOWHERE)
                if reuse is not None:
                    sp.wait_ge(y_out[u % 3], reuse)
                sp.dma_start(xt_rows[:, u, :], xs[bass.ds(row, P), :]).then_inc(rows_in[u], 16)

            for u in range(UNROLL):
                load_rows(u, u, None)
            with sp.Fori(1, FT // UNROLL) as i:
                for u in range(UNROLL):
                    load_rows(i * UNROLL + u, u, i * 32 - 16 + 16 * (u // 3))

            sp.wait_ge(fin_clear, 1)
            for u in range(3):
                sp.wait_ge(y_out[u], 16 * (FT // 3))
            for b in range(BATCHES):
                if b >= 2:
                    sp.wait_ge(fin_ready, b - 1)
                sp.dma_start(fin_in[:, b % 2, 0:TT - 1, :],
                             ys[b * SEQ:b * SEQ + (TT - 1) * P, :].rearrange("(t p) f -> p t f", p=P)
                             ).then_inc(fin_loaded[b % 2], 16)
                sp.dma_start(fin_in[0:LAST, b % 2, TT - 1, :],
                             ys[b * SEQ + (TT - 1) * P:(b + 1) * SEQ, :]).then_inc(fin_loaded[b % 2], 16)

        @block.gpsimd
        def _(pool):
            g = nc.gpsimd
            link = Link(pool_link, pool)

            def tick(before):
                if not isinstance(before, int) or before > 0:
                    pool.wait_ge(ticked, before)
                g.tensor_tensor(tick_pool[:, :], eps_c[0:1, 0:1], eps_c[0:1, 0:1], ALU.add).then_inc(ticked, 1)

            g.memset(x_sb[:, :, :], 0.0).then_inc(consts, 1)
            for src, dst in ((conv_b, bias2), (gamma, gamma_b), (beta, beta_b)):
                pool.dma_start(dst[:, :], src.partition_broadcast(P)).then_inc(consts_in, 16)
            g.memset(ident[:, :], 0.0)
            g.memset(ones_m[:, :], 1.0)
            g.memset(before_m[:, :], 1.0)
            g.memset(minus_half[:, :], -0.5)
            g.memset(eps_c[:, :], EPS)
            g.memset(tick_pool[:, :], 0.0)
            g.memset(causal[:, :], 1.0)
            g.memset(win_causal[:, :], 1.0)
            g.memset(kh[:, :, :].bitcast(F32), 0.0)
            g.memset(kl[:, :, :].bitcast(F32), 0.0)
            g.memset(vo[:, :, :, :], 1.0)
            g.memset(valid8[:, :, :], 1.0)
            g.memset(beyond[:, :, :], 0.0)
            g.memset(pad_rows[:, 0:DM], 0.0)
            g.memset(pad_rows[:, DM + 1:ROW], 0.0)
            g.memset(pad_rows[:, DM:DM + 1].bitcast(I32), OFF)
            g.iota(iota8[:, :, :], [[0, TT], [1, EXPERTS]], base=0, channel_multiplier=0,
                   allow_small_or_imprecise_dtypes=True)
            g.iota(place[:, :, :], [[TOPK * P, TT], [1, TOPK]], base=0, channel_multiplier=TOPK,
                   allow_small_or_imprecise_dtypes=True)
            g.iota(carry[:, 0, :], [[CAP, EXPERTS]], base=0, channel_multiplier=0,
                   allow_small_or_imprecise_dtypes=True)
            g.iota(carry0[:, :], [[CAP, EXPERTS]], base=0, channel_multiplier=0,
                   allow_small_or_imprecise_dtypes=True)
            g.iota(iota_p[:, :], [[0, 1]], base=0, channel_multiplier=1, allow_small_or_imprecise_dtypes=True)
            link(g.iota(iota_j[:, :], [[1, FT]], base=0, channel_multiplier=0,
                        allow_small_or_imprecise_dtypes=True))
            g.affine_select(out=ident[:, :], in_=ident[:, :], compare_op=ALU.not_equal, fill=1.0, base=0,
                            pattern=[[-1, P]], channel_multiplier=1)
            g.affine_select(out=before_m[:, :], in_=before_m[:, :], compare_op=ALU.is_ge, fill=0.0, base=-1,
                            pattern=[[1, P]], channel_multiplier=-1)
            g.affine_select(out=causal[:, :], in_=causal[:, :], compare_op=ALU.is_ge, fill=0.0, base=0,
                            pattern=[[1, P]], channel_multiplier=-1)
            g.affine_select(out=win_causal[:, W2:2 * W2], in_=win_causal[:, W2:2 * W2], compare_op=ALU.is_ge,
                            fill=0.0, base=0, pattern=[[1, W2]], channel_multiplier=-1)
            g.affine_select(out=win_causal[:, 0:W2], in_=win_causal[:, 0:W2], compare_op=ALU.is_ge, fill=0.0,
                            base=WINDOW - 1 - 2 * P, pattern=[[-1, W2]], channel_multiplier=1)
            g.affine_select(out=valid8[:, TT - 1, :], in_=valid8[:, TT - 1, :], compare_op=ALU.is_ge, fill=0.0,
                            base=LAST - 1, pattern=[[0, EXPERTS]], channel_multiplier=-1)
            pool.wait_ge(consts_in, 48)
            g.affine_select(out=beyond[:, TT - 1, :], in_=beyond[:, TT - 1, :], compare_op=ALU.is_ge,
                            fill=float(OFF), base=LAST - 1, pattern=[[0, TOPK]], channel_multiplier=-1)
            link(g.tensor_tensor(bias2[:, :], bias2[:, :], bias2[:, :], ALU.add))
            g.memset(carry[:, 1:, :], 0.0).then_inc(consts, 1)

            def rstd(which, mv, ve, r, count):
                pool.wait_ge(var_ready[which], count)
                link(g.tensor_tensor(ve[:, :], mv[:, :, 1], eps_c[:, :], ALU.add))
                g.tensor_tensor(r[:, :], ve[:, :], minus_half[:, :], ALU.pow).then_inc(rstd_ready[which], 1)

            def front_sum(b):
                pool.wait_ge(x_in, 32 * (b + 1))
                if not isinstance(b, int) or b > 0:
                    pool.wait_ge(z_ready, b)
                g.tensor_tensor(xsum[:, :, :], x_sb[:, :, 0:DM], x_sb[:, :, DM:2 * DM], ALU.add
                                ).then_inc(x_summed, 1)
                pool.wait_ge(x_summed, b + 1)
                g.tensor_tensor(xsum[:, :, :], xsum[:, :, :],
                                bias2[:, :].unsqueeze(1).to_broadcast([P, TT, DM]),
                                ALU.add).then_inc(xsum_ready, 1)

            def front_affine(b):
                pool.wait_ge(z_ready, b + 1)
                link(g.tensor_tensor(xsum[:, :, :], y_sb[:, :, :],
                                     gamma_b[:, :].unsqueeze(1).to_broadcast([P, TT, DM]), ALU.mult))
                g.tensor_tensor(h_batch(b), xsum[:, :, :],
                                beta_b[:, :].unsqueeze(1).to_broadcast([P, TT, DM]),
                                ALU.add).then_inc(h1_ready, 1)

            def front(b):
                rstd(0, mv1, ve1, rstd1, b + 1)
                front_affine(b)
                rstd(1, mv2, ve2, rstd2, b + 1)

            def dispatch(b):
                pool.wait_ge(slots_ready, b + 1)
                pool.wait_ge(copy_ready, b + 1)
                tick(b)
                for t in range(TT):
                    for k in range(TOPK):
                        g.indirect_dma_start(
                            out=xs, out_offset=bass.IndirectOffsetOnAxis(ap=slot[:, t, k:k + 1], axis=0),
                            in_=payload[:, k, t, :], in_offset=None,
                            bounds_check=EXPERTS * CAP - 1, oob_is_err=False).then_inc(scattered, 16)

            front_sum(0)
            front(0)

            def turn(tn):
                b = tn.b
                if tn.back:
                    rstd(2, mv3, ve3, rstd3, b)
                if tn.front:
                    front_sum(b + 1)
                    front(b + 1)
                if tn.back:
                    dispatch(b - 1)

            loop_links = 4
            turn(Turn(0))
            base = link.n
            with pool.Fori(1, BATCHES - 1) as b:
                link.n = (b - 1) * loop_links + base
                turn(Turn(b))
            link.n = base + loop_links * (BATCHES - 2)
            turn(Turn(BATCHES - 1))
            rstd(2, mv3, ve3, rstd3, BATCHES)
            dispatch(BATCHES - 1)

            g.dma_start(xs[NOWHERE:NOWHERE + P, :], pad_rows[:, :]).then_inc(pad_done, 16)
            pool.wait_ge(pad_ready, 1)
            for e in range(EXPERTS):
                g.indirect_dma_start(
                    out=xs, out_offset=bass.IndirectOffsetOnAxis(ap=padi[:, e:e + 1], axis=0),
                    in_=pad_rows[:, :], in_offset=None,
                    bounds_check=EXPERTS * CAP - 1, oob_is_err=False).then_inc(pad_done, 16)

            def scatter(j_done, u, fresh):
                pool.wait_ge(fy_done, j_done)
                tick(j_done + (BATCHES - 1))
                g.indirect_dma_start(
                    out=ys.rearrange("t (k d) -> (t k) d", k=TOPK),
                    out_offset=bass.IndirectOffsetOnAxis(ap=xt_rows[:, u, DM:DM + 1].bitcast(I32), axis=0),
                    in_=y_rows[:, u % 3, :], in_offset=None,
                    bounds_check=TOPK * TOK - 1, oob_is_err=False).then_inc(y_out[u % 3], 16)

            with pool.Fori(0, FT // UNROLL) as i:
                for u in range(UNROLL):
                    scatter(i * UNROLL + (u + 1), u, False)

        @block.scalar
        def _(act):
            s = nc.scalar
            F = ACT.Copy

            act.wait_ge(weights_in[0], 16)
            s.activation(cwh[:, :, :].rearrange("p c o -> p (c o)"), stage[:, ST_CONV:ST_Q], F
                         ).then_inc(split_hi, 1)

            def hi(tn, name, dst, width, src=None):
                act.wait_ge(filled, tn.upto(name))
                s.activation(dst, general(tn, name, width) if src is None else src, F).then_inc(hi_done, 1)

            def xt_hi(tn):
                for t in range(TT):
                    hi(tn, XT[t], xth[:, t, :], 512)

            def xnt_hi(tn):
                for c in range(2):
                    hi(tn, XNT[c], xnh[:, c, :], TT * P)

            xt_hi(Turn(-1))
            act.wait_ge(weights_in[1], 48)
            s.activation(wqh[:, :, :].rearrange("p c o -> p (c o)"), stage[:, ST_Q:ST_KV], F).then_inc(split_hi, 1)
            s.activation(wkvh[:, :, :, :].rearrange("p w c o -> p (w c o)"),
                         stage[:, ST_KV:ST_KV + 4 * KV * HD], F).then_inc(split_hi, 1)
            xnt_hi(Turn(-1))

            def turn(tn):
                b = tn.b
                for j in range(PAIRS):
                    hi(tn, f"q{j}", qh[:, j, :], QW)
                for c in range(2):
                    act.wait_ge(filled, tn.upto(f"k{c}"))
                    src = general(tn, f"k{c}", TT * P)
                    s.activation(kh[0:64, 2 * c, :], src[0:64, :], F)
                    s.activation(kh[64:128, 2 * c + 1, :], src[64:128, :], F).then_inc(hi_done, 1)
                for p in range(PAIRS):
                    n = b * PAIRS + p
                    if p == 0 and isinstance(b, int) and b == 0:
                        act.wait_ge(split_lo, 3)
                    act.wait_ge(scores, n + 1)
                    if not (isinstance(b, int) and b == 0 and p < NP_):
                        act.wait_ge(pv_done, 2 * n + (2 - 2 * NP_))
                    buf = prob[:, p % NP_, :]
                    s.activation(buf.rearrange("p (r c) -> p r c", r=3), ps[:, S_BANK:S_BANK + 3, 0:REG],
                                 ACT.Tanh, scale=SCALE / SOFTCAP).then_inc(capped, 1)
                    act.wait_ge(capped, n + 1)
                    s.activation(buf, buf, ACT.Exp, scale=SOFTCAP).then_inc(exped, 1)
                    if p == 1 and tn.front:
                        xt_hi(tn)
                    if p == 2 and tn.back:
                        copy_rows(b - 1)
                    if p == 3 and tn.back:
                        gate(tn)
                    if p == 4 and tn.back:
                        router_exp(b - 1)
                    if p == 6 and tn.front:
                        xnt_hi(tn)

            def copy_rows(b):
                act.wait_ge(xn2_ready, b + 1)
                s.activation(payload[:, 1, :, 0:DM], payload[:, 0, :, 0:DM], F).then_inc(copy_ready, 1)

            def gate(tn):
                act.wait_ge(filled, tn.upto("g"))
                s.activation(gate_t[:, :], general(tn, "g", TT * P)[0:GATE, :], ACT.Gelu,
                             bias=bg1_sb[:, 0:1]).then_inc(gate_ready, 1)

            def router_exp(b):
                act.wait_ge(shift_ready, b + 1)
                s.activation(expd[:, :, :], shifted[:, :, :], ACT.Exp).then_inc(expd_ready, 1)

            turns(act.Fori, turn)

            def expert_hi(e):
                for half, dst in enumerate((wih, woh)):
                    act.wait_ge(raw_in[half], 16 * (e + 1))
                    s.activation(dst[:, e * 1024:(e + 1) * 1024], raw[:, half, :], F).then_inc(exp_hi, 1)

            last = Turn(BATCHES)
            copy_rows(BATCHES - 1)
            gate(last)
            router_exp(BATCHES - 1)
            for e in range(EXPERTS):
                expert_hi(e)

            def fx_high(n, u):
                act.wait_ge(fx_filled, n + 1)
                s.activation(fxh[:, u % 2, :], ps[:, u % 2, 0:2 * P], F).then_inc(fx_hi, 1)

            def gelu(n, u):
                act.wait_ge(fh_filled, n + 1)
                s.activation(act_h[:, u % 2, :], ps[:, 2 + u % 2, :], ACT.Gelu).then_inc(gelued, 1)

            def ft_high(n, u):
                act.wait_ge(ft_filled, n + 1)
                s.activation(fhh[:, u % 2, :], ps[:, 4 + u % 2, :], F).then_inc(ft_hi, 1)

            def six(base, more):
                for u in range(UNROLL):
                    j = base + u
                    if more or u < UNROLL - 1:
                        fx_high(j + 1, u + 1)
                    ft_high(j, u)
                    if more or u < UNROLL - 1:
                        gelu(j + 1, u + 1)

            fx_high(0, 0)
            gelu(0, 0)
            with act.Fori(0, FT // UNROLL - 1) as i:
                six(i * UNROLL, True)
            six(FT - UNROLL, False)

            for b in range(BATCHES):
                act.wait_ge(fin_ready, b + 1)
                act.dma_start(out[b, 0:(TT - 1) * P, :].rearrange("(t p) f -> p t f", p=P),
                              fin_out[:, b % 2, 0:TT - 1, :]).then_inc(fin_stored[b % 2], 16)
                act.dma_start(out[b, (TT - 1) * P:SEQ, :], fin_out[0:LAST, b % 2, TT - 1, :]
                              ).then_inc(fin_stored[b % 2], 16)
            for i in range(2):
                act.wait_ge(fin_stored[i], 32 * (BATCHES // 2))

        @block.vector
        def _(dve):
            v = nc.vector
            link = Link(dve_link, dve)

            def tick():
                return v.memset(tick_dve[:, :], 0.0)

            def split_low(dst_lo, src, hi_ap, count):
                dve.wait_ge(split_hi, count)
                v.tensor_tensor(dst_lo, src, hi_ap.bitcast(F32), ALU.subtract).then_inc(split_lo, 1)

            split_low(cwl[:, :, :].rearrange("p c o -> p (c o)"), stage[:, ST_CONV:ST_Q],
                      cwh[:, :, :].rearrange("p c o -> p (c o)"), 1)

            def lo(tn, name, dst, hi_ap, width, nth):
                dve.wait_ge(hi_done, nth)
                v.tensor_tensor(dst, general(tn, name, width), hi_ap.bitcast(F32),
                                ALU.subtract).then_inc(drained, 1)

            def hi_count(b, k):
                return b * 15 + (5 + k)

            def xt_lo(tn, first):
                for t in range(TT):
                    lo(tn, XT[t], xtl[:, t, :], xth[:, t, :], 512, first + t + 1)

            def xnt_lo(tn, first):
                for c in range(2):
                    lo(tn, XNT[c], xnl[:, c, :], xnh[:, c, :], TT * P, first + c + 1)

            def moments(src, mv, which, st):
                tick()
                for t in range(TT):
                    last = v.bn_stats(st[:, t, :], src(t))
                link(last)
                tick()
                for t in range(TT):
                    last = v.bn_aggr(mv[:, t, :], st[:, t, :])
                last.then_inc(var_ready[which], 1)

            def conv_add(tn, b):
                dve.wait_ge(xsum_ready, b + 1)
                for t in range(TT):
                    dve.wait_ge(filled, tn.upto(CV[t]))
                    v.scalar_tensor_tensor(y_sb[:, t, :], xsum[:, t, :], 0.5, general(tn, CV[t], DM),
                                           ALU.mult, ALU.add).then_inc(drained, 1)
                dve.wait_ge(drained, tn.upto(CV[TT - 1]))
                moments(lambda t: y_sb[:, t, :], mv1, 0, stats)

            def norm(dst, src, mv, r, which, count, done):
                dve.wait_ge(rstd_ready[which], count)
                for t in range(TT):
                    last = v.tensor_scalar(dst(t), src(t), mv[:, t, 0:1], r[:, t:t + 1], ALU.subtract, ALU.mult)
                last.then_inc(done, 1)

            def front_norm(b):
                norm(lambda t: y_sb[:, t, :], lambda t: y_sb[:, t, :], mv1, rstd1, 0, b + 1, z_ready)

            def front_moments(b):
                dve.wait_ge(h1_ready, b + 1)
                moments(lambda t: h_tile(b, t), mv2, 1, stats)

            def front_xn(b):
                norm(lambda t: xn[:, t, :], lambda t: h_tile(b, t), mv2, rstd2, 1, b + 1, xn_ready)

            def residual(tn, b):
                for t in range(TT):
                    dve.wait_ge(filled, tn.upto(WO[t]))
                    v.tensor_tensor(h_tile(b, t), general(tn, WO[t], DM), h_tile(b, t), ALU.add
                                    ).then_inc(drained, 1)
                dve.wait_ge(drained, tn.upto(WO[TT - 1]))
                moments(lambda t: h_tile(b, t), mv3, 2, stats3)

            def back_xn(b):
                if not isinstance(b, int) or b > 0:
                    dve.wait_ge(scattered, 16 * TOPK * TT * b)
                norm(lambda t: payload[:, 0, t, 0:DM], lambda t: h_tile(b, t), mv3, rstd3, 2, b + 1, xn2_ready)

            def x2t_copy(tn):
                for c in range(2):
                    dve.wait_ge(filled, tn.upto(X2T[c]))
                    v.tensor_copy(x2t[:, c, :], general(tn, X2T[c], TT * P)).then_inc(drained, 1)

            def shift(tn, b):
                dve.wait_ge(filled, tn.upto("l"))
                src = general(tn, "l", TT * EXPERTS).rearrange("p (t e) -> p t e", t=TT)
                link(v.tensor_reduce(mx[:, :, :], src, AX.X, ALU.max))
                v.tensor_tensor(shifted[:, :, :], src, mx[:, :, :].to_broadcast([P, TT, EXPERTS]),
                                ALU.subtract).then_inc(shift_ready, 1)
                dve.wait_ge(shift_ready, b + 1)
                tick().then_inc(drained, 2)

            def choose(b):
                dve.wait_ge(expd_ready, b + 1)
                link(v.tensor_reduce(denom[:, :, :], expd[:, :, :], AX.X, ALU.add))
                link(v.reciprocal(rdenom[:, :, :], denom[:, :, :]))
                link(v.tensor_tensor(probs[:, :, :], expd[:, :, :],
                                     rdenom[:, :, :].to_broadcast([P, TT, EXPERTS]), ALU.mult))
                tick()
                for t in range(TT):
                    last = v.max(top8[:, t, :], probs[:, t, :])
                link(last)
                tick()
                for t in range(TT):
                    last = v.max_index(idx8[:, t, :], top8[:, t, :], probs[:, t, :])
                link(last)
                for k in range(TOPK):
                    v.tensor_copy(payload[:, k, :, DM:DM + 1].bitcast(I32), place[:, :, k:k + 1])
                    v.tensor_copy(payload[:, k, :, DM + 1:ROW], top8[:, :, k:k + 1])
                link(v.tensor_copy(idxf[:, :, :], idx8[:, :, 0:TOPK]))
                v.tensor_tensor(hot0[:, :, :], iota8[:, :, :], idxf[:, :, 0:1].to_broadcast([P, TT, EXPERTS]),
                                ALU.is_equal)
                link(v.tensor_tensor(hot1[:, :, :], iota8[:, :, :],
                                     idxf[:, :, 1:2].to_broadcast([P, TT, EXPERTS]), ALU.is_equal))
                v.tensor_scalar(place[:, :, :], place[:, :, :], float(TOPK * SEQ), None, ALU.add)
                link(v.tensor_tensor(hots[:, :, :], hot0[:, :, :], hot1[:, :, :], ALU.add))
                v.tensor_tensor(chosen[:, :, :], hots[:, :, :], valid8[:, :, :], ALU.mult
                                ).then_inc(chosen_ready, 1)

            def slots(tn, b):
                dve.wait_ge(filled, tn.upto("tot"))
                tot = general(tn, "tot", TT * EXPERTS).rearrange("p (t e) -> p t e", t=TT)
                tri = general(tn, "tri", TT * EXPERTS).rearrange("p (t e) -> p t e", t=TT)
                for t in range(TT):
                    link(v.tensor_tensor(carry[:, t + 1, :], carry[:, t, :], tot[:, t, :], ALU.add))
                link(v.tensor_tensor(rank[:, :, :], carry[:, 0:TT, :], tri, ALU.add))
                tick().then_inc(drained, 2)
                v.tensor_tensor(pick0[:, :, :], hot0[:, :, :], rank[:, :, :], ALU.mult)
                v.tensor_copy(carry[:, 0, :], carry[:, TT, :])
                link(v.tensor_tensor(pick1[:, :, :], hot1[:, :, :], rank[:, :, :], ALU.mult))
                v.tensor_reduce(slotf[:, :, 0:1], pick0[:, :, :], AX.X, ALU.add)
                link(v.tensor_reduce(slotf[:, :, 1:2], pick1[:, :, :], AX.X, ALU.add))
                link(v.tensor_tensor(slotg[:, :, :], slotf[:, :, :], beyond[:, :, :], ALU.add))
                v.tensor_copy(slot[:, :, :], slotg[:, :, :]).then_inc(slots_ready, 1)

            def attention_norm(n, j):
                oa, ob = ps[:, O_BANK, 0:QW], ps[:, O_BANK + 1, 0:QW]
                dve.wait_ge(pv_done, 2 * n + 1)
                link(v.reciprocal(recip[0:64, :], oa[64:128, :]))
                v.tensor_tensor(ot[0:64, j, :], oa[0:64, :], recip[0:64, :], ALU.mult).then_inc(normed, 1)
                dve.wait_ge(pv_done, 2 * n + 2)
                link(v.reciprocal(recip[64:128, :], ob[0:64, :]))
                v.tensor_tensor(ot[64:128, j, :], ob[64:128, :], recip[64:128, :], ALU.mult).then_inc(normed, 1)

            def mask(n, p):
                dve.wait_ge(exped, n + 1)
                r = prob[:, p % NP_, :]
                a = r[:, 0:2 * REG].rearrange("p (r c) -> p r c", r=2)
                v.tensor_tensor(a[:, :, 0:P], a[:, :, 0:P], causal[:, :].unsqueeze(1).to_broadcast([P, 2, P]),
                                ALU.mult)
                v.tensor_tensor(a[:, :, 2 * P:REG], a[:, :, 2 * P:REG],
                                win_causal[:, :].unsqueeze(1).to_broadcast([P, 2, 2 * W2]), ALU.mult)
                c = r[:, 2 * REG:3 * REG].rearrange("p (r c) -> p r c", r=2)
                v.tensor_tensor(c[:, :, 0:P], c[:, :, 0:P], causal[:, :].unsqueeze(1).to_broadcast([P, 2, P]),
                                ALU.mult).then_inc(masked, 1)

            first = Turn(-1)
            dve.wait_ge(consts, 2)
            xt_lo(first, 0)
            conv_add(first, 0)
            front_norm(0)
            front_moments(0)
            dve.wait_ge(weights_in[1], 48)
            split_low(wql[:, :, :].rearrange("p c o -> p (c o)"), stage[:, ST_Q:ST_KV],
                      wqh[:, :, :].rearrange("p c o -> p (c o)"), 2)
            split_low(wkvl[:, :, :, :].rearrange("p w c o -> p (w c o)"), stage[:, ST_KV:ST_KV + 4 * KV * HD],
                      wkvh[:, :, :, :].rearrange("p w c o -> p (w c o)"), 3)
            front_xn(0)
            xnt_lo(first, 3)

            def qkv_low(tn):
                b = tn.b
                for j in range(PAIRS):
                    lo(tn, f"q{j}", ql[:, j, :], qh[:, j, :], QW, hi_count(b, j + 1))
                    if j in (3, 7) and not (isinstance(b, int) and b == 0):
                        pair = PAIRS - LAG + (j == 7)
                        attention_norm((b - 1) * PAIRS + pair, pair)
                for c in range(2):
                    dve.wait_ge(hi_done, hi_count(b, PAIRS + c + 1))
                    src = general(tn, f"k{c}", TT * P)
                    v.tensor_tensor(kl[0:64, 2 * c, :], src[0:64, :], kh[0:64, 2 * c, :].bitcast(F32), ALU.subtract)
                    v.tensor_tensor(kl[64:128, 2 * c + 1, :], src[64:128, :], kh[64:128, 2 * c + 1, :].bitcast(F32),
                                    ALU.subtract).then_inc(drained, 1)
                for t in range(TT):
                    dve.wait_ge(filled, tn.upto(f"v{t}"))
                    src = general(tn, f"v{t}", DM).rearrange("p (g s d) -> p g s d", g=2, s=2)
                    dst = vo[:, t, :, :].rearrange("p (g s) c -> p g s c", s=2)
                    v.tensor_copy(dst[:, :, 0, 0:HD], src[:, :, 0, :])
                    v.tensor_copy(dst[:, :, 1, HD:P], src[:, :, 1, :]).then_inc(drained, 1)

            def turn(tn):
                b = tn.b
                qkv_low(tn)
                for p in range(PAIRS):
                    n = b * PAIRS + p
                    if p >= LAG:
                        attention_norm(n - LAG, p - LAG)
                    mask(n, p)
                    if tn.back:
                        if p == 0:
                            residual(tn, b - 1)
                        if p == 1:
                            back_xn(b - 1)
                    if p == 1 and tn.front:
                        xt_lo(tn, hi_count(b, PAIRS + 2))
                    if p == 2 and tn.front:
                        conv_add(tn, b + 1)
                    if p == 2 and tn.back:
                        x2t_copy(tn)
                    if p == 3 and tn.front:
                        front_norm(b + 1)
                    if p == 4:
                        if tn.front:
                            front_moments(b + 1)
                        if tn.back:
                            shift(tn, b - 1)
                    if p == 5:
                        if tn.back:
                            choose(b - 1)
                        if tn.front:
                            front_xn(b + 1)
                    if p == 6:
                        if tn.back:
                            slots(tn, b - 1)
                        if tn.front:
                            xnt_lo(tn, hi_count(b, PAIRS + 5))

            turn(Turn(0))
            start = link.n
            with dve.Fori(1, BATCHES - 1) as b:
                link.n = (b - 1) * LINKS + start
                turn(Turn(b))
                link_end = link.n
            link.n = start + LINKS * (BATCHES - 2)
            before_last = link.n
            turn(Turn(BATCHES - 1))
            assert link.n - before_last == LINKS - 2, (link.n, before_last, LINKS)

            last_turn = Turn(BATCHES)
            for pair in (PAIRS - 2, PAIRS - 1):
                attention_norm((BATCHES - 1) * PAIRS + pair, pair)
            residual(last_turn, BATCHES - 1)
            back_xn(BATCHES - 1)
            x2t_copy(last_turn)
            shift(last_turn, BATCHES - 1)
            choose(BATCHES - 1)
            slots(last_turn, BATCHES - 1)

            link(v.tensor_scalar(padf[:, :], carry[:, 0, :], iota_p[:, 0:1], None, ALU.add))
            v.tensor_tensor(cntf[:, :], carry[:, 0, :], carry0[:, :], ALU.subtract)
            v.tensor_copy(padi[:, :], padf[:, :]).then_inc(pad_ready, 1)
            dve.wait_ge(pad_ready, 1)
            link(v.tensor_scalar(cntf[:, :], cntf[:, :], float(P - 1), None, ALU.add))
            link(v.tensor_copy(cnti[:, :], cntf[:, :]))
            link(v.tensor_scalar(cnts[:, :], cnti[:, :], 7, None, ALU.logical_shift_right))
            link(v.tensor_copy(tilesf[:, :], cnts[:, :]))
            v.tensor_scalar(lag_rows[:, :], tilesf[:, :], float(-P), float(CAP), ALU.mult, ALU.add)
            link(v.tensor_copy(ends[:, 0:1], tilesf[:, 0:1]))
            for e in range(1, EXPERTS):
                link(v.tensor_tensor(ends[:, e:e + 1], ends[:, e - 1:e], tilesf[:, e:e + 1], ALU.add))
            link(v.tensor_scalar(total1[:, :], ends[0:1, EXPERTS - 1:EXPERTS], -1.0, None, ALU.add))
            v.tensor_scalar(past[:, :], iota_j[:, :], total1[:, 0:1], None, ALU.is_gt)
            link(v.tensor_scalar(tile_j[:, :], iota_j[:, :], total1[:, 0:1], None, ALU.min))
            link(v.tensor_tensor(over[:, :, :], ends[0:1, :].unsqueeze(1).to_broadcast([1, FT, EXPERTS]),
                                 tile_j[:, :].unsqueeze(2).to_broadcast([1, FT, EXPERTS]), ALU.is_le))
            v.tensor_reduce(expf[:, :], over[:, :, :], AX.X, ALU.add)
            link(v.tensor_tensor(overw[:, :, :], over[:, :, :],
                                 lag_rows[0:1, :].unsqueeze(1).to_broadcast([1, FT, EXPERTS]), ALU.mult))
            link(v.tensor_reduce(rowf[:, :], overw[:, :, :], AX.X, ALU.add))
            link(v.scalar_tensor_tensor(rowg[:, :], tile_j[:, :], float(P), rowf[:, :], ALU.mult, ALU.add))
            v.tensor_copy(table[:, 0, :], expf[:, :])
            link(v.scalar_tensor_tensor(rowh[:, :], past[:, :], float(NOWHERE), rowg[:, :], ALU.mult, ALU.add))
            link(v.tensor_scalar(rowh[:, :], rowh[:, :], float(NOWHERE), None, ALU.min))
            v.tensor_copy(table[:, 1, :], rowh[:, :]).then_inc(table_ready, 1)

            for e in range(EXPERTS):
                for half, (dst, high) in enumerate(((wil, wih), (wol, woh))):
                    dve.wait_ge(exp_hi, 2 * e + half + 1)
                    v.tensor_tensor(dst[:, e * 1024:(e + 1) * 1024], raw[:, half, :],
                                    high[:, e * 1024:(e + 1) * 1024].bitcast(F32), ALU.subtract
                                    ).then_inc(exp_lo, 1)

            def fx_low(n, u):
                dve.wait_ge(fx_hi, n + 1)
                v.tensor_tensor(fxl[:, u % 2, :], ps[:, u % 2, 0:2 * P], fxh[:, u % 2, :].bitcast(F32),
                                ALU.subtract).then_inc(fx_lo, 1)

            def ft_low(n, u):
                dve.wait_ge(ft_hi, n + 1)
                v.tensor_tensor(fhl[:, u % 2, :], ps[:, 4 + u % 2, :], fhh[:, u % 2, :].bitcast(F32),
                                ALU.subtract).then_inc(ft_lo, 1)

            def gated(n, u, reuse):
                if reuse is not None:
                    dve.wait_ge(y_out[u % 3], reuse)
                dve.wait_ge(fy_filled, n + 1)
                v.tensor_scalar(y_rows[:, u % 3, :], ps[:, 6 + u % 2, 0:DM], xt_rows[:, u % UNROLL, DM + 1:ROW],
                                None, ALU.mult).then_inc(fy_done, 1)

            def six(i, base, head, more):
                for u in range(UNROLL):
                    j = base + u
                    if more or u < UNROLL - 1:
                        fx_low(j + 1, u + 1)
                    ft_low(j, u)
                    gated(j, u, None if head and u < 3 else i * 32 + (16 * (u // 3)))

            fx_low(0, 0)
            six(0, 0, True, True)
            with dve.Fori(1, FT // UNROLL - 1) as i:
                six(i, i * UNROLL, False, True)
            six(FT // UNROLL - 1, FT - UNROLL, False, False)

            v.memset(fin_in[:, :, TT - 1, :], 0.0).then_inc(fin_clear, 1)
            dve.wait_ge(fin_clear, 1)
            for b in range(BATCHES):
                dve.wait_ge(fin_loaded[b % 2], 32 * (b // 2 + 1))
                if b >= 2:
                    dve.wait_ge(fin_stored[b % 2], 32 * (b // 2))
                o = fin_out[:, b % 2, :, :]
                link(v.tensor_tensor(o, fin_in[:, b % 2, :, 0:DM], fin_in[:, b % 2, :, DM:2 * DM], ALU.add))
                v.tensor_tensor(o, o, h_batch(b), ALU.add).then_inc(fin_ready, 1)

        @block.tensor
        def _(pe):
            t_ = nc.tensor

            def claim(tn, name):
                n = tn.before(name)
                if not isinstance(n, int):
                    pe.wait_ge(drained, n - 2)
                elif n >= 3:
                    pe.wait_ge(drained, n - 2)

            def three(out_ap, terms):
                steps = [(a, c) for ah, al, ch, cl in terms for a, c in ((ah, ch), (ah, cl), (al, ch))]
                for i, (a, c) in enumerate(steps):
                    last = t_.matmul(out_ap, a, c, start=(i == 0), stop=(i == len(steps) - 1))
                return last

            def transposes(tn):
                for t in range(TT):
                    claim(tn, XT[t])
                    dst = general(tn, XT[t])
                    for c in range(4):
                        last = t_.transpose(dst[:, c * P:(c + 1) * P], x_sb[:, t, c * P:(c + 1) * P], ident[:, :])
                    last.then_inc(filled, 1)

            def conv(tn, first):
                for t in range(TT):
                    claim(tn, CV[t])
                    if t == 0:
                        pe.wait_ge(drained, tn.upto(XT[TT - 1]))
                    three(general(tn, CV[t], DM),
                          [(xth[:, t, c * P:(c + 1) * P], xtl[:, t, c * P:(c + 1) * P], cwh[:, c, :], cwl[:, c, :])
                           for c in range(4)]).then_inc(filled, 1)

            def xn_transposes(tn, b):
                pe.wait_ge(xn_ready, b + 1)
                for c in range(2):
                    claim(tn, XNT[c])
                    dst = general(tn, XNT[c], TT * P)
                    for t in range(TT):
                        last = t_.transpose(dst[:, t * P:(t + 1) * P], xn[:, t, c * P:(c + 1) * P], ident[:, :])
                    last.then_inc(filled, 1)

            def project(tn):
                b = tn.b
                pe.wait_ge(drained, front_done(b))
                for j in range(PAIRS):
                    claim(tn, f"q{j}")
                    three(general(tn, f"q{j}", QW),
                          [(wqh[:, c, j * P:(j + 1) * P], wql[:, c, j * P:(j + 1) * P],
                            xnh[:, c, 0:QW], xnl[:, c, 0:QW]) for c in range(2)]).then_inc(filled, 1)
                    if j in (3, 7) and not (isinstance(b, int) and b == 0):
                        pair = PAIRS - LAG + (j == 7)
                        values((b - 1) * PAIRS + pair, pair)
                for j in range(2):
                    claim(tn, f"k{j}")
                    three(general(tn, f"k{j}", TT * P),
                          [(wkvh[:, 0, c, j * P:(j + 1) * P], wkvl[:, 0, c, j * P:(j + 1) * P],
                            xnh[:, c, :], xnl[:, c, :]) for c in range(2)]).then_inc(filled, 1)
                for t in range(TT):
                    claim(tn, f"v{t}")
                    cols = slice(t * P, (t + 1) * P)
                    three(general(tn, f"v{t}", DM),
                          [(xnh[:, c, cols], xnl[:, c, cols], wkvh[:, 1, c, :], wkvl[:, 1, c, :])
                           for c in range(2)]).then_inc(filled, 1)

            def score(n, j):
                if not isinstance(n, int) or n >= 1:
                    pe.wait_ge(capped, n)
                for half in range(2):
                    g = 2 * (j // 4) + half
                    region = ps[:, S_BANK + half, :]
                    for kt, dst in ((0, region[:, 0:W0]), (2, region[:, W0:REG]),
                                    (1, ps[:, S_BANK + 2, half * W1:(half + 1) * W1])):
                        cols = slice(kt * P, (kt + 1) * P)
                        last = three(dst, [(kh[:, g, cols], kl[:, g, cols], qh[:, j, kt * P:QW], ql[:, j, kt * P:QW])])
                last.then_inc(scores, 1)

            def values(n, p):
                pe.wait_ge(masked, n + 1)
                buf = prob[:, p % NP_, :]
                for half in range(2):
                    g = 2 * (p // 4) + half
                    if not isinstance(n, int) or n >= 1:
                        pe.wait_ge(normed, 2 * n + (half - 1))
                    dst = ps[:, O_BANK + half, :]
                    r = buf[:, half * REG:(half + 1) * REG]
                    mid = buf[:, 2 * REG + half * W1:2 * REG + (half + 1) * W1]
                    t_.matmul(dst[:, 0:QW], vo[:, 0, g, :], r[:, 0:W0], start=True, stop=False)
                    t_.matmul(dst[:, P:QW], vo[:, 1, g, :], mid, start=False, stop=False)
                    t_.matmul(dst[:, 2 * P:QW], vo[0:LAST, 2, g, :], r[0:LAST, W0:REG],
                              start=False, stop=True).then_inc(pv_done, 1)

            def output(tn, b):
                pe.wait_ge(normed, (b + 1) * (2 * PAIRS))
                for t in range(TT):
                    claim(tn, WO[t])
                    rows = P if t < TT - 1 else QW - t * P
                    for c in range(PAIRS):
                        last = t_.matmul(general(tn, WO[t], DM)[0:rows, :], ot[:, c, t * P:t * P + rows],
                                         wo_sb[:, c, :], start=(c == 0), stop=(c == PAIRS - 1))
                    last.then_inc(filled, 1)

            def x2_transposes(tn, b):
                pe.wait_ge(xn2_ready, b + 1)
                for c in range(2):
                    claim(tn, X2T[c])
                    dst = general(tn, X2T[c], TT * P)
                    for t in range(TT):
                        last = t_.transpose(dst[:, t * P:(t + 1) * P], payload[:, 0, t, c * P:(c + 1) * P],
                                            ident[:, :])
                    last.then_inc(filled, 1)

            def router_hidden(tn, b):
                claim(tn, "g")
                pe.wait_ge(drained, tn.upto(X2T[1]))
                for c in range(2):
                    last = t_.matmul(general(tn, "g", TT * P)[0:GATE, :], wg1_sb[:, c, :], x2t[:, c, :],
                                     start=(c == 0), stop=(c == 1))
                last.then_inc(filled, 1)

            def router_logits(tn, b):
                claim(tn, "l")
                pe.wait_ge(gate_ready, b + 1)
                for t in range(TT):
                    last = t_.matmul(general(tn, "l")[:, t * EXPERTS:(t + 1) * EXPERTS],
                                     gate_t[:, t * P:(t + 1) * P], wg2_sb[:, :], start=True, stop=True)
                last.then_inc(filled, 1)

            def counts(tn, b):
                pe.wait_ge(chosen_ready, b + 1)
                for name, m in (("tri", before_m), ("tot", ones_m)):
                    claim(tn, name)
                    t_.matmul(general(tn, name, TT * EXPERTS), m[:, :],
                              chosen[:, :, :].rearrange("p t e -> p (t e)"), start=True, stop=True
                              ).then_inc(filled, 1)

            first = Turn(-1)
            pe.wait_ge(consts, 2)
            pe.wait_ge(x_in, 32)
            transposes(first)
            pe.wait_ge(split_lo, 1)
            conv(first, True)
            xn_transposes(first, 0)
            pe.wait_ge(split_lo, 3)

            def turn(tn):
                b = tn.b
                project(tn)
                for p in range(PAIRS):
                    n = b * PAIRS + p
                    if p == 0:
                        pe.wait_ge(drained, tn.upto("v2"))
                    score(n, p)
                    if p >= LAG:
                        values(n - LAG, p - LAG)
                    if p == 0 and tn.back:
                        pe.wait_ge(weights_in[2], 64)
                        output(tn, b - 1)
                    if p == 1 and tn.front:
                        pe.wait_ge(x_in, 32 * (b + 2))
                        transposes(tn)
                    if p == 2:
                        if tn.front:
                            conv(tn, False)
                        if tn.back:
                            x2_transposes(tn, b - 1)
                    if p == 3 and tn.back:
                        router_hidden(tn, b - 1)
                    if p == 4 and tn.back:
                        router_logits(tn, b - 1)
                    if p == 6:
                        if tn.back:
                            counts(tn, b - 1)
                        if tn.front:
                            xn_transposes(tn, b + 1)

            turns(pe.Fori, turn)
            last_turn = Turn(BATCHES)
            for pair in (PAIRS - 2, PAIRS - 1):
                values((BATCHES - 1) * PAIRS + pair, pair)
            output(last_turn, BATCHES - 1)
            x2_transposes(last_turn, BATCHES - 1)
            router_hidden(last_turn, BATCHES - 1)
            router_logits(last_turn, BATCHES - 1)
            counts(last_turn, BATCHES - 1)

            def row_transposes(n, u, i):
                pe.wait_ge(rows_in[u % UNROLL], (i + 1) * 16)
                if not isinstance(n, int) or n >= 2:
                    pe.wait_ge(fx_lo, n - 1)
                for c in range(2):
                    last = t_.transpose(ps[:, u % 2, c * P:(c + 1) * P],
                                        xt_rows[:, u % UNROLL, c * P:(c + 1) * P], ident[:, :])
                last.then_inc(fx_filled, 1)

            def up(n, u, e):
                pe.wait_ge(fx_lo, n + 1)
                if not isinstance(n, int) or n >= 2:
                    pe.wait_ge(gelued, n - 1)
                three(ps[:, 2 + u % 2, :],
                      [(fxh[:, u % 2, c * P:(c + 1) * P], fxl[:, u % 2, c * P:(c + 1) * P],
                        wih[:, bass.ds(e * 1024 + c * HID, HID)], wil[:, bass.ds(e * 1024 + c * HID, HID)])
                       for c in range(2)]).then_inc(fh_filled, 1)

            def h_transposes(n, u):
                pe.wait_ge(gelued, n + 1)
                if not isinstance(n, int) or n >= 2:
                    pe.wait_ge(ft_lo, n - 1)
                for c in range(4):
                    last = t_.transpose(ps[:, 4 + u % 2, c * P:(c + 1) * P], act_h[:, u % 2, c * P:(c + 1) * P],
                                        ident[:, :])
                last.then_inc(ft_filled, 1)

            def down(n, u, e):
                pe.wait_ge(ft_lo, n + 1)
                if not isinstance(n, int) or n >= 2:
                    pe.wait_ge(fy_done, n - 1)
                three(ps[:, 6 + u % 2, 0:DM],
                      [(fhh[:, u % 2, c * P:(c + 1) * P], fhl[:, u % 2, c * P:(c + 1) * P],
                        woh[:, bass.ds(e * 1024 + c * DM, DM)], wol[:, bass.ds(e * 1024 + c * DM, DM)])
                       for c in range(4)]).then_inc(fy_filled, 1)

            def expert_of(j):
                e = pe.value_load(table[0:1, 0, bass.ds(j, 1)], min_val=0, max_val=EXPERTS - 1)
                pe.wait_ge(exp_lo, e * 2 + 2)
                return e

            def six(i, base, more):
                for u in range(UNROLL):
                    j = base + u
                    go_on = more or u < UNROLL - 1
                    if go_on:
                        row_transposes(j + 1, u + 1, i if u < UNROLL - 1 else i + 1)
                    h_transposes(j, u)
                    if go_on:
                        up(j + 1, u + 1, expert_of(j + 1))
                    down(j, u, expert_of(j))

            pe.wait_ge(table_ready, 1)
            row_transposes(0, 0, 0)
            up(0, 0, expert_of(0))
            six(0, 0, True)
            with pe.Fori(1, FT // UNROLL - 1) as i:
                six(i, i * UNROLL, True)
            six(FT // UNROLL - 1, FT - UNROLL, False)


LINKS = 35


def kernel(x, L0_tok_conv_w, L0_tok_conv_b, L0_tok_ln_gamma, L0_tok_ln_beta, L0_attn_Wq, L0_attn_Wk, L0_attn_Wv,
           L0_attn_Wo, L0_ffn_wg1, L0_ffn_bg1, L0_ffn_wg2, L0_ffn_w_in, L0_ffn_w_out):
    import numpy as np
    import concourse.bacc as bacc
    from concourse.bass_utils import run_bass_kernel_spmd

    def paired(w):
        w = np.asarray(w).reshape(2, 2, HEADS // KV, HD, -1)
        return w.transpose(0, 2, 1, 3, 4).reshape(HEADS * HD, -1)

    arrays = {
        "x": np.asarray(x).reshape(BATCHES, SEQ, 2 * DM),
        "conv_w": np.asarray(L0_tok_conv_w).transpose(2, 1, 0).reshape(2 * DM, DM),
        "conv_b": np.asarray(L0_tok_conv_b),
        "gamma": np.asarray(L0_tok_ln_gamma),
        "beta": np.asarray(L0_tok_ln_beta),
        "wq": paired(L0_attn_Wq).T,
        "wk": np.asarray(L0_attn_Wk).T,
        "wv": np.asarray(L0_attn_Wv).T,
        "wo": paired(np.asarray(L0_attn_Wo).T),
        "wg1": np.asarray(L0_ffn_wg1),
        "bg1": np.asarray(L0_ffn_bg1),
        "wg2": np.asarray(L0_ffn_wg2),
        "w_in": np.asarray(L0_ffn_w_in),
        "w_out": np.asarray(L0_ffn_w_out),
    }
    arrays = {n: np.ascontiguousarray(a) for n, a in arrays.items()}
    nc = bacc.Bacc("TRN2", target_bir_lowering=False, num_devices=1)
    args = [nc.dram_tensor(n, a.shape, mybir.dt.from_np(a.dtype), kind="ExternalInput").ap()
            for n, a in arrays.items()]
    xs = nc.dram_tensor("expert_rows", (NOWHERE + P, ROW), F32).ap()
    ys = nc.dram_tensor("gated_rows", (TOK, TOPK * DM), F32).ap()
    out = nc.dram_tensor("out", (BATCHES, SEQ, DM), F32, kind="ExternalOutput").ap()
    build(nc, *args, xs, ys, out)
    result = run_bass_kernel_spmd(nc, [arrays], core_ids=[0])
    return result.results[0]["out"]
```

```python
import concourse.bass as bass
from concourse import mybir
from contextlib import ExitStack

F32 = mybir.dt.float32
F32R = mybir.dt.float32r
I32 = mybir.dt.int32
U32 = mybir.dt.uint32
ALU = mybir.AluOpType
ACT = mybir.ActivationFunctionType
AX = mybir.AxisListType

BATCHES, FRAMES, DM = 8, 750, 256
SEQ = FRAMES // 2
P = 128
TT = -(-SEQ // P)
LAST = SEQ - (TT - 1) * P
QW = SEQ + SEQ % 2
TOK = BATCHES * SEQ
HEADS, KV, HD = 16, 4, 64
PAIRS = HEADS // 2
WINDOW = 256
SOFTCAP = 30.0
SCALE = HD ** -0.5
EPS = 1e-5
EXPERTS, HID, TOPK, GATE = 8, 512, 2, 64
CAP = TOK + P
ROW = DM + 2
FT = (TOK * TOPK + EXPERTS * (P - 1)) // P
NOWHERE = EXPERTS * CAP
OFF = 1 << 20
UNROLL = 6
HALVES = (slice(0, HID // 2), slice(HID // 2, HID))
EARLY_EXPERTS = 4
assert FT % UNROLL == 0 and TT == 3 and SEQ <= WINDOW + P

W0, W1, W2 = QW, QW - P, QW - 2 * P
REG = W0 + W2
assert REG == 2 * W1 and REG <= 512
LAG = 2
NP_ = 4

LATE_PAIRS = {1: PAIRS - 2, 4: PAIRS - 1}
LOWER, UPPER = slice(0, 64), slice(64, 128)
NR = 4
SR = 8
SW = QW // SR
assert QW % SR == 0

EARLY_Q = 6
QKV = ["k0", "k1"] + [f"q{j}" for j in range(EARLY_Q)] + ["v0", "v1", "v2"]
LATE_QS = [f"q{j}" for j in range(EARLY_Q, PAIRS)]
WO = ["w0", "w1", "w2"]
XT = ["xt0", "xt1", "xt2"]
CV = ["cv0", "cv1", "cv2"]
X2T = ["x2t0", "x2t1"]
XNT = ["xnt0", "xnt1"]
RK = ["tri", "tot"]


def jobs_of(back, front, attention=True):
    out = list(QKV) if attention else []
    out += XT if front else []
    out += LATE_QS if attention else []
    out += CV if front else []
    out += WO if back else []
    out += X2T + ["g", "l"] if back else []
    out += XNT if front else []
    out += RK if back else []
    return out


PER_TURN = len(jobs_of(True, True))
assert PER_TURN % 3 == 0
PROLOGUE = XT + CV + XNT
FIRST_JOB = PER_TURN - len(PROLOGUE) - len(jobs_of(False, True))


class Turn:

    def __init__(self, b):
        self.b = b
        self.attention = not (isinstance(b, int) and b in (-1, BATCHES))
        self.back = not (isinstance(b, int) and b <= 0)
        self.front = not (isinstance(b, int) and b >= BATCHES - 1)
        if isinstance(b, int) and b == -1:
            names, self.base = PROLOGUE, FIRST_JOB
        elif isinstance(b, int) and b == 0:
            names, self.base = jobs_of(False, True), FIRST_JOB + len(PROLOGUE)
        elif isinstance(b, int) and b == BATCHES:
            names, self.base = jobs_of(True, False, False), PER_TURN * (BATCHES - 1) + len(jobs_of(True, False))
        else:
            names, self.base = jobs_of(True, self.front), b * PER_TURN
        start = 0 if not isinstance(self.base, int) else self.base % 3
        self.local = {name: k for k, name in enumerate(names)}
        self.bank_start = start

    def bank(self, name):
        return (self.bank_start + self.local[name]) % 3

    def before(self, name):
        return self.base + (self.local[name] - FIRST_JOB)

    def upto(self, name):
        return self.base + (self.local[name] - FIRST_JOB + 1)


def turns(engine_loop, body):
    body(Turn(0))
    body(Turn(1))
    with engine_loop(2, BATCHES - 1) as b:
        body(Turn(b))
    body(Turn(BATCHES - 1))


def front_done(b):
    behind = 0 if isinstance(b, int) and b <= 1 else len(RK)
    return Turn(b).base - (FIRST_JOB + behind)


def recip_uses(n, p):
    per_batch = PAIRS // NR
    if isinstance(n, int):
        return n // PAIRS * per_batch + p // NR + 1
    return (n - p) // NR + (p // NR + 1)


def sent(b):
    return b * (16 * TOPK * TT)


class Link:

    def __init__(self, sem, engine):
        self.sem, self.engine, self.n = sem, engine, 0

    def __call__(self, instruction):
        instruction.then_inc(self.sem, 1)
        self.n = self.n + 1
        self.engine.wait_ge(self.sem, self.n)


def build(nc, x, conv_w, conv_b, gamma, beta, wq, wk, wv, wo, wg1, bg1, wg2, w_in, w_out, xs, ys, rs_dram, out):
    ctx = ExitStack()
    with ctx:
        def sem(name):
            return ctx.enter_context(nc.semaphore(name))

        def sb(stack, name, shape, dt=F32):
            return stack.enter_context(nc.sbuf_tensor(name, shape, dt))

        keep = ctx
        h_all = sb(keep, "h_all", [P, BATCHES * TT * DM])
        payload = sb(keep, "payload", [P, TOPK, TT, ROW])
        x2t = sb(keep, "x2t", [P, 2, TT * P])
        gate_t = sb(keep, "gate_t", [GATE, TT * P])
        wg1_sb = sb(keep, "wg1_sb", [P, 2, GATE])
        bg1_sb = sb(keep, "bg1_sb", [GATE, 1])
        wg2_sb = sb(keep, "wg2_sb", [GATE, EXPERTS])
        ident = sb(keep, "ident", [P, P])
        before_m = sb(keep, "before_m", [P, P])
        ones_m = sb(keep, "ones_m", [P, P])
        stats3 = sb(keep, "stats3", [P, TT, 6])
        mv3 = sb(keep, "mv3", [P, TT, 2])
        ve3 = sb(keep, "ve3", [P, TT])
        rstd3 = sb(keep, "rstd3", [P, TT])
        minus_half = sb(keep, "minus_half", [P, TT])
        mx = sb(keep, "mx", [P, TT, 1])
        shifted = sb(keep, "shifted", [P, TT, EXPERTS])
        expd = sb(keep, "expd", [P, TT, EXPERTS])
        denom = sb(keep, "denom", [P, TT, 1])
        rdenom = sb(keep, "rdenom", [P, TT, 1])
        probs = sb(keep, "probs", [P, TT, EXPERTS])
        top8 = sb(keep, "top8", [P, TT, 8])
        idx8 = sb(keep, "idx8", [P, TT, 8], U32)
        idxf = sb(keep, "idxf", [P, TT, TOPK])
        iota8 = sb(keep, "iota8", [P, TT, EXPERTS])
        hot0 = sb(keep, "hot0", [P, TT, EXPERTS])
        hot1 = sb(keep, "hot1", [P, TT, EXPERTS])
        hots = sb(keep, "hots", [P, TT, EXPERTS])
        chosen = sb(keep, "chosen", [P, TT, EXPERTS])
        valid8 = sb(keep, "valid8", [P, TT, EXPERTS])
        beyond = sb(keep, "beyond", [P, TT, TOPK])
        carry = sb(keep, "carry", [P, TT + 1, EXPERTS])
        carry0 = sb(keep, "carry0", [P, EXPERTS])
        rank = sb(keep, "rank", [P, TT, EXPERTS])
        pick0 = sb(keep, "pick0", [P, TT, EXPERTS])
        pick1 = sb(keep, "pick1", [P, TT, EXPERTS])
        slotf = sb(keep, "slotf", [P, TT, TOPK])
        slotg = sb(keep, "slotg", [P, TT, TOPK])
        slot = sb(keep, "slot", [P, TT, TOPK], I32)
        place = sb(keep, "place", [P, TT, TOPK])
        padi = sb(keep, "padi", [1, EXPERTS], I32)
        cntf = sb(keep, "cntf", [P, EXPERTS])
        cnti = sb(keep, "cnti", [P, EXPERTS], I32)
        cnts = sb(keep, "cnts", [P, EXPERTS], I32)
        tilesf = sb(keep, "tilesf", [P, EXPERTS])
        ends = sb(keep, "ends", [P, EXPERTS])
        lag_rows = sb(keep, "lag_rows", [P, EXPERTS])
        iota_j = sb(keep, "iota_j", [1, FT])
        tile_j = sb(keep, "tile_j", [1, FT])
        total1 = sb(keep, "total1", [1, 1])
        over = sb(keep, "over", [1, FT, EXPERTS])
        overw = sb(keep, "overw", [1, FT, EXPERTS])
        expf = sb(keep, "expf", [1, FT])
        rowf = sb(keep, "rowf", [1, FT])
        rowg = sb(keep, "rowg", [1, FT])
        past = sb(keep, "past", [1, FT])
        rowh = sb(keep, "rowh", [1, FT])
        table = sb(keep, "table", [1, 2, FT], I32)
        pad_rows = sb(keep, "pad_rows", [P, ROW])
        tick_dve = sb(keep, "tick_dve", [1, 1])
        tick_pool = sb(keep, "tick_pool", [1, 1])
        eps_c = sb(keep, "eps_c", [P, TT])

        early = ExitStack()
        x_sb = sb(early, "x_sb", [P, TT, 2 * DM])
        xsum = sb(early, "xsum", [P, TT, DM])
        bias2 = sb(early, "bias2", [P, DM])
        gamma_b = sb(early, "gamma_b", [P, DM])
        beta_b = sb(early, "beta_b", [P, DM])
        xth = sb(early, "xth", [P, TT, 2 * DM], F32R)
        xtl = sb(early, "xtl", [P, TT, 2 * DM], F32R)
        y_sb = sb(early, "y_sb", [P, TT, DM])
        xn = y_sb
        stats = sb(early, "stats", [P, TT, 6])
        mv1 = sb(early, "mv1", [P, TT, 2])
        ve1 = sb(early, "ve1", [P, TT])
        rstd1 = sb(early, "rstd1", [P, TT])
        mv2 = sb(early, "mv2", [P, TT, 2])
        ve2 = sb(early, "ve2", [P, TT])
        rstd2 = sb(early, "rstd2", [P, TT])
        xnh = sb(early, "xnh", [P, 2, TT * P], F32R)
        xnl = sb(early, "xnl", [P, 2, TT * P], F32R)
        qs = sb(early, "qs", [P, 2, PAIRS, QW], F32R)
        kh = sb(early, "kh", [P, KV, TT * P], F32R)
        kl = sb(early, "kl", [P, KV, TT * P], F32R)
        vo = sb(early, "vo", [P, TT, KV, P])
        prob = sb(early, "prob", [P, NP_, 3 * REG])
        ring = sb(early, "ring", [P, NR, 2, QW])
        sums = sb(early, "sums", [2 * SR, NR, SW])
        rsums = sb(early, "rsums", [2 * SR, NR, SW])
        recip = sb(early, "recip", [P, NR, QW])
        ot = sb(early, "ot", [P, PAIRS, QW])
        cwh = sb(early, "cwh", [P, 4, DM], F32R)
        cwl = sb(early, "cwl", [P, 4, DM], F32R)
        wqh = sb(early, "wqh", [P, 2, HEADS * HD], F32R)
        wql = sb(early, "wql", [P, 2, HEADS * HD], F32R)
        wkvh = sb(early, "wkvh", [P, 2, 2, KV * HD], F32R)
        wkvl = sb(early, "wkvl", [P, 2, 2, KV * HD], F32R)
        wo_sb = sb(early, "wo_sb", [P, PAIRS, DM])
        causal = sb(early, "causal", [P, P])
        win_causal = sb(early, "win_causal", [P, 2 * W2])
        early.close()

        late = ExitStack()
        wih = sb(late, "wih", [P, EXPERTS * 2 * HID], F32R)
        wil = sb(late, "wil", [P, EXPERTS * 2 * HID], F32R)
        woh = sb(late, "woh", [P, EXPERTS * 4 * DM], F32R)
        wol = sb(late, "wol", [P, EXPERTS * 4 * DM], F32R)
        raw = sb(late, "raw", [P, 2, 2, 2 * HID])
        xt_rows = sb(late, "xt_rows", [P, UNROLL, ROW])
        fxh = sb(late, "fxh", [P, 2, 2 * P], F32R)
        fxl = sb(late, "fxl", [P, 2, 2 * P], F32R)
        act_h = sb(late, "act_h", [P, 2, HID])
        fhh = sb(late, "fhh", [P, 2, HID], F32R)
        fhl = sb(late, "fhl", [P, 2, HID], F32R)
        y_rows = sb(late, "y_rows", [P, 3, DM])
        late.close()
        final = ExitStack()
        fin_in = sb(final, "fin_in", [P, BATCHES, TT, 2 * DM])
        final.close()

        ps = ctx.enter_context(nc.psum_tensor("ps", [P, 8, 512], F32))
        S_BANK, O_BANK, G_BANK = 0, 3, 5

        weights_in = [sem(f"weights_in{i}") for i in range(3)]
        consts_in = sem("consts_in")
        x_in = sem("x_in")
        x_summed = sem("x_summed")
        consts = sem("consts")
        kv_clear = sem("kv_clear")
        split_hi = sem("split_hi")
        split_lo = sem("split_lo")
        filled = sem("filled")
        drained = sem("drained")
        hi_done = sem("hi_done")
        scores = sem("scores")
        capped = sem("capped")
        exped = sem("exped")
        masked = sem("masked")
        pv_done = sem("pv_done")
        raised = [sem(f"raised{i}") for i in range(2)]
        sums_in = [sem(f"sums_in{i}") for i in range(NR)]
        rsums_ready = sem("rsums_ready")
        rsums_out = sem("rsums_out")
        recip_in = [sem(f"recip_in{i}") for i in range(NR)]
        normed = sem("normed")
        xsum_ready = sem("xsum_ready")
        var_ready = [sem(f"var_ready{i}") for i in range(3)]
        rstd_ready = [sem(f"rstd_ready{i}") for i in range(3)]
        z_ready = sem("z_ready")
        h1_ready = sem("h1_ready")
        xn_ready = sem("xn_ready")
        xn2_ready = sem("xn2_ready")
        copy_ready = sem("copy_ready")
        x2t_ready = sem("x2t_ready")
        gate_ready = sem("gate_ready")
        shift_ready = sem("shift_ready")
        expd_ready = sem("expd_ready")
        chosen_ready = sem("chosen_ready")
        slots_ready = sem("slots_ready")
        scattered = sem("scattered")
        dve_link = sem("dve_link")
        pool_link = sem("pool_link")
        pad_ready = sem("pad_ready")
        ticked = sem("ticked")
        pad_done = sem("pad_done")
        table_ready = sem("table_ready")
        raw_in = [[sem(f"raw_in{i}{half}") for half in range(2)] for i in range(2)]
        exp_hi = sem("exp_hi")
        exp_lo = sem("exp_lo")
        rows_in = [sem(f"rows_in{i}") for i in range(UNROLL)]
        fx_filled = sem("fx_filled")
        fx_hi = sem("fx_hi")
        fx_lo = sem("fx_lo")
        fh_filled = sem("fh_filled")
        gelued = sem("gelued")
        ft_filled = sem("ft_filled")
        ft_hi = sem("ft_hi")
        ft_lo = sem("ft_lo")
        fy_filled = sem("fy_filled")
        fy_done = sem("fy_done")
        y_out = [sem(f"y_out{i}") for i in range(3)]
        fin_loaded = [sem(f"fin_loaded{i}") for i in range(BATCHES)]
        fin_clear = sem("fin_clear")
        fin_ready = sem("fin_ready")
        fin_stored = sem("fin_stored")

        block = ctx.enter_context(nc.Block())

        def general(turn, name, width=512):
            return ps[:, G_BANK + turn.bank(name), 0:width]

        def h_tile(b, t):
            return h_all[:, bass.ds((b * TT + t) * DM, DM)]

        def h_batch(b):
            return h_all[:, bass.ds(b * (TT * DM), TT * DM)].rearrange("p (t d) -> p t d", t=TT)

        stage = prob[:, :, :].rearrange("p n c -> p (n c)")
        ST_CONV, ST_Q = 0, 4 * DM
        ST_KV = ST_Q + 2 * HEADS * HD

        @block.sync
        def _(sp):
            def load_x(b):
                sp.dma_start(x_sb[:, 0:TT - 1, :],
                             x[bass.ds(b, 1), 0:(TT - 1) * P, :].rearrange("a (t p) f -> p (a t) f", p=P)
                             ).then_inc(x_in, 16)
                sp.dma_start(x_sb[0:LAST, TT - 1, :],
                             x[bass.ds(b, 1), (TT - 1) * P:SEQ, :].rearrange("a p f -> p (a f)")).then_inc(x_in, 16)

            sp.wait_ge(consts, 1)
            load_x(0)
            sp.dma_start(stage[:, ST_CONV:ST_Q].rearrange("p (c o) -> p c o", c=4),
                         conv_w.rearrange("(c p) o -> p c o", p=P)).then_inc(weights_in[0], 16)
            sp.dma_start(stage[:, ST_Q:ST_KV].rearrange("p (c o) -> p c o", c=2),
                         wq.rearrange("(c p) o -> p c o", p=P)).then_inc(weights_in[1], 16)
            for i, w in enumerate((wk, wv)):
                at = ST_KV + i * 2 * KV * HD
                sp.dma_start(stage[:, at:at + 2 * KV * HD].rearrange("p (c o) -> p c o", c=2),
                             w.rearrange("(c p) o -> p c o", p=P)).then_inc(weights_in[1], 16)
            sp.dma_start(wo_sb[:, :, :], wo.rearrange("(c p) o -> p c o", p=P)).then_inc(weights_in[2], 16)
            sp.dma_start(wg1_sb[:, :, :], wg1.rearrange("(c p) o -> p c o", p=P)).then_inc(weights_in[2], 16)
            sp.dma_start(wg2_sb[:, :], wg2).then_inc(weights_in[2], 16)
            sp.dma_start(bg1_sb[:, :], bg1.rearrange("(g a) -> g a", a=1)).then_inc(weights_in[2], 16)

            def next_x(b):
                sp.wait_ge(drained, Turn(b - 2).upto(XT[-1]))
                sp.wait_ge(x_summed, b)
                load_x(b)

            next_x(1)
            sp.wait_ge(consts, 3)
            sp.dma_start(xs[NOWHERE:NOWHERE + P, :], pad_rows[:, :]).then_inc(pad_done, 16)

            def spread_sums(n, slot):
                sp.wait_ge(raised[0], n + 1)
                sp.dma_start(sums[0:SR, slot, :], ring[64:65, slot, 0, :]).then_inc(sums_in[slot], 16)
                sp.wait_ge(raised[1], n + 1)
                sp.dma_start(sums[SR:2 * SR, slot, :], ring[0:1, slot, 1, :]).then_inc(sums_in[slot], 16)

            def spread_recip(n, slot):
                sp.wait_ge(rsums_ready, n + 1)
                sp.dma_start(rs_dram[slot, :, :].rearrange("s (r c) -> (s r) c", r=SR),
                             rsums[:, slot, :]).then_inc(rsums_out, 16)
                sp.wait_ge(rsums_out, (n + 1) * 16)
                for half in range(2):
                    sp.dma_start(recip[64 * half:64 * half + 64, slot, :],
                                 rs_dram[slot, half, :].partition_broadcast(64)).then_inc(recip_in[slot], 16)

            def turn_loads(b, load):
                for p in range(PAIRS):
                    n = b * PAIRS + p
                    if p == 0 and not (isinstance(b, int) and b == 0):
                        spread_recip(n - 1, (p - 1) % NR)
                    spread_sums(n, p % NR)
                    if p > 0:
                        spread_recip(n - 1, (p - 1) % NR)
                    if p == 1 and load:
                        load()

            turn_loads(0, lambda: next_x(2))
            with sp.Fori(3, BATCHES) as loaded:
                turn_loads(loaded - 2, lambda: next_x(loaded))
            turn_loads(BATCHES - 2, None)
            turn_loads(BATCHES - 1, None)
            spread_recip(BATCHES * PAIRS - 1, (PAIRS - 1) % NR)

            last = Turn(BATCHES)
            sp.wait_ge(filled, last.upto("w2"))
            sp.wait_ge(drained, last.upto("w2"))

            def load_expert(e):
                for half, w in enumerate((w_in, w_out)):
                    if e >= 2:
                        sp.wait_ge(exp_lo, 2 * (e - 2) + half + 1)
                    c = 2 if half == 0 else 4
                    sp.dma_start(raw[:, e % 2, half, :].rearrange("p (c o) -> p c o", c=c),
                                 w[e, :, :].rearrange("(c p) o -> p c o", p=P)).then_inc(raw_in[e % 2][half], 16)

            for e in range(EARLY_EXPERTS):
                load_expert(e)
            sp.wait_ge(pad_ready, 1)
            for e in range(EXPERTS):
                row = sp.value_load(padi[0:1, e:e + 1], min_val=0, max_val=NOWHERE - P)
                sp.dma_start(xs[bass.ds(row, P), :], pad_rows[:, :]).then_inc(pad_done, 16)

            sp.wait_ge(table_ready, 1)
            sp.wait_ge(pad_done, 16 * (EXPERTS + 1))
            sp.wait_ge(scattered, sent(BATCHES))

            def load_rows(j, u, reuse):
                row = sp.value_load(table[0:1, 1, bass.ds(j, 1)], min_val=0, max_val=NOWHERE)
                if reuse is not None:
                    sp.wait_ge(y_out[u % 3], reuse)
                sp.dma_start(xt_rows[:, u, :], xs[bass.ds(row, P), :]).then_inc(rows_in[u], 16)

            for u in range(UNROLL):
                load_rows(u, u, None)
            for e in range(EARLY_EXPERTS, EXPERTS):
                load_expert(e)
            with sp.Fori(1, FT // UNROLL) as i:
                for u in range(UNROLL):
                    load_rows(i * UNROLL + u, u, i * 32 - 16 + 16 * (u // 3))

            sp.wait_ge(fin_clear, 1)
            for u in range(3):
                sp.wait_ge(y_out[u], 16 * (FT // 3))
            for b in range(BATCHES):
                sp.dma_start(fin_in[:, b, 0:TT - 1, :],
                             ys[b * SEQ:b * SEQ + (TT - 1) * P, :].rearrange("(t p) f -> p t f", p=P)
                             ).then_inc(fin_loaded[b], 16)
                sp.dma_start(fin_in[0:LAST, b, TT - 1, :],
                             ys[b * SEQ + (TT - 1) * P:(b + 1) * SEQ, :]).then_inc(fin_loaded[b], 16)

        @block.gpsimd
        def _(pool):
            g = nc.gpsimd
            link = Link(pool_link, pool)

            def tick(before):
                pool.wait_ge(ticked, before + 1)
                g.tensor_tensor(tick_pool[:, :], eps_c[0:1, 0:1], eps_c[0:1, 0:1], ALU.add).then_inc(ticked, 1)

            g.memset(x_sb[:, TT - 1, :], 0.0).then_inc(consts, 1)
            g.memset(tick_pool[:, :], 0.0).then_inc(ticked, 1)
            g.memset(eps_c[:, :], EPS)
            g.memset(minus_half[:, :], -0.5)
            link(g.memset(ident[:, :], 0.0))
            g.affine_select(out=ident[:, :], in_=ident[:, :], compare_op=ALU.not_equal, fill=1.0, base=0,
                            pattern=[[-1, P]], channel_multiplier=1).then_inc(consts, 1)

            def other_constants():
                g.memset(ones_m[:, :], 1.0)
                g.memset(before_m[:, :], 1.0)
                g.memset(causal[:, :], 1.0)
                g.memset(win_causal[:, :], 1.0)
                g.memset(valid8[:, :, :], 1.0)
                g.memset(beyond[:, :, :], 0.0)
                g.memset(pad_rows[:, 0:DM], 0.0)
                g.memset(pad_rows[:, DM + 1:ROW], 0.0)
                g.memset(pad_rows[:, DM:DM + 1].bitcast(I32), OFF)
                g.memset(carry[:, 1:, :], 0.0)
                g.iota(iota8[:, :, :], [[0, TT], [1, EXPERTS]], base=0, channel_multiplier=0,
                       allow_small_or_imprecise_dtypes=True)
                g.iota(place[:, :, :], [[TOPK * P, TT], [1, TOPK]], base=0, channel_multiplier=TOPK,
                       allow_small_or_imprecise_dtypes=True)
                g.iota(carry[:, 0, :], [[CAP, EXPERTS]], base=0, channel_multiplier=0,
                       allow_small_or_imprecise_dtypes=True)
                g.iota(carry0[:, :], [[CAP, EXPERTS]], base=0, channel_multiplier=0,
                       allow_small_or_imprecise_dtypes=True)
                link(g.iota(iota_j[:, :], [[1, FT]], base=0, channel_multiplier=0,
                            allow_small_or_imprecise_dtypes=True))
                g.affine_select(out=before_m[:, :], in_=before_m[:, :], compare_op=ALU.is_ge, fill=0.0, base=-1,
                                pattern=[[1, P]], channel_multiplier=-1)
                g.affine_select(out=causal[:, :], in_=causal[:, :], compare_op=ALU.is_ge, fill=0.0, base=0,
                                pattern=[[1, P]], channel_multiplier=-1)
                g.affine_select(out=win_causal[:, W2:2 * W2], in_=win_causal[:, W2:2 * W2], compare_op=ALU.is_ge,
                                fill=0.0, base=0, pattern=[[1, W2]], channel_multiplier=-1)
                g.affine_select(out=win_causal[:, 0:W2], in_=win_causal[:, 0:W2], compare_op=ALU.is_ge, fill=0.0,
                                base=WINDOW - 1 - 2 * P, pattern=[[-1, W2]], channel_multiplier=1)
                g.affine_select(out=valid8[:, TT - 1, :], in_=valid8[:, TT - 1, :], compare_op=ALU.is_ge, fill=0.0,
                                base=LAST - 1, pattern=[[0, EXPERTS]], channel_multiplier=-1)
                g.affine_select(out=beyond[:, TT - 1, :], in_=beyond[:, TT - 1, :], compare_op=ALU.is_ge,
                                fill=float(OFF), base=LAST - 1, pattern=[[0, TOPK]], channel_multiplier=-1
                                ).then_inc(consts, 1)

            def rstd(which, mv, ve, r, count):
                pool.wait_ge(var_ready[which], count)
                link(g.tensor_tensor(ve[:, :], mv[:, :, 1], eps_c[:, :], ALU.add))
                g.tensor_tensor(r[:, :], ve[:, :], minus_half[:, :], ALU.pow).then_inc(rstd_ready[which], 1)

            def front_sum(b):
                pool.wait_ge(x_in, 32 * (b + 1))
                if not isinstance(b, int) or b > 0:
                    pool.wait_ge(z_ready, b)
                g.tensor_tensor(xsum[:, :, :], x_sb[:, :, 0:DM], x_sb[:, :, DM:2 * DM], ALU.add
                                ).then_inc(x_summed, 1)
                pool.wait_ge(x_summed, b + 1)
                g.tensor_tensor(xsum[:, :, :], xsum[:, :, :],
                                bias2[:, :].unsqueeze(1).to_broadcast([P, TT, DM]),
                                ALU.add).then_inc(xsum_ready, 1)

            def front_affine(b):
                pool.wait_ge(z_ready, b + 1)
                link(g.tensor_tensor(xsum[:, :, :], y_sb[:, :, :],
                                     gamma_b[:, :].unsqueeze(1).to_broadcast([P, TT, DM]), ALU.mult))
                g.tensor_tensor(h_batch(b), xsum[:, :, :],
                                beta_b[:, :].unsqueeze(1).to_broadcast([P, TT, DM]),
                                ALU.add).then_inc(h1_ready, 1)

            def front(b):
                rstd(0, mv1, ve1, rstd1, b + 1)
                front_affine(b)
                rstd(1, mv2, ve2, rstd2, b + 1)

            def dispatch(b):
                pool.wait_ge(slots_ready, b + 1)
                pool.wait_ge(copy_ready, b + 1)
                tick(b)
                for t in range(TT):
                    for k in range(TOPK):
                        g.indirect_dma_start(
                            out=xs, out_offset=bass.IndirectOffsetOnAxis(ap=slot[:, t, k:k + 1], axis=0),
                            in_=payload[:, k, t, :], in_offset=None,
                            bounds_check=EXPERTS * CAP - 1, oob_is_err=False).then_inc(scattered, 16)

            def divide(n, p):
                slot = p % NR
                pool.wait_ge(recip_in[slot], recip_uses(n, p) * 32)
                for half in range(2):
                    rows = slice(64 * half, 64 * half + 64)
                    last = g.tensor_tensor(ot[rows, p, :], ring[rows, slot, half, :], recip[rows, slot, :], ALU.mult)
                last.then_inc(normed, 1)

            pool.wait_ge(consts_in, 48)
            link(g.tensor_tensor(bias2[:, :], bias2[:, :], bias2[:, :], ALU.add))
            front_sum(0)
            other_constants()
            front(0)

            def late_divides(b, all_rows_end):
                all_rows_end()
                for p in (PAIRS - 2, PAIRS - 1):
                    divide(b * PAIRS + p, p)
                pool.wait_ge(normed, (b + 1) * PAIRS)

            def turn(tn):
                b = tn.b
                first = b * PAIRS
                if tn.front:
                    front_sum(b + 1)
                if tn.back:
                    late_divides(b - 1, lambda: pool.wait_ge(xsum_ready, b + 2) if tn.front else None)
                if not isinstance(b, int) or b > 1:
                    dispatch(b - 2)
                if tn.front:
                    rstd(0, mv1, ve1, rstd1, b + 2)
                    front_affine(b + 1)
                    rstd(1, mv2, ve2, rstd2, b + 2)
                if tn.back:
                    rstd(2, mv3, ve3, rstd3, b)
                    pool.wait_ge(rstd_ready[2], b)
                else:
                    pool.wait_ge(rstd_ready[1], b + 2)
                if not isinstance(b, int) or b > 1:
                    pool.wait_ge(scattered, sent(b - 1))
                for p in range(PAIRS - 2):
                    divide(first + p, p)
                pool.wait_ge(normed, first + (PAIRS - 2))

            loop_links = 4
            turn(Turn(0))
            turn(Turn(1))
            base = link.n
            with pool.Fori(2, BATCHES - 1) as b:
                link.n = (b - 2) * loop_links + base
                turn(Turn(b))
            link.n = base + loop_links * (BATCHES - 3)
            turn(Turn(BATCHES - 1))
            late_divides(BATCHES - 1, lambda: None)
            dispatch(BATCHES - 2)
            rstd(2, mv3, ve3, rstd3, BATCHES)
            dispatch(BATCHES - 1)

            def scatter(j_done, u, fresh):
                pool.wait_ge(fy_done, j_done)
                tick(j_done + (BATCHES - 1))
                g.indirect_dma_start(
                    out=ys.rearrange("t (k d) -> (t k) d", k=TOPK),
                    out_offset=bass.IndirectOffsetOnAxis(ap=xt_rows[:, u, DM:DM + 1].bitcast(I32), axis=0),
                    in_=y_rows[:, u % 3, :], in_offset=None,
                    bounds_check=TOPK * TOK - 1, oob_is_err=False).then_inc(y_out[u % 3], 16)

            with pool.Fori(0, FT // UNROLL) as i:
                for u in range(UNROLL):
                    scatter(i * UNROLL + (u + 1), u, False)

        @block.scalar
        def _(act):
            s = nc.scalar
            F = ACT.Copy

            for src, dst in ((conv_b, bias2), (gamma, gamma_b), (beta, beta_b)):
                act.dma_start(dst[:, :], src.partition_broadcast(P)).then_inc(consts_in, 16)
            act.wait_ge(weights_in[0], 16)
            s.activation(cwh[:, :, :].rearrange("p c o -> p (c o)"), stage[:, ST_CONV:ST_Q], F
                         ).then_inc(split_hi, 1)

            def hi(tn, name, dst, width, src=None):
                act.wait_ge(filled, tn.upto(name))
                s.activation(dst, general(tn, name, width) if src is None else src, F).then_inc(hi_done, 1)

            def xt_hi(tn):
                for t in range(TT):
                    hi(tn, XT[t], xth[:, t, :], 512)

            def xnt_hi(tn):
                for c in range(2):
                    hi(tn, XNT[c], xnh[:, c, :], TT * P)

            xt_hi(Turn(-1))
            act.wait_ge(weights_in[1], 48)
            s.activation(wqh[:, :, :].rearrange("p c o -> p (c o)"), stage[:, ST_Q:ST_KV], F).then_inc(split_hi, 1)
            s.activation(wkvh[:, :, :, :].rearrange("p w c o -> p (w c o)"),
                         stage[:, ST_KV:ST_KV + 4 * KV * HD], F).then_inc(split_hi, 1)
            xnt_hi(Turn(-1))

            def raise_a(n, p):
                act.wait_ge(pv_done, 2 * n + 1)
                if not isinstance(n, int) or n >= NR:
                    act.wait_ge(normed, n - (NR - 1))
                s.activation(ring[:, p % NR, 0, :], ps[:, O_BANK, 0:QW], F).then_inc(raised[0], 1)

            def q_hi(tn, j):
                act.wait_ge(filled, tn.upto(f"q{j}"))
                src = general(tn, f"q{j}", QW)
                s.activation(qs[LOWER, 0, j, :], src[LOWER, :], F)
                s.activation(qs[UPPER, 1, j, :], src[UPPER, :], F).then_inc(hi_done, 1)

            def turn(tn):
                b = tn.b
                for c in range(2):
                    act.wait_ge(filled, tn.upto(f"k{c}"))
                    src = general(tn, f"k{c}", TT * P)
                    for own, other, g in ((LOWER, UPPER, 2 * c), (UPPER, LOWER, 2 * c + 1)):
                        s.activation(kh[other, g, :], src[own, :], F)
                        last = s.activation(kh[own, g, :], src[own, :], F)
                    last.then_inc(hi_done, 1)
                for j in range(EARLY_Q):
                    q_hi(tn, j)
                    if j in LATE_PAIRS and not (isinstance(b, int) and b == 0):
                        pair = LATE_PAIRS[j]
                        raise_a((b - 1) * PAIRS + pair, pair)
                for p in range(PAIRS):
                    n = b * PAIRS + p
                    if p == 0 and isinstance(b, int) and b == 0:
                        act.wait_ge(split_lo, 3)
                    if p == 1:
                        for j in range(EARLY_Q, PAIRS):
                            q_hi(tn, j)
                    act.wait_ge(scores, n + 1)
                    if not (isinstance(b, int) and b == 0 and p < NP_):
                        act.wait_ge(pv_done, 2 * n + (2 - 2 * NP_))
                    buf = prob[:, p % NP_, :]
                    s.activation(buf.rearrange("p (r c) -> p r c", r=3), ps[:, S_BANK:S_BANK + 3, 0:REG],
                                 ACT.Tanh, scale=SCALE / SOFTCAP).then_inc(capped, 1)
                    if p == 5 and tn.back:
                        gate(tn)
                    act.wait_ge(capped, n + 1)
                    s.activation(buf, buf, ACT.Exp, scale=SOFTCAP).then_inc(exped, 1)
                    if p >= LAG:
                        raise_a(n - LAG, p - LAG)
                    if p == 0 and tn.front:
                        xt_hi(tn)
                    if p == 4 and tn.back:
                        copy_rows(b - 1)
                    if p == 5 and tn.back:
                        router_exp(b - 1)
                    if p == 6 and tn.front:
                        xnt_hi(tn)

            def copy_rows(b):
                act.wait_ge(xn2_ready, b + 1)
                s.activation(payload[:, 1, :, 0:DM], payload[:, 0, :, 0:DM], F).then_inc(copy_ready, 1)

            def gate(tn):
                act.wait_ge(filled, tn.upto("g"))
                s.activation(gate_t[:, :], general(tn, "g", TT * P)[0:GATE, :], ACT.Gelu,
                             bias=bg1_sb[:, 0:1]).then_inc(gate_ready, 1)

            def router_exp(b):
                act.wait_ge(shift_ready, b + 1)
                s.activation(expd[:, :, :], shifted[:, :, :], ACT.Exp).then_inc(expd_ready, 1)

            turns(act.Fori, turn)

            def expert_hi(e):
                for half, dst in enumerate((wih, woh)):
                    act.wait_ge(raw_in[e % 2][half], 16 * (e // 2 + 1))
                    s.activation(dst[:, e * 1024:(e + 1) * 1024], raw[:, e % 2, half, :], F).then_inc(exp_hi, 1)

            last = Turn(BATCHES)
            for pair in (PAIRS - 2, PAIRS - 1):
                raise_a((BATCHES - 1) * PAIRS + pair, pair)
            expert_hi(0)
            copy_rows(BATCHES - 1)
            expert_hi(1)
            gate(last)
            router_exp(BATCHES - 1)
            for e in range(2, EXPERTS):
                expert_hi(e)

            def fx_high(n, u):
                act.wait_ge(fx_filled, n + 1)
                s.activation(fxh[:, u % 2, :], ps[:, u % 2, 0:2 * P], F).then_inc(fx_hi, 1)

            def gelu(n, u):
                act.wait_ge(fh_filled, n + 1)
                s.activation(act_h[:, u % 2, :], ps[:, 2 + u % 2, :], ACT.Gelu).then_inc(gelued, 1)

            def ft_high(n, u):
                for half, cols in enumerate(HALVES):
                    act.wait_ge(ft_filled, n * 2 + (half + 1))
                    s.activation(fhh[:, u % 2, cols], ps[:, 4 + half, 0:HID // 2], F).then_inc(ft_hi, 1)

            def six(base, more):
                for u in range(UNROLL):
                    j = base + u
                    ft_high(j, u)
                    if more or u + 1 < UNROLL:
                        gelu(j + 1, u + 1)
                    if more or u + 2 < UNROLL:
                        fx_high(j + 2, u + 2)

            fx_high(0, 0)
            fx_high(1, 1)
            gelu(0, 0)
            with act.Fori(0, FT // UNROLL - 1) as i:
                six(i * UNROLL, True)
            six(FT - UNROLL, False)

            for b in range(BATCHES):
                act.wait_ge(fin_ready, b + 1)
                act.dma_start(out[b, 0:(TT - 1) * P, :].rearrange("(t p) f -> p t f", p=P),
                              fin_in[:, b, 0:TT - 1, 0:DM]).then_inc(fin_stored, 16)
                act.dma_start(out[b, (TT - 1) * P:SEQ, :], fin_in[0:LAST, b, TT - 1, 0:DM]
                              ).then_inc(fin_stored, 16)
            act.wait_ge(fin_stored, 32 * BATCHES)

        @block.vector
        def _(dve):
            v = nc.vector
            link = Link(dve_link, dve)

            def tick():
                return v.memset(tick_dve[:, :], 0.0)

            def split_low(dst_lo, src, hi_ap, count):
                dve.wait_ge(split_hi, count)
                v.tensor_tensor(dst_lo, src, hi_ap.bitcast(F32), ALU.subtract).then_inc(split_lo, 1)

            split_low(cwl[:, :, :].rearrange("p c o -> p (c o)"), stage[:, ST_CONV:ST_Q],
                      cwh[:, :, :].rearrange("p c o -> p (c o)"), 1)

            def lo(tn, name, dst, hi_ap, width, nth):
                dve.wait_ge(hi_done, nth)
                v.tensor_tensor(dst, general(tn, name, width), hi_ap.bitcast(F32),
                                ALU.subtract).then_inc(drained, 1)

            def hi_count(b, k):
                return b * 15 + (5 + k)

            def xt_lo(tn, first):
                for t in range(TT):
                    lo(tn, XT[t], xtl[:, t, :], xth[:, t, :], 512, first + t + 1)

            def xnt_lo(tn, first):
                for c in range(2):
                    lo(tn, XNT[c], xnl[:, c, :], xnh[:, c, :], TT * P, first + c + 1)

            def moments(src, mv, which, st):
                tick()
                for t in range(TT):
                    last = v.bn_stats(st[:, t, :], src(t))
                link(last)
                tick()
                for t in range(TT):
                    last = v.bn_aggr(mv[:, t, :], st[:, t, :])
                last.then_inc(var_ready[which], 1)

            def conv_add(tn, b):
                dve.wait_ge(xsum_ready, b + 1)
                for t in range(TT):
                    dve.wait_ge(filled, tn.upto(CV[t]))
                    v.scalar_tensor_tensor(y_sb[:, t, :], xsum[:, t, :], 0.5, general(tn, CV[t], DM),
                                           ALU.mult, ALU.add).then_inc(drained, 1)
                dve.wait_ge(drained, tn.upto(CV[TT - 1]))
                moments(lambda t: y_sb[:, t, :], mv1, 0, stats)

            def norm(dst, src, mv, r, which, count, done):
                dve.wait_ge(rstd_ready[which], count)
                for t in range(TT):
                    last = v.tensor_scalar(dst(t), src(t), mv[:, t, 0:1], r[:, t:t + 1], ALU.subtract, ALU.mult)
                last.then_inc(done, 1)

            def front_norm(b):
                norm(lambda t: y_sb[:, t, :], lambda t: y_sb[:, t, :], mv1, rstd1, 0, b + 1, z_ready)

            def front_moments(b):
                dve.wait_ge(h1_ready, b + 1)
                moments(lambda t: h_tile(b, t), mv2, 1, stats)

            def front_xn(b):
                norm(lambda t: xn[:, t, :], lambda t: h_tile(b, t), mv2, rstd2, 1, b + 1, xn_ready)

            def residual(tn, b):
                for t in range(TT):
                    dve.wait_ge(filled, tn.upto(WO[t]))
                    v.tensor_tensor(h_tile(b, t), general(tn, WO[t], DM), h_tile(b, t), ALU.add
                                    ).then_inc(drained, 1)
                dve.wait_ge(drained, tn.upto(WO[TT - 1]))
                moments(lambda t: h_tile(b, t), mv3, 2, stats3)

            def back_xn(b):
                if not isinstance(b, int) or b > 0:
                    dve.wait_ge(scattered, sent(b))
                norm(lambda t: payload[:, 0, t, 0:DM], lambda t: h_tile(b, t), mv3, rstd3, 2, b + 1, xn2_ready)

            def x2t_copy(tn):
                for c in range(2):
                    dve.wait_ge(filled, tn.upto(X2T[c]))
                    v.tensor_copy(x2t[:, c, :], general(tn, X2T[c], TT * P)).then_inc(drained, 1)

            def shift(tn, b):
                dve.wait_ge(filled, tn.upto("l"))
                src = general(tn, "l", TT * EXPERTS).rearrange("p (t e) -> p t e", t=TT)
                link(v.tensor_reduce(mx[:, :, :], src, AX.X, ALU.max))
                v.tensor_tensor(shifted[:, :, :], src, mx[:, :, :].to_broadcast([P, TT, EXPERTS]),
                                ALU.subtract).then_inc(shift_ready, 1)
                dve.wait_ge(shift_ready, b + 1)
                tick().then_inc(drained, 2)

            def choose(b):
                dve.wait_ge(expd_ready, b + 1)
                link(v.tensor_reduce(denom[:, :, :], expd[:, :, :], AX.X, ALU.add))
                link(v.reciprocal(rdenom[:, :, :], denom[:, :, :]))
                link(v.tensor_tensor(probs[:, :, :], expd[:, :, :],
                                     rdenom[:, :, :].to_broadcast([P, TT, EXPERTS]), ALU.mult))
                tick()
                for t in range(TT):
                    last = v.max(top8[:, t, :], probs[:, t, :])
                link(last)
                tick()
                for t in range(TT):
                    last = v.max_index(idx8[:, t, :], top8[:, t, :], probs[:, t, :])
                link(last)
                for k in range(TOPK):
                    v.tensor_copy(payload[:, k, :, DM:DM + 1].bitcast(I32), place[:, :, k:k + 1])
                    v.tensor_copy(payload[:, k, :, DM + 1:ROW], top8[:, :, k:k + 1])
                link(v.tensor_copy(idxf[:, :, :], idx8[:, :, 0:TOPK]))
                v.tensor_tensor(hot0[:, :, :], iota8[:, :, :], idxf[:, :, 0:1].to_broadcast([P, TT, EXPERTS]),
                                ALU.is_equal)
                link(v.tensor_tensor(hot1[:, :, :], iota8[:, :, :],
                                     idxf[:, :, 1:2].to_broadcast([P, TT, EXPERTS]), ALU.is_equal))
                v.tensor_scalar(place[:, :, :], place[:, :, :], float(TOPK * SEQ), None, ALU.add)
                link(v.tensor_tensor(hots[:, :, :], hot0[:, :, :], hot1[:, :, :], ALU.add))
                v.tensor_tensor(chosen[:, :, :], hots[:, :, :], valid8[:, :, :], ALU.mult
                                ).then_inc(chosen_ready, 1)

            def slots(tn, b):
                dve.wait_ge(filled, tn.upto("tot"))
                tot = general(tn, "tot", TT * EXPERTS).rearrange("p (t e) -> p t e", t=TT)
                tri = general(tn, "tri", TT * EXPERTS).rearrange("p (t e) -> p t e", t=TT)
                for t in range(TT):
                    link(v.tensor_tensor(carry[:, t + 1, :], carry[:, t, :], tot[:, t, :], ALU.add))
                link(v.tensor_tensor(rank[:, :, :], carry[:, 0:TT, :], tri, ALU.add))
                tick().then_inc(drained, 2)
                v.tensor_tensor(pick0[:, :, :], hot0[:, :, :], rank[:, :, :], ALU.mult)
                v.tensor_copy(carry[:, 0, :], carry[:, TT, :])
                link(v.tensor_tensor(pick1[:, :, :], hot1[:, :, :], rank[:, :, :], ALU.mult))
                v.tensor_reduce(slotf[:, :, 0:1], pick0[:, :, :], AX.X, ALU.add)
                link(v.tensor_reduce(slotf[:, :, 1:2], pick1[:, :, :], AX.X, ALU.add))
                link(v.tensor_tensor(slotg[:, :, :], slotf[:, :, :], beyond[:, :, :], ALU.add))
                v.tensor_copy(slot[:, :, :], slotg[:, :, :]).then_inc(slots_ready, 1)

            def raise_b(n, p):
                dve.wait_ge(pv_done, 2 * n + 2)
                if not isinstance(n, int) or n >= NR:
                    dve.wait_ge(normed, n - (NR - 1))
                v.tensor_copy(ring[:, p % NR, 1, :], ps[:, O_BANK + 1, 0:QW]).then_inc(raised[1], 1)

            def invert(n, p):
                slot_ = p % NR
                dve.wait_ge(sums_in[slot_], recip_uses(n, p) * 32)
                v.reciprocal(rsums[:, slot_, :], sums[:, slot_, :]).then_inc(rsums_ready, 1)

            def mask(n, p):
                dve.wait_ge(exped, n + 1)
                r = prob[:, p % NP_, :]
                a = r[:, 0:2 * REG].rearrange("p (r c) -> p r c", r=2)
                v.tensor_tensor(a[:, :, 0:P], a[:, :, 0:P], causal[:, :].unsqueeze(1).to_broadcast([P, 2, P]),
                                ALU.mult)
                v.tensor_tensor(a[:, :, 2 * P:REG], a[:, :, 2 * P:REG],
                                win_causal[:, :].unsqueeze(1).to_broadcast([P, 2, 2 * W2]), ALU.mult)
                c = r[:, 2 * REG:3 * REG].rearrange("p (r c) -> p r c", r=2)
                v.tensor_tensor(c[:, :, 0:P], c[:, :, 0:P], causal[:, :].unsqueeze(1).to_broadcast([P, 2, P]),
                                ALU.mult).then_inc(masked, 1)

            first = Turn(-1)
            v.memset(kl[:, :, :].bitcast(F32), 0.0)
            v.memset(vo[:, :, :, :], 1.0).then_inc(kv_clear, 1)
            xt_lo(first, 0)
            conv_add(first, 0)
            front_norm(0)
            front_moments(0)
            dve.wait_ge(weights_in[1], 48)
            split_low(wql[:, :, :].rearrange("p c o -> p (c o)"), stage[:, ST_Q:ST_KV],
                      wqh[:, :, :].rearrange("p c o -> p (c o)"), 2)
            split_low(wkvl[:, :, :, :].rearrange("p w c o -> p (w c o)"), stage[:, ST_KV:ST_KV + 4 * KV * HD],
                      wkvh[:, :, :, :].rearrange("p w c o -> p (w c o)"), 3)
            front_xn(0)
            xnt_lo(first, 3)
            dve.wait_ge(consts, 3)
            dve.wait_ge(kv_clear, 1)

            def q_low(tn, j, nth):
                dve.wait_ge(hi_done, hi_count(tn.b, nth))
                src = general(tn, f"q{j}", QW)
                for own, other, head in ((LOWER, UPPER, 0), (UPPER, LOWER, 1)):
                    last = v.tensor_tensor(qs[other, head, j, :], src[own, :],
                                           qs[own, head, j, :].bitcast(F32), ALU.subtract)
                last.then_inc(drained, 1)

            def qk_low(tn):
                b = tn.b
                for c in range(2):
                    dve.wait_ge(hi_done, hi_count(b, c + 1))
                    src = general(tn, f"k{c}", TT * P)
                    for own, g in ((LOWER, 2 * c), (UPPER, 2 * c + 1)):
                        last = v.tensor_tensor(kl[own, g, :], src[own, :], kh[own, g, :].bitcast(F32), ALU.subtract)
                    last.then_inc(drained, 1)
                for j in range(EARLY_Q):
                    q_low(tn, j, j + 3)
                    if not (isinstance(b, int) and b == 0):
                        before = (b - 1) * PAIRS
                        if j in LATE_PAIRS:
                            pair = LATE_PAIRS[j]
                            raise_b(before + pair, pair)
                        if j == 2:
                            invert(before + PAIRS - 3, PAIRS - 3)
                        if j == 5:
                            invert(before + PAIRS - 2, PAIRS - 2)

            def v_copies(tn):
                for t in range(TT):
                    dve.wait_ge(filled, tn.upto(f"v{t}"))
                    src = general(tn, f"v{t}", DM).rearrange("p (g s d) -> p g s d", g=2, s=2)
                    dst = vo[:, t, :, :].rearrange("p (g s) c -> p g s c", s=2)
                    v.tensor_copy(dst[:, :, 0, 0:HD], src[:, :, 0, :])
                    v.tensor_copy(dst[:, :, 1, HD:P], src[:, :, 1, :]).then_inc(drained, 1)

            def turn(tn):
                b = tn.b
                qk_low(tn)
                for p in range(PAIRS):
                    n = b * PAIRS + p
                    if p == 0:
                        v_copies(tn)
                    if p == 7 and tn.back:
                        slots(tn, b - 1)
                    if p == 5 and tn.back:
                        x2t_copy(tn)
                    mask(n, p)
                    if p >= LAG:
                        raise_b(n - LAG, p - LAG)
                    if p == 0:
                        if not (isinstance(b, int) and b == 0):
                            invert(n - 1, PAIRS - 1)
                        if tn.front:
                            xt_lo(tn, hi_count(b, EARLY_Q + 2))
                        for j in range(EARLY_Q, PAIRS):
                            q_low(tn, j, j + 3 + (TT if tn.front else 0))
                    if p == 1 and tn.front:
                        conv_add(tn, b + 1)
                        front_norm(b + 1)
                    if p == 2:
                        if tn.front:
                            front_moments(b + 1)
                        if tn.back:
                            residual(tn, b - 1)
                    if p == 3:
                        if tn.back:
                            back_xn(b - 1)
                        if tn.front:
                            front_xn(b + 1)
                    if p == 5 and tn.back:
                        shift(tn, b - 1)
                        choose(b - 1)
                    if p == 6 and tn.front:
                        xnt_lo(tn, hi_count(b, PAIRS + 5))
                    if p > LAG:
                        invert(n - LAG - 1, p - LAG - 1)

            def expert_lo(e):
                for half, (dst, high) in enumerate(((wil, wih), (wol, woh))):
                    dve.wait_ge(exp_hi, 2 * e + half + 1)
                    v.tensor_tensor(dst[:, e * 1024:(e + 1) * 1024], raw[:, e % 2, half, :],
                                    high[:, e * 1024:(e + 1) * 1024].bitcast(F32), ALU.subtract
                                    ).then_inc(exp_lo, 1)

            turn(Turn(0))
            turn(Turn(1))
            start = link.n
            with dve.Fori(2, BATCHES - 1) as b:
                link.n = (b - 2) * LINKS + start
                turn(Turn(b))
            link.n = start + LINKS * (BATCHES - 3)
            before_last = link.n
            turn(Turn(BATCHES - 1))
            assert link.n - before_last == LINKS - 2, (link.n, before_last, LINKS)

            last_turn = Turn(BATCHES)
            last_pair = BATCHES * PAIRS - 1
            raise_b(last_pair - 1, PAIRS - 2)
            raise_b(last_pair, PAIRS - 1)
            for back in (2, 1, 0):
                invert(last_pair - back, PAIRS - 1 - back)
            residual(last_turn, BATCHES - 1)
            back_xn(BATCHES - 1)
            expert_lo(0)
            x2t_copy(last_turn)
            expert_lo(1)
            shift(last_turn, BATCHES - 1)
            choose(BATCHES - 1)
            slots(last_turn, BATCHES - 1)

            v.tensor_tensor(cntf[:, :], carry[:, 0, :], carry0[:, :], ALU.subtract)
            v.tensor_copy(padi[:, :], carry[0:1, 0, :]).then_inc(pad_ready, 1)
            dve.wait_ge(pad_ready, 1)
            link(v.tensor_scalar(cntf[:, :], cntf[:, :], float(P - 1), None, ALU.add))
            link(v.tensor_copy(cnti[:, :], cntf[:, :]))
            link(v.tensor_scalar(cnts[:, :], cnti[:, :], 7, None, ALU.logical_shift_right))
            link(v.tensor_copy(tilesf[:, :], cnts[:, :]))
            v.tensor_scalar(lag_rows[:, :], tilesf[:, :], float(-P), float(CAP), ALU.mult, ALU.add)
            link(v.tensor_copy(ends[:, 0:1], tilesf[:, 0:1]))
            for e in range(1, EXPERTS):
                link(v.tensor_tensor(ends[:, e:e + 1], ends[:, e - 1:e], tilesf[:, e:e + 1], ALU.add))
            link(v.tensor_scalar(total1[:, :], ends[0:1, EXPERTS - 1:EXPERTS], -1.0, None, ALU.add))
            v.tensor_scalar(past[:, :], iota_j[:, :], total1[:, 0:1], None, ALU.is_gt)
            link(v.tensor_scalar(tile_j[:, :], iota_j[:, :], total1[:, 0:1], None, ALU.min))
            link(v.tensor_tensor(over[:, :, :], ends[0:1, :].unsqueeze(1).to_broadcast([1, FT, EXPERTS]),
                                 tile_j[:, :].unsqueeze(2).to_broadcast([1, FT, EXPERTS]), ALU.is_le))
            v.tensor_reduce(expf[:, :], over[:, :, :], AX.X, ALU.add)
            link(v.tensor_tensor(overw[:, :, :], over[:, :, :],
                                 lag_rows[0:1, :].unsqueeze(1).to_broadcast([1, FT, EXPERTS]), ALU.mult))
            link(v.tensor_reduce(rowf[:, :], overw[:, :, :], AX.X, ALU.add))
            link(v.scalar_tensor_tensor(rowg[:, :], tile_j[:, :], float(P), rowf[:, :], ALU.mult, ALU.add))
            v.tensor_copy(table[:, 0, :], expf[:, :])
            link(v.scalar_tensor_tensor(rowh[:, :], past[:, :], float(NOWHERE), rowg[:, :], ALU.mult, ALU.add))
            link(v.tensor_scalar(rowh[:, :], rowh[:, :], float(NOWHERE), None, ALU.min))
            v.tensor_copy(table[:, 1, :], rowh[:, :]).then_inc(table_ready, 1)

            for e in range(2, EXPERTS):
                expert_lo(e)

            def fx_low(n, u):
                dve.wait_ge(fx_hi, n + 1)
                v.tensor_tensor(fxl[:, u % 2, :], ps[:, u % 2, 0:2 * P], fxh[:, u % 2, :].bitcast(F32),
                                ALU.subtract).then_inc(fx_lo, 1)

            def ft_low(n, u):
                for half, cols in enumerate(HALVES):
                    dve.wait_ge(ft_hi, n * 2 + (half + 1))
                    v.tensor_tensor(fhl[:, u % 2, cols], ps[:, 4 + half, 0:HID // 2], fhh[:, u % 2, cols].bitcast(F32),
                                    ALU.subtract).then_inc(ft_lo, 1)

            def gated(n, u, reuse):
                if reuse is not None:
                    dve.wait_ge(y_out[u % 3], reuse)
                dve.wait_ge(fy_filled, n + 1)
                v.tensor_scalar(y_rows[:, u % 3, :], ps[:, 6 + u % 2, 0:DM], xt_rows[:, u % UNROLL, DM + 1:ROW],
                                None, ALU.mult).then_inc(fy_done, 1)

            def six(i, base, head, more):
                for u in range(UNROLL):
                    j = base + u
                    ft_low(j, u)
                    if more or u + 2 < UNROLL:
                        fx_low(j + 2, u + 2)
                    gated(j, u, None if head and u < 3 else i * 32 + (16 * (u // 3)))

            fx_low(0, 0)
            fx_low(1, 1)
            six(0, 0, True, True)
            with dve.Fori(1, FT // UNROLL - 1) as i:
                six(i, i * UNROLL, False, True)
            six(FT // UNROLL - 1, FT - UNROLL, False, False)

            v.memset(fin_in[:, :, TT - 1, :], 0.0).then_inc(fin_clear, 1)
            dve.wait_ge(fin_clear, 1)
            for b in range(BATCHES):
                dve.wait_ge(fin_loaded[b], 32)
                o = fin_in[:, b, :, 0:DM]
                link(v.tensor_tensor(o, o, fin_in[:, b, :, DM:2 * DM], ALU.add))
                v.tensor_tensor(o, o, h_batch(b), ALU.add).then_inc(fin_ready, 1)

        @block.tensor
        def _(pe):
            t_ = nc.tensor

            def claim(tn, name):
                n = tn.before(name)
                if not isinstance(n, int):
                    pe.wait_ge(drained, n - 2)
                elif n >= 3:
                    pe.wait_ge(drained, n - 2)

            def three(out_ap, terms):
                steps = [(a, c) for ah, al, ch, cl in terms for a, c in ((ah, ch), (ah, cl), (al, ch))]
                for i, (a, c) in enumerate(steps):
                    last = t_.matmul(out_ap, a, c, start=(i == 0), stop=(i == len(steps) - 1))
                return last

            def transposes(tn):
                for t in range(TT):
                    claim(tn, XT[t])
                    dst = general(tn, XT[t])
                    for c in range(4):
                        last = t_.transpose(dst[:, c * P:(c + 1) * P], x_sb[:, t, c * P:(c + 1) * P], ident[:, :])
                    last.then_inc(filled, 1)

            def conv(tn):
                for t in range(TT):
                    claim(tn, CV[t])
                    if t == 0:
                        pe.wait_ge(drained, tn.upto(XT[TT - 1]))
                    three(general(tn, CV[t], DM),
                          [(xth[:, t, c * P:(c + 1) * P], xtl[:, t, c * P:(c + 1) * P], cwh[:, c, :], cwl[:, c, :])
                           for c in range(4)]).then_inc(filled, 1)

            def xn_transposes(tn, b):
                pe.wait_ge(xn_ready, b + 1)
                for c in range(2):
                    claim(tn, XNT[c])
                    dst = general(tn, XNT[c], TT * P)
                    for t in range(TT):
                        last = t_.transpose(dst[:, t * P:(t + 1) * P], xn[:, t, c * P:(c + 1) * P], ident[:, :])
                    last.then_inc(filled, 1)

            def project_query(tn, j):
                claim(tn, f"q{j}")
                three(general(tn, f"q{j}", QW),
                      [(wqh[:, c, j * P:(j + 1) * P], wql[:, c, j * P:(j + 1) * P],
                        xnh[:, c, 0:QW], xnl[:, c, 0:QW]) for c in range(2)]).then_inc(filled, 1)

            def project(tn):
                b = tn.b
                pe.wait_ge(drained, front_done(b))
                for j in range(2):
                    claim(tn, f"k{j}")
                    three(general(tn, f"k{j}", TT * P),
                          [(wkvh[:, 0, c, j * P:(j + 1) * P], wkvl[:, 0, c, j * P:(j + 1) * P],
                            xnh[:, c, :], xnl[:, c, :]) for c in range(2)]).then_inc(filled, 1)
                for j in range(EARLY_Q):
                    project_query(tn, j)
                    if j in LATE_PAIRS and not (isinstance(b, int) and b == 0):
                        pair = LATE_PAIRS[j]
                        values((b - 1) * PAIRS + pair, pair)

            def project_values(tn):
                for t in range(TT):
                    claim(tn, f"v{t}")
                    cols = slice(t * P, (t + 1) * P)
                    three(general(tn, f"v{t}", DM),
                          [(xnh[:, c, cols], xnl[:, c, cols], wkvh[:, 1, c, :], wkvl[:, 1, c, :])
                           for c in range(2)]).then_inc(filled, 1)

            def score(n, j):
                if not isinstance(n, int) or n >= 1:
                    pe.wait_ge(capped, n)
                for half in range(2):
                    g = 2 * (j // 4) + half
                    region = ps[:, S_BANK + half, :]
                    for kt, dst in ((0, region[:, 0:W0]), (2, region[:, W0:REG]),
                                    (1, ps[:, S_BANK + 2, half * W1:(half + 1) * W1])):
                        cols = slice(kt * P, (kt + 1) * P)
                        t_.matmul(dst, kh[:, g, cols], qs[:, half, j, kt * P:QW], start=True, stop=False)
                        last = t_.matmul(dst, kl[:, g, cols], qs[:, half, j, kt * P:QW], start=False, stop=True)
                last.then_inc(scores, 1)

            def values(n, p):
                pe.wait_ge(masked, n + 1)
                buf = prob[:, p % NP_, :]
                for half in range(2):
                    g = 2 * (p // 4) + half
                    if not isinstance(n, int) or n >= 1:
                        pe.wait_ge(raised[half], n)
                    dst = ps[:, O_BANK + half, :]
                    r = buf[:, half * REG:(half + 1) * REG]
                    mid = buf[:, 2 * REG + half * W1:2 * REG + (half + 1) * W1]
                    t_.matmul(dst[:, 0:QW], vo[:, 0, g, :], r[:, 0:W0], start=True, stop=False)
                    t_.matmul(dst[:, P:QW], vo[:, 1, g, :], mid, start=False, stop=False)
                    t_.matmul(dst[:, 2 * P:QW], vo[0:LAST, 2, g, :], r[0:LAST, W0:REG],
                              start=False, stop=True).then_inc(pv_done, 1)

            def output(tn, b):
                pe.wait_ge(normed, (b + 1) * PAIRS)
                for t in range(TT):
                    claim(tn, WO[t])
                    rows = P if t < TT - 1 else QW - t * P
                    for c in range(PAIRS):
                        last = t_.matmul(general(tn, WO[t], DM)[0:rows, :], ot[:, c, t * P:t * P + rows],
                                         wo_sb[:, c, :], start=(c == 0), stop=(c == PAIRS - 1))
                    last.then_inc(filled, 1)

            def x2_transposes(tn, b):
                pe.wait_ge(xn2_ready, b + 1)
                for c in range(2):
                    claim(tn, X2T[c])
                    dst = general(tn, X2T[c], TT * P)
                    for t in range(TT):
                        last = t_.transpose(dst[:, t * P:(t + 1) * P], payload[:, 0, t, c * P:(c + 1) * P],
                                            ident[:, :])
                    last.then_inc(filled, 1)

            def router_hidden(tn, b):
                claim(tn, "g")
                pe.wait_ge(drained, tn.upto(X2T[1]))
                for c in range(2):
                    last = t_.matmul(general(tn, "g", TT * P)[0:GATE, :], wg1_sb[:, c, :], x2t[:, c, :],
                                     start=(c == 0), stop=(c == 1))
                last.then_inc(filled, 1)

            def router_logits(tn, b):
                claim(tn, "l")
                pe.wait_ge(gate_ready, b + 1)
                for t in range(TT):
                    last = t_.matmul(general(tn, "l")[:, t * EXPERTS:(t + 1) * EXPERTS],
                                     gate_t[:, t * P:(t + 1) * P], wg2_sb[:, :], start=True, stop=True)
                last.then_inc(filled, 1)

            def counts(tn, b):
                pe.wait_ge(chosen_ready, b + 1)
                for name, m in (("tri", before_m), ("tot", ones_m)):
                    claim(tn, name)
                    t_.matmul(general(tn, name, TT * EXPERTS), m[:, :],
                              chosen[:, :, :].rearrange("p t e -> p (t e)"), start=True, stop=True
                              ).then_inc(filled, 1)

            first = Turn(-1)
            pe.wait_ge(consts, 2)
            pe.wait_ge(x_in, 32)
            transposes(first)
            pe.wait_ge(split_lo, 1)
            conv(first)
            xn_transposes(first, 0)
            pe.wait_ge(split_lo, 3)
            pe.wait_ge(consts, 3)

            def turn(tn):
                b = tn.b
                project(tn)
                for p in range(PAIRS):
                    n = b * PAIRS + p
                    pe.wait_ge(drained, tn.upto(f"q{p}"))
                    score(n, p)
                    if p == 0:
                        project_values(tn)
                        if tn.front:
                            pe.wait_ge(x_in, 32 * (b + 2))
                            transposes(tn)
                    if p == 5 and tn.back:
                        router_hidden(tn, b - 1)
                    if p == 7 and tn.back:
                        counts(tn, b - 1)
                    if p == LAG:
                        pe.wait_ge(drained, tn.upto("v2"))
                    if p >= LAG:
                        values(n - LAG, p - LAG)
                    if p == 1:
                        for j in range(EARLY_Q, PAIRS):
                            project_query(tn, j)
                        if tn.front:
                            conv(tn)
                    if p == 2 and tn.back:
                        pe.wait_ge(weights_in[2], 64)
                        output(tn, b - 1)
                    if p == 4 and tn.back:
                        x2_transposes(tn, b - 1)
                    if p == 5 and tn.back:
                        router_logits(tn, b - 1)
                    if p == 6 and tn.front:
                        xn_transposes(tn, b + 1)

            turns(pe.Fori, turn)
            last_turn = Turn(BATCHES)
            for pair in (PAIRS - 2, PAIRS - 1):
                values((BATCHES - 1) * PAIRS + pair, pair)
            output(last_turn, BATCHES - 1)
            x2_transposes(last_turn, BATCHES - 1)
            router_hidden(last_turn, BATCHES - 1)
            router_logits(last_turn, BATCHES - 1)
            counts(last_turn, BATCHES - 1)

            def row_transposes(n, u, i):
                pe.wait_ge(rows_in[u % UNROLL], (i + 1) * 16)
                if not isinstance(n, int) or n >= 2:
                    pe.wait_ge(fx_lo, n - 1)
                for c in range(2):
                    last = t_.transpose(ps[:, u % 2, c * P:(c + 1) * P],
                                        xt_rows[:, u % UNROLL, c * P:(c + 1) * P], ident[:, :])
                last.then_inc(fx_filled, 1)

            def up(n, u, e):
                pe.wait_ge(fx_lo, n + 1)
                if not isinstance(n, int) or n >= 2:
                    pe.wait_ge(gelued, n - 1)
                three(ps[:, 2 + u % 2, :],
                      [(fxh[:, u % 2, c * P:(c + 1) * P], fxl[:, u % 2, c * P:(c + 1) * P],
                        wih[:, bass.ds(e * 1024 + c * HID, HID)], wil[:, bass.ds(e * 1024 + c * HID, HID)])
                       for c in range(2)]).then_inc(fh_filled, 1)

            def h_transposes(n, u):
                pe.wait_ge(gelued, n + 1)
                for half in range(2):
                    if not isinstance(n, int) or n >= 1:
                        pe.wait_ge(ft_lo, n * 2 + (half - 1))
                    for c in (2 * half, 2 * half + 1):
                        last = t_.transpose(ps[:, 4 + half, c % 2 * P:(c % 2 + 1) * P],
                                            act_h[:, u % 2, c * P:(c + 1) * P], ident[:, :])
                    last.then_inc(ft_filled, 1)

            def down(n, u, e):
                if not isinstance(n, int) or n >= 2:
                    pe.wait_ge(fy_done, n - 1)
                dst = ps[:, 6 + u % 2, 0:DM]
                for half in range(2):
                    pe.wait_ge(ft_lo, n * 2 + (half + 1))
                    for c in (2 * half, 2 * half + 1):
                        cols = slice(c * P, (c + 1) * P)
                        at = bass.ds(e * 1024 + c * DM, DM)
                        t_.matmul(dst, fhh[:, u % 2, cols], woh[:, at], start=(c == 0), stop=False)
                        t_.matmul(dst, fhh[:, u % 2, cols], wol[:, at], start=False, stop=False)
                        last = t_.matmul(dst, fhl[:, u % 2, cols], woh[:, at], start=False, stop=(c == 3))
                last.then_inc(fy_filled, 1)

            def expert_of(j):
                e = pe.value_load(table[0:1, 0, bass.ds(j, 1)], min_val=0, max_val=EXPERTS - 1)
                pe.wait_ge(exp_lo, e * 2 + 2)
                return e

            def six(i, base, more):
                e = expert_of(base)
                for u in range(UNROLL):
                    j = base + u
                    h_transposes(j, u)
                    if more or u + 1 < UNROLL:
                        after = expert_of(j + 1)
                        up(j + 1, u + 1, after)
                    if more or u + 2 < UNROLL:
                        row_transposes(j + 2, u + 2, i if u + 2 < UNROLL else i + 1)
                    down(j, u, e)
                    e = after

            pe.wait_ge(table_ready, 1)
            row_transposes(0, 0, 0)
            row_transposes(1, 1, 0)
            up(0, 0, expert_of(0))
            six(0, 0, True)
            with pe.Fori(1, FT // UNROLL - 1) as i:
                six(i, i * UNROLL, True)
            six(FT // UNROLL - 1, FT - UNROLL, False)


LINKS = 19


def kernel(x, L0_tok_conv_w, L0_tok_conv_b, L0_tok_ln_gamma, L0_tok_ln_beta, L0_attn_Wq, L0_attn_Wk, L0_attn_Wv,
           L0_attn_Wo, L0_ffn_wg1, L0_ffn_bg1, L0_ffn_wg2, L0_ffn_w_in, L0_ffn_w_out):
    import numpy as np
    import concourse.bacc as bacc
    from concourse.bass_utils import run_bass_kernel_spmd

    def paired(w):
        w = np.asarray(w).reshape(2, 2, HEADS // KV, HD, -1)
        return w.transpose(0, 2, 1, 3, 4).reshape(HEADS * HD, -1)

    arrays = {
        "x": np.asarray(x).reshape(BATCHES, SEQ, 2 * DM),
        "conv_w": np.asarray(L0_tok_conv_w).transpose(2, 1, 0).reshape(2 * DM, DM),
        "conv_b": np.asarray(L0_tok_conv_b),
        "gamma": np.asarray(L0_tok_ln_gamma),
        "beta": np.asarray(L0_tok_ln_beta),
        "wq": paired(L0_attn_Wq).T,
        "wk": np.asarray(L0_attn_Wk).T,
        "wv": np.asarray(L0_attn_Wv).T,
        "wo": paired(np.asarray(L0_attn_Wo).T),
        "wg1": np.asarray(L0_ffn_wg1),
        "bg1": np.asarray(L0_ffn_bg1),
        "wg2": np.asarray(L0_ffn_wg2),
        "w_in": np.asarray(L0_ffn_w_in),
        "w_out": np.asarray(L0_ffn_w_out),
    }
    arrays = {n: np.ascontiguousarray(a) for n, a in arrays.items()}
    nc = bacc.Bacc("TRN2", target_bir_lowering=False, num_devices=1, dynamic_dma_scratch_size=8192)
    args = [nc.dram_tensor(n, a.shape, mybir.dt.from_np(a.dtype), kind="ExternalInput").ap()
            for n, a in arrays.items()]
    xs = nc.dram_tensor("expert_rows", (NOWHERE + P, ROW), F32).ap()
    ys = nc.dram_tensor("gated_rows", (TOK, TOPK * DM), F32).ap()
    out = nc.dram_tensor("out", (BATCHES, SEQ, DM), F32, kind="ExternalOutput").ap()
    rs_dram = nc.dram_tensor("sum_reciprocals", (NR, 2, QW), F32).ap()
    build(nc, *args, xs, ys, rs_dram, out)
    result = run_bass_kernel_spmd(nc, [arrays], core_ids=[0])
    return result.results[0]["out"]
```

```python
import concourse.bass as bass
from concourse import mybir
from contextlib import ExitStack

F32 = mybir.dt.float32
F32R = mybir.dt.float32r
I32 = mybir.dt.int32
U32 = mybir.dt.uint32
ALU = mybir.AluOpType
ACT = mybir.ActivationFunctionType
AX = mybir.AxisListType

BATCHES, FRAMES, DM = 8, 750, 256
SEQ = FRAMES // 2
P = 128
TT = -(-SEQ // P)
LAST = SEQ - (TT - 1) * P
QW = SEQ + SEQ % 2
TOK = BATCHES * SEQ
HEADS, KV, HD = 16, 4, 64
PAIRS = HEADS // 2
WINDOW = 256
SOFTCAP = 30.0
SCALE = HD ** -0.5
EPS = 1e-5
EXPERTS, HID, TOPK, GATE = 8, 512, 2, 64
CAP = TOK + P
ROW = DM + 2
FT = (TOK * TOPK + EXPERTS * (P - 1)) // P
NOWHERE = EXPERTS * CAP
OFF = 1 << 20
UNROLL = 6
HALVES = (slice(0, HID // 2), slice(HID // 2, HID))
LISTED = BATCHES - 2
FIRST = 24
REST = FT - FIRST
EW = 4 * 2 * HID
DURING = 4
assert FIRST % UNROLL == 0 and FIRST > 2 * UNROLL
assert P * FIRST + EXPERTS * (P - 1) <= LISTED * SEQ * TOPK
assert FT % UNROLL == 0 and TT == 3 and SEQ <= WINDOW + P

W0, W1, W2 = QW, QW - P, QW - 2 * P
REG = W0 + W2
assert REG == 2 * W1 and REG <= 512
LAG = 2
NP_ = 4

LATE_PAIRS = {1: PAIRS - 2, 4: PAIRS - 1}
LOWER, UPPER = slice(0, 64), slice(64, 128)
NR = 4
SR = 8
SW = QW // SR
assert QW % SR == 0

AT_TRANSPOSES, AT_HIDDEN, AT_LOGITS, AT_SLOTS = 2, 4, 5, 7
SPLITS = [(e, half) for e in range(EXPERTS) for half in range(2)]
SPLIT_FROM = 4

EARLY_Q = 6
QKV = ["k0", "k1"] + [f"q{j}" for j in range(EARLY_Q)] + ["v0", "v1", "v2"]
LATE_QS = [f"q{j}" for j in range(EARLY_Q, PAIRS)]
WO = ["w0", "w1", "w2"]
XT = ["xt0", "xt1", "xt2"]
CV = ["cv0", "cv1", "cv2"]
X2T = ["x2t0", "x2t1"]
XNT = ["xnt0", "xnt1"]
RK = ["tri", "tot"]


def jobs_of(back, front, attention=True):
    out = list(QKV) if attention else []
    out += XT if front else []
    out += LATE_QS if attention else []
    out += CV if front else []
    out += WO if back else []
    out += X2T + ["g", "l"] if back else []
    out += XNT if front else []
    out += RK if back else []
    return out


PER_TURN = len(jobs_of(True, True))
assert PER_TURN % 3 == 0
PROLOGUE = XT + CV + XNT
FIRST_JOB = PER_TURN - len(PROLOGUE) - len(jobs_of(False, True))


class Turn:

    def __init__(self, b):
        self.b = b
        self.attention = not (isinstance(b, int) and b in (-1, BATCHES))
        self.back = not (isinstance(b, int) and b <= 0)
        self.front = not (isinstance(b, int) and b >= BATCHES - 1)
        if isinstance(b, int) and b == -1:
            names, self.base = PROLOGUE, FIRST_JOB
        elif isinstance(b, int) and b == 0:
            names, self.base = jobs_of(False, True), FIRST_JOB + len(PROLOGUE)
        elif isinstance(b, int) and b == BATCHES:
            names, self.base = jobs_of(True, False, False), PER_TURN * (BATCHES - 1) + len(jobs_of(True, False))
        else:
            names, self.base = jobs_of(True, self.front), b * PER_TURN
        start = 0 if not isinstance(self.base, int) else self.base % 3
        self.local = {name: k for k, name in enumerate(names)}
        self.bank_start = start

    def bank(self, name):
        if not self.attention and self.b == BATCHES and name not in WO:
            return 2
        return (self.bank_start + self.local[name]) % 3

    def before(self, name):
        return self.base + (self.local[name] - FIRST_JOB)

    def upto(self, name):
        return self.base + (self.local[name] - FIRST_JOB + 1)


def turns(engine_loop, body):
    body(Turn(0))
    body(Turn(1))
    with engine_loop(2, BATCHES - 1) as b:
        body(Turn(b))
    body(Turn(BATCHES - 1))


def front_done(b):
    behind = 0 if isinstance(b, int) and b <= 1 else len(RK)
    return Turn(b).base - (FIRST_JOB + behind)


def recip_uses(n, p):
    per_batch = PAIRS // NR
    if isinstance(n, int):
        return n // PAIRS * per_batch + p // NR + 1
    return (n - p) // NR + (p // NR + 1)


def sent(b):
    return b * (16 * TOPK * TT)


class Link:

    def __init__(self, sem, engine):
        self.sem, self.engine, self.n = sem, engine, 0

    def __call__(self, instruction):
        instruction.then_inc(self.sem, 1)
        self.n = self.n + 1
        self.engine.wait_ge(self.sem, self.n)


def build(nc, x, conv_w, conv_b, gamma, beta, wq, wk, wv, wo, wg1, bg1, wg2, w_in, w_out, xs, ys, rs_dram, out):
    ctx = ExitStack()
    with ctx:
        def sem(name):
            return ctx.enter_context(nc.semaphore(name))

        def sb(stack, name, shape, dt=F32):
            return stack.enter_context(nc.sbuf_tensor(name, shape, dt))

        keep = ctx
        h_all = sb(keep, "h_all", [P, BATCHES * TT * DM])
        payload = sb(keep, "payload", [P, TOPK, TT, ROW])
        x2t = sb(keep, "x2t", [P, 2, TT * P])
        gate_t = sb(keep, "gate_t", [GATE, TT * P])
        wg1_sb = sb(keep, "wg1_sb", [P, 2, GATE])
        bg1_sb = sb(keep, "bg1_sb", [GATE, 1])
        wg2_sb = sb(keep, "wg2_sb", [GATE, EXPERTS])
        ident = sb(keep, "ident", [P, P])
        before_m = sb(keep, "before_m", [P, P])
        ones_m = sb(keep, "ones_m", [P, P])
        stats3 = sb(keep, "stats3", [P, TT, 6])
        mv3 = sb(keep, "mv3", [P, TT, 2])
        ve3 = sb(keep, "ve3", [P, TT])
        rstd3 = sb(keep, "rstd3", [P, TT])
        minus_half = sb(keep, "minus_half", [P, TT])
        mx = sb(keep, "mx", [P, TT, 1])
        shifted = sb(keep, "shifted", [P, TT, EXPERTS])
        expd = sb(keep, "expd", [P, TT, EXPERTS])
        denom = sb(keep, "denom", [P, TT, 1])
        rdenom = sb(keep, "rdenom", [P, TT, 1])
        probs = sb(keep, "probs", [P, TT, EXPERTS])
        top8 = sb(keep, "top8", [P, TT, 8])
        idx8 = sb(keep, "idx8", [P, TT, 8], U32)
        idxf = sb(keep, "idxf", [P, TT, TOPK])
        iota8 = sb(keep, "iota8", [P, TT, EXPERTS])
        hot0 = sb(keep, "hot0", [P, TT, EXPERTS])
        hot1 = sb(keep, "hot1", [P, TT, EXPERTS])
        hots = sb(keep, "hots", [P, TT, EXPERTS])
        chosen = sb(keep, "chosen", [P, TT, EXPERTS])
        valid8 = sb(keep, "valid8", [P, TT, EXPERTS])
        beyond = sb(keep, "beyond", [P, TT, TOPK])
        carry = sb(keep, "carry", [P, TT + 1, EXPERTS])
        carry0 = sb(keep, "carry0", [P, EXPERTS])
        rank = sb(keep, "rank", [P, TT, EXPERTS])
        pick0 = sb(keep, "pick0", [P, TT, EXPERTS])
        pick1 = sb(keep, "pick1", [P, TT, EXPERTS])
        slotf = sb(keep, "slotf", [P, TT, TOPK])
        slotg = sb(keep, "slotg", [P, TT, TOPK])
        slot = sb(keep, "slot", [P, TT, TOPK], I32)
        place = sb(keep, "place", [P, TT, TOPK])
        padi = sb(keep, "padi", [1, EXPERTS], I32)
        cntf = sb(keep, "cntf", [P, EXPERTS])
        cnti = sb(keep, "cnti", [P, EXPERTS], I32)
        cnts = sb(keep, "cnts", [P, EXPERTS], I32)
        tilesf = sb(keep, "tilesf", [P, EXPERTS])
        starts = sb(keep, "starts", [P, EXPERTS])
        done = sb(keep, "done", [P, EXPERTS])
        onward = sb(keep, "onward", [P, EXPERTS])
        ends = sb(keep, "ends", [P, EXPERTS])
        lag_rows = sb(keep, "lag_rows", [P, EXPERTS])
        iota_j = sb(keep, "iota_j", [1, FT])
        tile_j = sb(keep, "tile_j", [1, FT])
        total1 = sb(keep, "total1", [1, 1])
        over = sb(keep, "over", [1, FT, EXPERTS])
        expf = sb(keep, "expf", [1, FT])
        rowf = sb(keep, "rowf", [1, FT])
        rowg = sb(keep, "rowg", [1, FT])
        past = sb(keep, "past", [1, FT])
        rowh = sb(keep, "rowh", [1, FT])
        table = sb(keep, "table", [1, 2, FT], I32)
        pad_rows = sb(keep, "pad_rows", [P, ROW])
        tick_dve = sb(keep, "tick_dve", [1, 1])
        tick_pool = sb(keep, "tick_pool", [1, 1])
        eps_c = sb(keep, "eps_c", [P, TT])

        early = ExitStack()
        qs = sb(early, "qs", [P, 2, PAIRS, QW], F32R)
        kh = sb(early, "kh", [P, KV, TT * P], F32R)
        kl = sb(early, "kl", [P, KV, TT * P], F32R)
        scores_bytes = 4 * (2 * PAIRS * QW + 2 * KV * TT * P)
        x_sb = sb(early, "x_sb", [P, TT, 2 * DM])
        xsum = sb(early, "xsum", [P, TT, DM])
        bias2 = sb(early, "bias2", [P, DM])
        gamma_b = sb(early, "gamma_b", [P, DM])
        beta_b = sb(early, "beta_b", [P, DM])
        xth = sb(early, "xth", [P, TT, 2 * DM], F32R)
        xtl = sb(early, "xtl", [P, TT, 2 * DM], F32R)
        y_sb = sb(early, "y_sb", [P, TT, DM])
        xn = y_sb
        xnh = sb(early, "xnh", [P, 2, TT * P], F32R)
        xnl = sb(early, "xnl", [P, 2, TT * P], F32R)
        cwh = sb(early, "cwh", [P, 4, DM], F32R)
        cwl = sb(early, "cwl", [P, 4, DM], F32R)
        wqh = sb(early, "wqh", [P, 2, HEADS * HD], F32R)
        wql = sb(early, "wql", [P, 2, HEADS * HD], F32R)
        wkvh = sb(early, "wkvh", [P, 2, 2, KV * HD], F32R)
        wkvl = sb(early, "wkvl", [P, 2, 2, KV * HD], F32R)
        stats = sb(early, "stats", [P, TT, 6])
        mv1 = sb(early, "mv1", [P, TT, 2])
        ve1 = sb(early, "ve1", [P, TT])
        rstd1 = sb(early, "rstd1", [P, TT])
        mv2 = sb(early, "mv2", [P, TT, 2])
        ve2 = sb(early, "ve2", [P, TT])
        rstd2 = sb(early, "rstd2", [P, TT])
        prob = sb(early, "prob", [P, NP_, 3 * REG])
        vo = sb(early, "vo", [P, TT, KV, P])
        causal = sb(early, "causal", [P, P])
        win_causal = sb(early, "win_causal", [P, 2 * W2])
        before_ring = (TT * 2 * DM + TT * DM + 3 * DM + 2 * TT * 2 * DM + TT * DM + 4 * TT * P + 8 * DM
                       + 4 * HEADS * HD + 8 * KV * HD + NP_ * 3 * REG + TT * KV * P + P + 2 * W2 + TT * 14)
        sb(early, "before_ring", [P, max(6 * EW - before_ring, 1)])
        ring = sb(early, "ring", [P, NR, 2, QW])
        sums = sb(early, "sums", [2 * SR, NR, SW])
        rsums = sb(early, "rsums", [2 * SR, NR, SW])
        recip = sb(early, "recip", [P, NR, QW])
        ot = sb(early, "ot", [P, PAIRS, QW])
        wo_sb = sb(early, "wo_sb", [P, PAIRS, DM])
        early.close()

        late = ExitStack()
        xt_rows = sb(late, "xt_rows", [P, UNROLL, ROW])
        fxh = sb(late, "fxh", [P, 2, 2 * P], F32R)
        fxl = sb(late, "fxl", [P, 2, 2 * P], F32R)
        act_h = sb(late, "act_h", [P, 2, HID])
        fhh = sb(late, "fhh", [P, 2, HID], F32R)
        fhl = sb(late, "fhl", [P, 2, HID], F32R)
        y_rows = sb(late, "y_rows", [P, UNROLL, DM])
        work_bytes = 4 * (UNROLL * ROW + 4 * 2 * P + 6 * HID + UNROLL * DM)
        assert work_bytes <= scores_bytes
        sb(late, "behind_work", [P, (scores_bytes - work_bytes) // 4])
        ew = sb(late, "ew", [P, EXPERTS * EW], F32R)
        late.close()
        final = ExitStack()
        sb(final, "before_sums", [P, scores_bytes // 4])
        fin_in = sb(final, "fin_in", [P, BATCHES, TT, 2 * DM])
        final.close()

        ps = ctx.enter_context(nc.psum_tensor("ps", [P, 8, 512], F32))
        S_BANK, O_BANK, G_BANK = 0, 3, 5

        weights_in = [sem(f"weights_in{i}") for i in range(3)]
        consts_in = sem("consts_in")
        x_in = sem("x_in")
        x_summed = sem("x_summed")
        consts = sem("consts")
        kv_clear = sem("kv_clear")
        split_hi = sem("split_hi")
        split_lo = sem("split_lo")
        filled = sem("filled")
        drained = sem("drained")
        hi_done = sem("hi_done")
        scores = sem("scores")
        capped = sem("capped")
        exped = sem("exped")
        masked = sem("masked")
        pv_done = sem("pv_done")
        raised = [sem(f"raised{i}") for i in range(2)]
        sums_in = [sem(f"sums_in{i}") for i in range(NR)]
        rsums_ready = sem("rsums_ready")
        rsums_out = [sem(f"rsums_out{i}") for i in range(NR)]
        recip_in = [sem(f"recip_in{i}") for i in range(NR)]
        normed = sem("normed")
        xsum_ready = sem("xsum_ready")
        var_ready = [sem(f"var_ready{i}") for i in range(3)]
        rstd_ready = [sem(f"rstd_ready{i}") for i in range(3)]
        z_ready = sem("z_ready")
        h1_ready = sem("h1_ready")
        xn_ready = sem("xn_ready")
        xn2_ready = sem("xn2_ready")
        copy_ready = sem("copy_ready")
        x2t_ready = sem("x2t_ready")
        gate_ready = sem("gate_ready")
        shift_ready = sem("shift_ready")
        expd_ready = sem("expd_ready")
        chosen_ready = sem("chosen_ready")
        slots_ready = sem("slots_ready")
        scattered = sem("scattered")
        dve_link = sem("dve_link")
        pool_link = sem("pool_link")
        pad_ready = sem("pad_ready")
        ticked = sem("ticked")
        pad_done = sem("pad_done")
        table_ready = sem("table_ready")
        raw_in = [[sem(f"raw_in{e}_{half}") for half in range(2)] for e in range(EXPERTS)]
        exp_hi = sem("exp_hi")
        exp_lo = sem("exp_lo")
        rows_in = [sem(f"rows_in{i}") for i in range(UNROLL)]
        fx_filled = sem("fx_filled")
        fx_hi = sem("fx_hi")
        fx_lo = sem("fx_lo")
        fh_filled = sem("fh_filled")
        gelued = sem("gelued")
        ft_filled = sem("ft_filled")
        ft_hi = sem("ft_hi")
        ft_lo = sem("ft_lo")
        fy_filled = sem("fy_filled")
        fy_done = sem("fy_done")
        y_out = [sem(f"y_out{i}") for i in range(UNROLL)]
        fin_loaded = [sem(f"fin_loaded{i}") for i in range(BATCHES)]
        fin_clear = sem("fin_clear")
        fin_ready = sem("fin_ready")
        fin_stored = sem("fin_stored")

        block = ctx.enter_context(nc.Block())

        def general(turn, name, width=512):
            at = 256 if not turn.attention and name == RK[1] else 0
            return ps[:, G_BANK + turn.bank(name), at:min(at + width, 512)]

        def h_tile(b, t):
            return h_all[:, bass.ds((b * TT + t) * DM, DM)]

        def h_batch(b):
            return h_all[:, bass.ds(b * (TT * DM), TT * DM)].rearrange("p (t d) -> p t d", t=TT)

        def weight(e, half, low):
            return ew[:, e * EW + (2 * half + low) * 2 * HID:e * EW + (2 * half + low + 1) * 2 * HID]

        def load_expert(engine, e, half):
            engine.dma_start(weight(e, half, 1).bitcast(F32).rearrange("p (c o) -> p c o", c=2 + 2 * half),
                             (w_in, w_out)[half][e, :, :].rearrange("(c p) o -> p c o", p=P)
                             ).then_inc(raw_in[e][half], 16)

        stage = prob[:, :, :].rearrange("p n c -> p (n c)")
        ST_CONV, ST_Q = 0, 4 * DM
        ST_KV = ST_Q + 2 * HEADS * HD

        @block.sync
        def _(sp):
            def load_x(b):
                sp.dma_start(x_sb[:, 0:TT - 1, :],
                             x[bass.ds(b, 1), 0:(TT - 1) * P, :].rearrange("a (t p) f -> p (a t) f", p=P)
                             ).then_inc(x_in, 16)
                sp.dma_start(x_sb[0:LAST, TT - 1, :],
                             x[bass.ds(b, 1), (TT - 1) * P:SEQ, :].rearrange("a p f -> p (a f)")).then_inc(x_in, 16)

            sp.wait_ge(consts, 1)
            load_x(0)
            sp.dma_start(stage[:, ST_CONV:ST_Q].rearrange("p (c o) -> p c o", c=4),
                         conv_w.rearrange("(c p) o -> p c o", p=P)).then_inc(weights_in[0], 16)
            sp.dma_start(stage[:, ST_Q:ST_KV].rearrange("p (c o) -> p c o", c=2),
                         wq.rearrange("(c p) o -> p c o", p=P)).then_inc(weights_in[1], 16)
            for i, w in enumerate((wk, wv)):
                at = ST_KV + i * 2 * KV * HD
                sp.dma_start(stage[:, at:at + 2 * KV * HD].rearrange("p (c o) -> p c o", c=2),
                             w.rearrange("(c p) o -> p c o", p=P)).then_inc(weights_in[1], 16)
            sp.dma_start(wo_sb[:, :, :], wo.rearrange("(c p) o -> p c o", p=P)).then_inc(weights_in[2], 16)
            sp.dma_start(wg1_sb[:, :, :], wg1.rearrange("(c p) o -> p c o", p=P)).then_inc(weights_in[2], 16)
            sp.dma_start(wg2_sb[:, :], wg2).then_inc(weights_in[2], 16)
            sp.dma_start(bg1_sb[:, :], bg1.rearrange("(g a) -> g a", a=1)).then_inc(weights_in[2], 16)

            def next_x(b):
                sp.wait_ge(drained, Turn(b - 2).upto(XT[-1]))
                sp.wait_ge(x_summed, b)
                load_x(b)

            next_x(1)
            sp.wait_ge(consts, 3)
            sp.dma_start(xs[NOWHERE:NOWHERE + P, :], pad_rows[:, :]).then_inc(pad_done, 16)

            def spread_sums(n, slot):
                sp.wait_ge(raised[0], n + 1)
                sp.dma_start(sums[0:SR, slot, :], ring[64:65, slot, 0, :]).then_inc(sums_in[slot], 16)
                sp.wait_ge(raised[1], n + 1)
                sp.dma_start(sums[SR:2 * SR, slot, :], ring[0:1, slot, 1, :]).then_inc(sums_in[slot], 16)

            def write_recip(n, p):
                sp.wait_ge(rsums_ready, n + 1)
                sp.dma_start(rs_dram[p % NR, :, :].rearrange("s (r c) -> (s r) c", r=SR),
                             rsums[:, p % NR, :]).then_inc(rsums_out[p % NR], 16)

            def spread_recip(n, p):
                slot = p % NR
                sp.wait_ge(rsums_out[slot], recip_uses(n, p) * 16)
                for half in range(2):
                    sp.dma_start(recip[64 * half:64 * half + 64, slot, :],
                                 rs_dram[slot, half, :].partition_broadcast(64)).then_inc(recip_in[slot], 16)

            def turn_loads(b, load):
                for p in range(PAIRS):
                    n = b * PAIRS + p
                    if p == 0 and not (isinstance(b, int) and b == 0):
                        write_recip(n - 1, PAIRS - 1)
                        spread_recip(n - 2, PAIRS - 2)
                        spread_recip(n - 1, PAIRS - 1)
                    spread_sums(n, p % NR)
                    if p > 0:
                        write_recip(n - 1, p - 1)
                    if p > 1:
                        spread_recip(n - 2, p - 2)
                    if p == 1 and load:
                        load()

            turn_loads(0, lambda: next_x(2))
            with sp.Fori(3, BATCHES) as loaded:
                turn_loads(loaded - 2, lambda: next_x(loaded))
            turn_loads(BATCHES - 2, None)
            turn_loads(BATCHES - 1, None)
            last_pair = BATCHES * PAIRS - 1
            write_recip(last_pair, PAIRS - 1)
            spread_recip(last_pair - 1, PAIRS - 2)
            spread_recip(last_pair, PAIRS - 1)
            sp.wait_ge(pv_done, 2 * BATCHES * PAIRS)
            for e, half in SPLITS[2 * DURING:-4]:
                load_expert(sp, e, half)

            def load_rows(j, u, reuse):
                row = sp.value_load(table[0:1, 1, bass.ds(j, 1)], min_val=0, max_val=NOWHERE)
                if reuse is not None:
                    sp.wait_ge(y_out[u], reuse)
                sp.dma_start(xt_rows[:, u, :], xs[bass.ds(row, P), :]).then_inc(rows_in[u], 16)

            def load_six(i):
                for u in range(UNROLL):
                    load_rows(i * UNROLL + u, u, i * 16)

            sp.wait_ge(table_ready, 1)
            sp.wait_ge(scattered, sent(LISTED))
            for u in range(UNROLL):
                load_rows(u, u, None)
            sp.wait_ge(normed, BATCHES * PAIRS)
            for half in range(2):
                load_expert(sp, 6, half)
            sp.wait_ge(filled, Turn(BATCHES).upto("w2"))
            for half in range(2):
                load_expert(sp, 7, half)
            with sp.Fori(1, FIRST // UNROLL) as i:
                load_six(i)

            sp.wait_ge(pad_ready, 1)
            for e in range(EXPERTS):
                row = sp.value_load(padi[0:1, e:e + 1], min_val=0, max_val=NOWHERE - P)
                sp.dma_start(xs[bass.ds(row, P), :], pad_rows[:, :]).then_inc(pad_done, 16)
            sp.wait_ge(table_ready, 2)
            sp.wait_ge(pad_done, 16 * (EXPERTS + 1))
            sp.wait_ge(scattered, sent(BATCHES))
            with sp.Fori(FIRST // UNROLL, FT // UNROLL) as i:
                load_six(i)

            sp.wait_ge(fin_clear, 1)
            for u in range(UNROLL):
                sp.wait_ge(y_out[u], 16 * (FT // UNROLL))
            for b in range(BATCHES):
                sp.dma_start(fin_in[:, b, 0:TT - 1, :],
                             ys[b * SEQ:b * SEQ + (TT - 1) * P, :].rearrange("(t p) f -> p t f", p=P)
                             ).then_inc(fin_loaded[b], 16)
                sp.dma_start(fin_in[0:LAST, b, TT - 1, :],
                             ys[b * SEQ + (TT - 1) * P:(b + 1) * SEQ, :]).then_inc(fin_loaded[b], 16)

        @block.gpsimd
        def _(pool):
            g = nc.gpsimd
            link = Link(pool_link, pool)

            def tick(before):
                pool.wait_ge(ticked, before + 1)
                g.tensor_tensor(tick_pool[:, :], eps_c[0:1, 0:1], eps_c[0:1, 0:1], ALU.add).then_inc(ticked, 1)

            g.memset(x_sb[:, TT - 1, :], 0.0).then_inc(consts, 1)
            g.memset(tick_pool[:, :], 0.0).then_inc(ticked, 1)
            g.memset(eps_c[:, :], EPS)
            g.memset(minus_half[:, :], -0.5)
            link(g.memset(ident[:, :], 0.0))
            g.affine_select(out=ident[:, :], in_=ident[:, :], compare_op=ALU.not_equal, fill=1.0, base=0,
                            pattern=[[-1, P]], channel_multiplier=1).then_inc(consts, 1)

            def other_constants():
                g.memset(ones_m[:, :], 1.0)
                g.memset(before_m[:, :], 1.0)
                g.memset(causal[:, :], 1.0)
                g.memset(win_causal[:, :], 1.0)
                g.memset(valid8[:, :, :], 1.0)
                g.memset(beyond[:, :, :], 0.0)
                g.memset(pad_rows[:, 0:DM], 0.0)
                g.memset(pad_rows[:, DM + 1:ROW], 0.0)
                g.memset(pad_rows[:, DM:DM + 1].bitcast(I32), OFF)
                g.memset(carry[:, 1:, :], 0.0)
                g.iota(iota8[:, :, :], [[0, TT], [1, EXPERTS]], base=0, channel_multiplier=0,
                       allow_small_or_imprecise_dtypes=True)
                g.iota(place[:, :, :], [[TOPK * P, TT], [1, TOPK]], base=0, channel_multiplier=TOPK,
                       allow_small_or_imprecise_dtypes=True)
                g.iota(carry[:, 0, :], [[CAP, EXPERTS]], base=0, channel_multiplier=0,
                       allow_small_or_imprecise_dtypes=True)
                g.iota(carry0[:, :], [[CAP, EXPERTS]], base=0, channel_multiplier=0,
                       allow_small_or_imprecise_dtypes=True)
                link(g.iota(iota_j[:, :], [[1, FT]], base=0, channel_multiplier=0,
                            allow_small_or_imprecise_dtypes=True))
                g.affine_select(out=before_m[:, :], in_=before_m[:, :], compare_op=ALU.is_ge, fill=0.0, base=-1,
                                pattern=[[1, P]], channel_multiplier=-1)
                g.affine_select(out=causal[:, :], in_=causal[:, :], compare_op=ALU.is_ge, fill=0.0, base=0,
                                pattern=[[1, P]], channel_multiplier=-1)
                g.affine_select(out=win_causal[:, W2:2 * W2], in_=win_causal[:, W2:2 * W2], compare_op=ALU.is_ge,
                                fill=0.0, base=0, pattern=[[1, W2]], channel_multiplier=-1)
                g.affine_select(out=win_causal[:, 0:W2], in_=win_causal[:, 0:W2], compare_op=ALU.is_ge, fill=0.0,
                                base=WINDOW - 1 - 2 * P, pattern=[[-1, W2]], channel_multiplier=1)
                g.affine_select(out=valid8[:, TT - 1, :], in_=valid8[:, TT - 1, :], compare_op=ALU.is_ge, fill=0.0,
                                base=LAST - 1, pattern=[[0, EXPERTS]], channel_multiplier=-1)
                g.affine_select(out=beyond[:, TT - 1, :], in_=beyond[:, TT - 1, :], compare_op=ALU.is_ge,
                                fill=float(OFF), base=LAST - 1, pattern=[[0, TOPK]], channel_multiplier=-1
                                ).then_inc(consts, 1)

            def rstd(which, mv, ve, r, count):
                pool.wait_ge(var_ready[which], count)
                link(g.tensor_tensor(ve[:, :], mv[:, :, 1], eps_c[:, :], ALU.add))
                g.tensor_tensor(r[:, :], ve[:, :], minus_half[:, :], ALU.pow).then_inc(rstd_ready[which], 1)

            def front_sum(b):
                pool.wait_ge(x_in, 32 * (b + 1))
                if not isinstance(b, int) or b > 0:
                    pool.wait_ge(z_ready, b)
                g.tensor_tensor(xsum[:, :, :], x_sb[:, :, 0:DM], x_sb[:, :, DM:2 * DM], ALU.add
                                ).then_inc(x_summed, 1)
                pool.wait_ge(x_summed, b + 1)
                g.tensor_tensor(xsum[:, :, :], xsum[:, :, :],
                                bias2[:, :].unsqueeze(1).to_broadcast([P, TT, DM]),
                                ALU.add).then_inc(xsum_ready, 1)

            def front_affine(b):
                pool.wait_ge(z_ready, b + 1)
                link(g.tensor_tensor(xsum[:, :, :], y_sb[:, :, :],
                                     gamma_b[:, :].unsqueeze(1).to_broadcast([P, TT, DM]), ALU.mult))
                g.tensor_tensor(h_batch(b), xsum[:, :, :],
                                beta_b[:, :].unsqueeze(1).to_broadcast([P, TT, DM]),
                                ALU.add).then_inc(h1_ready, 1)

            def front(b):
                rstd(0, mv1, ve1, rstd1, b + 1)
                front_affine(b)
                rstd(1, mv2, ve2, rstd2, b + 1)

            def dispatch(b, tiles=0):
                pool.wait_ge(slots_ready, b + 1)
                pool.wait_ge(copy_ready, b + 1)
                tick(b + tiles)
                for t in range(TT):
                    for k in range(TOPK):
                        g.indirect_dma_start(
                            out=xs, out_offset=bass.IndirectOffsetOnAxis(ap=slot[:, t, k:k + 1], axis=0),
                            in_=payload[:, k, t, :], in_offset=None,
                            bounds_check=EXPERTS * CAP - 1, oob_is_err=False).then_inc(scattered, 16)

            def divide(n, p):
                slot = p % NR
                pool.wait_ge(recip_in[slot], recip_uses(n, p) * 32)
                for half in range(2):
                    rows = slice(64 * half, 64 * half + 64)
                    last = g.tensor_tensor(ot[rows, p, :], ring[rows, slot, half, :], recip[rows, slot, :], ALU.mult)
                last.then_inc(normed, 1)

            pool.wait_ge(consts_in, 48)
            link(g.tensor_tensor(bias2[:, :], bias2[:, :], bias2[:, :], ALU.add))
            front_sum(0)
            other_constants()
            front(0)

            def late_divides(b, all_rows_end):
                all_rows_end()
                for p in (PAIRS - 2, PAIRS - 1):
                    divide(b * PAIRS + p, p)
                pool.wait_ge(normed, (b + 1) * PAIRS)

            def turn(tn):
                b = tn.b
                first = b * PAIRS
                if tn.front:
                    front_sum(b + 1)
                if tn.back:
                    late_divides(b - 1, lambda: pool.wait_ge(xsum_ready, b + 2) if tn.front else None)
                if not isinstance(b, int) or b > 1:
                    dispatch(b - 2)
                if tn.front:
                    rstd(0, mv1, ve1, rstd1, b + 2)
                    front_affine(b + 1)
                    rstd(1, mv2, ve2, rstd2, b + 2)
                if tn.back:
                    rstd(2, mv3, ve3, rstd3, b)
                    pool.wait_ge(rstd_ready[2], b)
                else:
                    pool.wait_ge(rstd_ready[1], b + 2)
                if not isinstance(b, int) or b > 1:
                    pool.wait_ge(scattered, sent(b - 1))
                for p in range(PAIRS - 2):
                    divide(first + p, p)
                pool.wait_ge(normed, first + (PAIRS - 2))

            loop_links = 4
            turn(Turn(0))
            turn(Turn(1))
            base = link.n
            with pool.Fori(2, BATCHES - 1) as b:
                link.n = (b - 2) * loop_links + base
                turn(Turn(b))
            link.n = base + loop_links * (BATCHES - 3)
            turn(Turn(BATCHES - 1))
            late_divides(BATCHES - 1, lambda: None)
            dispatch(BATCHES - 2)
            rstd(2, mv3, ve3, rstd3, BATCHES)

            def scatter(j_done, u):
                pool.wait_ge(fy_done, j_done)
                last_dispatched = not isinstance(j_done, int) or j_done > AT_SLOTS + 1
                tick(j_done + (BATCHES - 1 if last_dispatched else BATCHES - 2))
                g.indirect_dma_start(
                    out=ys.rearrange("t (k d) -> (t k) d", k=TOPK),
                    out_offset=bass.IndirectOffsetOnAxis(ap=xt_rows[:, u, DM:DM + 1].bitcast(I32), axis=0),
                    in_=y_rows[:, u, :], in_offset=None,
                    bounds_check=TOPK * TOK - 1, oob_is_err=False).then_inc(y_out[u], 16)

            for j in range(2 * UNROLL):
                if j == AT_SLOTS + 1:
                    dispatch(BATCHES - 1, AT_SLOTS + 1)
                scatter(j + 1, j % UNROLL)
            with pool.Fori(2, FT // UNROLL) as i:
                for u in range(UNROLL):
                    scatter(i * UNROLL + (u + 1), u)

        @block.scalar
        def _(act):
            s = nc.scalar
            F = ACT.Copy

            for src, dst in ((conv_b, bias2), (gamma, gamma_b), (beta, beta_b)):
                act.dma_start(dst[:, :], src.partition_broadcast(P)).then_inc(consts_in, 16)
            act.wait_ge(weights_in[0], 16)
            s.activation(cwh[:, :, :].rearrange("p c o -> p (c o)"), stage[:, ST_CONV:ST_Q], F
                         ).then_inc(split_hi, 1)

            def hi(tn, name, dst, width, src=None):
                act.wait_ge(filled, tn.upto(name))
                s.activation(dst, general(tn, name, width) if src is None else src, F).then_inc(hi_done, 1)

            def xt_hi(tn):
                for t in range(TT):
                    hi(tn, XT[t], xth[:, t, :], 512)

            def xnt_hi(tn):
                for c in range(2):
                    hi(tn, XNT[c], xnh[:, c, :], TT * P)

            xt_hi(Turn(-1))
            act.wait_ge(weights_in[1], 48)
            s.activation(wqh[:, :, :].rearrange("p c o -> p (c o)"), stage[:, ST_Q:ST_KV], F).then_inc(split_hi, 1)
            s.activation(wkvh[:, :, :, :].rearrange("p w c o -> p (w c o)"),
                         stage[:, ST_KV:ST_KV + 4 * KV * HD], F).then_inc(split_hi, 1)
            xnt_hi(Turn(-1))

            def raise_a(n, p):
                act.wait_ge(pv_done, 2 * n + 1)
                if not isinstance(n, int) or n >= NR:
                    act.wait_ge(normed, n - (NR - 1))
                s.activation(ring[:, p % NR, 0, :], ps[:, O_BANK, 0:QW], F).then_inc(raised[0], 1)

            def q_hi(tn, j):
                act.wait_ge(filled, tn.upto(f"q{j}"))
                src = general(tn, f"q{j}", QW)
                s.activation(qs[LOWER, 0, j, :], src[LOWER, :], F)
                s.activation(qs[UPPER, 1, j, :], src[UPPER, :], F).then_inc(hi_done, 1)

            def turn(tn):
                b = tn.b
                for c in range(2):
                    act.wait_ge(filled, tn.upto(f"k{c}"))
                    src = general(tn, f"k{c}", TT * P)
                    for own, other, g in ((LOWER, UPPER, 2 * c), (UPPER, LOWER, 2 * c + 1)):
                        s.activation(kh[other, g, :], src[own, :], F)
                        last = s.activation(kh[own, g, :], src[own, :], F)
                    last.then_inc(hi_done, 1)
                for j in range(EARLY_Q):
                    q_hi(tn, j)
                    if j in LATE_PAIRS and not (isinstance(b, int) and b == 0):
                        pair = LATE_PAIRS[j]
                        raise_a((b - 1) * PAIRS + pair, pair)
                for p in range(PAIRS):
                    n = b * PAIRS + p
                    if p == 0 and isinstance(b, int) and b == 0:
                        act.wait_ge(split_lo, 3)
                    if p == 1:
                        for j in range(EARLY_Q, PAIRS):
                            q_hi(tn, j)
                    act.wait_ge(scores, n + 1)
                    if not (isinstance(b, int) and b == 0 and p < NP_):
                        act.wait_ge(pv_done, 2 * n + (2 - 2 * NP_))
                    buf = prob[:, p % NP_, :]
                    s.activation(buf.rearrange("p (r c) -> p r c", r=3), ps[:, S_BANK:S_BANK + 3, 0:REG],
                                 ACT.Tanh, scale=SCALE / SOFTCAP).then_inc(capped, 1)
                    if p == 5 and tn.back:
                        gate(tn)
                    act.wait_ge(capped, n + 1)
                    s.activation(buf, buf, ACT.Exp, scale=SOFTCAP).then_inc(exped, 1)
                    if p >= LAG:
                        raise_a(n - LAG, p - LAG)
                    if p == 0 and tn.front:
                        xt_hi(tn)
                    if p == 4 and tn.back:
                        copy_rows(b - 1)
                    if p == 5 and tn.back:
                        router_exp(b - 1)
                    if p == 6 and tn.front:
                        xnt_hi(tn)
                    if isinstance(b, int) and b == BATCHES - 1 and LAG <= p < LAG + DURING:
                        if p == LAG:
                            act.wait_ge(filled, tn.upto(LATE_QS[-1]))
                            act.wait_ge(h1_ready, BATCHES)
                        for half in range(2):
                            load_expert(act, p - LAG, half)
                    if isinstance(b, int) and b == BATCHES - 1 and p >= SPLIT_FROM:
                        expert_hi(*SPLITS[p - SPLIT_FROM])

            def copy_rows(b):
                act.wait_ge(xn2_ready, b + 1)
                s.activation(payload[:, 1, :, 0:DM], payload[:, 0, :, 0:DM], F).then_inc(copy_ready, 1)

            def gate(tn):
                act.wait_ge(filled, tn.upto("g"))
                s.activation(gate_t[:, :], general(tn, "g", TT * P)[0:GATE, :], ACT.Gelu,
                             bias=bg1_sb[:, 0:1]).then_inc(gate_ready, 1)

            def router_exp(b):
                act.wait_ge(shift_ready, b + 1)
                s.activation(expd[:, :, :], shifted[:, :, :], ACT.Exp).then_inc(expd_ready, 1)

            def expert_hi(e, half):
                act.wait_ge(raw_in[e][half], 16)
                s.activation(weight(e, half, 0), weight(e, half, 1).bitcast(F32), F).then_inc(exp_hi, 1)

            turns(act.Fori, turn)

            last = Turn(BATCHES)
            for pair in (PAIRS - 2, PAIRS - 1):
                raise_a((BATCHES - 1) * PAIRS + pair, pair)
            for e, half in SPLITS[PAIRS - SPLIT_FROM:]:
                expert_hi(e, half)

            def beside(j):
                if j == AT_TRANSPOSES:
                    copy_rows(BATCHES - 1)
                if j == AT_HIDDEN:
                    gate(last)
                if j == AT_LOGITS + 1:
                    router_exp(BATCHES - 1)

            def fx_high(n, u):
                act.wait_ge(fx_filled, n + 1)
                s.activation(fxh[:, u % 2, :], ps[:, u % 2, 0:2 * P], F).then_inc(fx_hi, 1)

            def gelu(n, u):
                act.wait_ge(fh_filled, n + 1)
                s.activation(act_h[:, u % 2, :], ps[:, 2 + u % 2, :], ACT.Gelu).then_inc(gelued, 1)

            def ft_high(n, u):
                for half, cols in enumerate(HALVES):
                    act.wait_ge(ft_filled, n * 2 + (half + 1))
                    s.activation(fhh[:, u % 2, cols], ps[:, 4 + half, 0:HID // 2], F).then_inc(ft_hi, 1)

            def six(base, more):
                for u in range(UNROLL):
                    j = base + u
                    if isinstance(j, int):
                        beside(j)
                    ft_high(j, u)
                    if more or u + 1 < UNROLL:
                        gelu(j + 1, u + 1)
                    if more or u + 2 < UNROLL:
                        fx_high(j + 2, u + 2)

            fx_high(0, 0)
            fx_high(1, 1)
            gelu(0, 0)
            six(0, True)
            six(UNROLL, True)
            with act.Fori(2, FT // UNROLL - 1) as i:
                six(i * UNROLL, True)
            six(FT - UNROLL, False)

            for b in range(BATCHES):
                act.wait_ge(fin_ready, b + 1)
                act.dma_start(out[b, 0:(TT - 1) * P, :].rearrange("(t p) f -> p t f", p=P),
                              fin_in[:, b, 0:TT - 1, 0:DM]).then_inc(fin_stored, 16)
                act.dma_start(out[b, (TT - 1) * P:SEQ, :], fin_in[0:LAST, b, TT - 1, 0:DM]
                              ).then_inc(fin_stored, 16)
            act.wait_ge(fin_stored, 32 * BATCHES)

        @block.vector
        def _(dve):
            v = nc.vector
            link = Link(dve_link, dve)

            def tick():
                return v.memset(tick_dve[:, :], 0.0)

            def split_low(dst_lo, src, hi_ap, count):
                dve.wait_ge(split_hi, count)
                v.tensor_tensor(dst_lo, src, hi_ap.bitcast(F32), ALU.subtract).then_inc(split_lo, 1)

            split_low(cwl[:, :, :].rearrange("p c o -> p (c o)"), stage[:, ST_CONV:ST_Q],
                      cwh[:, :, :].rearrange("p c o -> p (c o)"), 1)

            def lo(tn, name, dst, hi_ap, width, nth):
                dve.wait_ge(hi_done, nth)
                v.tensor_tensor(dst, general(tn, name, width), hi_ap.bitcast(F32),
                                ALU.subtract).then_inc(drained, 1)

            def hi_count(b, k):
                return b * 15 + (5 + k)

            def xt_lo(tn, first):
                for t in range(TT):
                    lo(tn, XT[t], xtl[:, t, :], xth[:, t, :], 512, first + t + 1)

            def xnt_lo(tn, first):
                for c in range(2):
                    lo(tn, XNT[c], xnl[:, c, :], xnh[:, c, :], TT * P, first + c + 1)

            def moments(src, mv, which, st):
                tick()
                for t in range(TT):
                    last = v.bn_stats(st[:, t, :], src(t))
                link(last)
                tick()
                for t in range(TT):
                    last = v.bn_aggr(mv[:, t, :], st[:, t, :])
                last.then_inc(var_ready[which], 1)

            def conv_add(tn, b):
                dve.wait_ge(xsum_ready, b + 1)
                for t in range(TT):
                    dve.wait_ge(filled, tn.upto(CV[t]))
                    v.scalar_tensor_tensor(y_sb[:, t, :], xsum[:, t, :], 0.5, general(tn, CV[t], DM),
                                           ALU.mult, ALU.add).then_inc(drained, 1)
                dve.wait_ge(drained, tn.upto(CV[TT - 1]))
                moments(lambda t: y_sb[:, t, :], mv1, 0, stats)

            def norm(dst, src, mv, r, which, count, done):
                dve.wait_ge(rstd_ready[which], count)
                for t in range(TT):
                    last = v.tensor_scalar(dst(t), src(t), mv[:, t, 0:1], r[:, t:t + 1], ALU.subtract, ALU.mult)
                last.then_inc(done, 1)

            def front_norm(b):
                norm(lambda t: y_sb[:, t, :], lambda t: y_sb[:, t, :], mv1, rstd1, 0, b + 1, z_ready)

            def front_moments(b):
                dve.wait_ge(h1_ready, b + 1)
                moments(lambda t: h_tile(b, t), mv2, 1, stats)

            def front_xn(b):
                norm(lambda t: xn[:, t, :], lambda t: h_tile(b, t), mv2, rstd2, 1, b + 1, xn_ready)

            def residual(tn, b):
                for t in range(TT):
                    dve.wait_ge(filled, tn.upto(WO[t]))
                    v.tensor_tensor(h_tile(b, t), general(tn, WO[t], DM), h_tile(b, t), ALU.add
                                    ).then_inc(drained, 1)
                dve.wait_ge(drained, tn.upto(WO[TT - 1]))
                moments(lambda t: h_tile(b, t), mv3, 2, stats3)

            def back_xn(b):
                if not isinstance(b, int) or b > 0:
                    dve.wait_ge(scattered, sent(b))
                norm(lambda t: payload[:, 0, t, 0:DM], lambda t: h_tile(b, t), mv3, rstd3, 2, b + 1, xn2_ready)

            def x2t_copy(tn, parts=(0, 1)):
                for c in parts:
                    dve.wait_ge(filled, tn.upto(X2T[c]))
                    v.tensor_copy(x2t[:, c, :], general(tn, X2T[c], TT * P)).then_inc(drained, 1)

            def shift(tn, b):
                dve.wait_ge(filled, tn.upto("l"))
                src = general(tn, "l", TT * EXPERTS).rearrange("p (t e) -> p t e", t=TT)
                link(v.tensor_reduce(mx[:, :, :], src, AX.X, ALU.max))
                v.tensor_tensor(shifted[:, :, :], src, mx[:, :, :].to_broadcast([P, TT, EXPERTS]),
                                ALU.subtract).then_inc(shift_ready, 1)
                dve.wait_ge(shift_ready, b + 1)
                tick().then_inc(drained, 2)

            def choose(b):
                dve.wait_ge(expd_ready, b + 1)
                link(v.tensor_reduce(denom[:, :, :], expd[:, :, :], AX.X, ALU.add))
                link(v.reciprocal(rdenom[:, :, :], denom[:, :, :]))
                link(v.tensor_tensor(probs[:, :, :], expd[:, :, :],
                                     rdenom[:, :, :].to_broadcast([P, TT, EXPERTS]), ALU.mult))
                tick()
                for t in range(TT):
                    last = v.max(top8[:, t, :], probs[:, t, :])
                link(last)
                tick()
                for t in range(TT):
                    last = v.max_index(idx8[:, t, :], top8[:, t, :], probs[:, t, :])
                link(last)
                for k in range(TOPK):
                    v.tensor_copy(payload[:, k, :, DM:DM + 1].bitcast(I32), place[:, :, k:k + 1])
                    v.tensor_copy(payload[:, k, :, DM + 1:ROW], top8[:, :, k:k + 1])
                link(v.tensor_copy(idxf[:, :, :], idx8[:, :, 0:TOPK]))
                v.tensor_tensor(hot0[:, :, :], iota8[:, :, :], idxf[:, :, 0:1].to_broadcast([P, TT, EXPERTS]),
                                ALU.is_equal)
                link(v.tensor_tensor(hot1[:, :, :], iota8[:, :, :],
                                     idxf[:, :, 1:2].to_broadcast([P, TT, EXPERTS]), ALU.is_equal))
                v.tensor_scalar(place[:, :, :], place[:, :, :], float(TOPK * SEQ), None, ALU.add)
                link(v.tensor_tensor(hots[:, :, :], hot0[:, :, :], hot1[:, :, :], ALU.add))
                v.tensor_tensor(chosen[:, :, :], hots[:, :, :], valid8[:, :, :], ALU.mult
                                ).then_inc(chosen_ready, 1)

            def slots(tn, b):
                dve.wait_ge(filled, tn.upto("tot"))
                tot = general(tn, "tot", TT * EXPERTS).rearrange("p (t e) -> p t e", t=TT)
                tri = general(tn, "tri", TT * EXPERTS).rearrange("p (t e) -> p t e", t=TT)
                for t in range(TT):
                    link(v.tensor_tensor(carry[:, t + 1, :], carry[:, t, :], tot[:, t, :], ALU.add))
                link(v.tensor_tensor(rank[:, :, :], carry[:, 0:TT, :], tri, ALU.add))
                tick().then_inc(drained, 2)
                v.tensor_tensor(pick0[:, :, :], hot0[:, :, :], rank[:, :, :], ALU.mult)
                v.tensor_copy(carry[:, 0, :], carry[:, TT, :])
                link(v.tensor_tensor(pick1[:, :, :], hot1[:, :, :], rank[:, :, :], ALU.mult))
                v.tensor_reduce(slotf[:, :, 0:1], pick0[:, :, :], AX.X, ALU.add)
                link(v.tensor_reduce(slotf[:, :, 1:2], pick1[:, :, :], AX.X, ALU.add))
                link(v.tensor_tensor(slotg[:, :, :], slotf[:, :, :], beyond[:, :, :], ALU.add))
                v.tensor_copy(slot[:, :, :], slotg[:, :, :]).then_inc(slots_ready, 1)

            def raise_b(n, p):
                dve.wait_ge(pv_done, 2 * n + 2)
                if not isinstance(n, int) or n >= NR:
                    dve.wait_ge(normed, n - (NR - 1))
                v.tensor_copy(ring[:, p % NR, 1, :], ps[:, O_BANK + 1, 0:QW]).then_inc(raised[1], 1)

            def invert(n, p):
                slot_ = p % NR
                dve.wait_ge(sums_in[slot_], recip_uses(n, p) * 32)
                v.reciprocal(rsums[:, slot_, :], sums[:, slot_, :]).then_inc(rsums_ready, 1)

            def mask(n, p):
                dve.wait_ge(exped, n + 1)
                r = prob[:, p % NP_, :]
                a = r[:, 0:2 * REG].rearrange("p (r c) -> p r c", r=2)
                v.tensor_tensor(a[:, :, 0:P], a[:, :, 0:P], causal[:, :].unsqueeze(1).to_broadcast([P, 2, P]),
                                ALU.mult)
                v.tensor_tensor(a[:, :, 2 * P:REG], a[:, :, 2 * P:REG],
                                win_causal[:, :].unsqueeze(1).to_broadcast([P, 2, 2 * W2]), ALU.mult)
                c = r[:, 2 * REG:3 * REG].rearrange("p (r c) -> p r c", r=2)
                v.tensor_tensor(c[:, :, 0:P], c[:, :, 0:P], causal[:, :].unsqueeze(1).to_broadcast([P, 2, P]),
                                ALU.mult).then_inc(masked, 1)

            first = Turn(-1)
            xt_lo(first, 0)
            dve.wait_ge(weights_in[1], 48)
            split_low(wql[:, :, :].rearrange("p c o -> p (c o)"), stage[:, ST_Q:ST_KV],
                      wqh[:, :, :].rearrange("p c o -> p (c o)"), 2)
            split_low(wkvl[:, :, :, :].rearrange("p w c o -> p (w c o)"), stage[:, ST_KV:ST_KV + 4 * KV * HD],
                      wkvh[:, :, :, :].rearrange("p w c o -> p (w c o)"), 3)
            conv_add(first, 0)
            front_norm(0)
            v.memset(kl[:, :, :].bitcast(F32), 0.0)
            v.memset(vo[:, :, :, :], 1.0).then_inc(kv_clear, 1)
            front_moments(0)
            front_xn(0)
            xnt_lo(first, 3)
            dve.wait_ge(consts, 3)
            dve.wait_ge(kv_clear, 1)

            def q_low(tn, j, nth):
                dve.wait_ge(hi_done, hi_count(tn.b, nth))
                src = general(tn, f"q{j}", QW)
                for own, other, head in ((LOWER, UPPER, 0), (UPPER, LOWER, 1)):
                    last = v.tensor_tensor(qs[other, head, j, :], src[own, :],
                                           qs[own, head, j, :].bitcast(F32), ALU.subtract)
                last.then_inc(drained, 1)

            def qk_low(tn):
                b = tn.b
                for c in range(2):
                    dve.wait_ge(hi_done, hi_count(b, c + 1))
                    src = general(tn, f"k{c}", TT * P)
                    for own, g in ((LOWER, 2 * c), (UPPER, 2 * c + 1)):
                        last = v.tensor_tensor(kl[own, g, :], src[own, :], kh[own, g, :].bitcast(F32), ALU.subtract)
                    last.then_inc(drained, 1)
                for j in range(EARLY_Q):
                    q_low(tn, j, j + 3)
                    if not (isinstance(b, int) and b == 0):
                        before = (b - 1) * PAIRS
                        if j in LATE_PAIRS:
                            pair = LATE_PAIRS[j]
                            raise_b(before + pair, pair)
                        if j == 2:
                            invert(before + PAIRS - 3, PAIRS - 3)
                        if j == 5:
                            invert(before + PAIRS - 2, PAIRS - 2)

            def v_copies(tn):
                for t in range(TT):
                    dve.wait_ge(filled, tn.upto(f"v{t}"))
                    src = general(tn, f"v{t}", DM).rearrange("p (g s d) -> p g s d", g=2, s=2)
                    dst = vo[:, t, :, :].rearrange("p (g s) c -> p g s c", s=2)
                    v.tensor_copy(dst[:, :, 0, 0:HD], src[:, :, 0, :])
                    v.tensor_copy(dst[:, :, 1, HD:P], src[:, :, 1, :]).then_inc(drained, 1)

            def turn(tn):
                b = tn.b
                qk_low(tn)
                for p in range(PAIRS):
                    n = b * PAIRS + p
                    if p == 0:
                        v_copies(tn)
                    if p == 7 and tn.back:
                        slots(tn, b - 1)
                    if p == 5 and tn.front:
                        front_xn(b + 1)
                    mask(n, p)
                    if p >= LAG:
                        raise_b(n - LAG, p - LAG)
                    if p == 0:
                        if not (isinstance(b, int) and b == 0):
                            invert(n - 1, PAIRS - 1)
                        if tn.front:
                            xt_lo(tn, hi_count(b, EARLY_Q + 2))
                        for j in range(EARLY_Q, PAIRS):
                            q_low(tn, j, j + 3 + (TT if tn.front else 0))
                    if p == 1 and tn.front:
                        conv_add(tn, b + 1)
                        front_norm(b + 1)
                    if p == 2:
                        if tn.front:
                            front_moments(b + 1)
                        if isinstance(b, int) and b == BATCHES - 1:
                            first_table()
                        if tn.back:
                            residual(tn, b - 1)
                    if p == 3 and tn.back:
                        back_xn(b - 1)
                    if p == 4 and tn.back:
                        x2t_copy(tn)
                    if p == 5 and tn.back:
                        shift(tn, b - 1)
                        choose(b - 1)
                    if p == 6 and tn.front:
                        xnt_lo(tn, hi_count(b, PAIRS + 5))
                    if p > LAG:
                        invert(n - LAG - 1, p - LAG - 1)
                    if isinstance(b, int) and b == BATCHES - 1 and p >= SPLIT_FROM:
                        expert_lo(*SPLITS[p - SPLIT_FROM])

            def expert_lo(e, half):
                dve.wait_ge(exp_hi, 2 * e + half + 1)
                v.tensor_tensor(weight(e, half, 1), weight(e, half, 1).bitcast(F32),
                                weight(e, half, 0).bitcast(F32), ALU.subtract).then_inc(exp_lo, 1)

            def prefix(tiles):
                link(v.tensor_copy(ends[:, 0:1], tiles[:, 0:1]))
                for e in range(1, EXPERTS):
                    link(v.tensor_tensor(ends[:, e:e + 1], ends[:, e - 1:e], tiles[:, e:e + 1], ALU.add))

            def whole_tiles(extra):
                link(v.tensor_tensor(cntf[:, :], carry[:, 0, :], carry0[:, :], ALU.subtract))
                link(v.tensor_scalar(cntf[:, :], cntf[:, :], float(extra), None, ALU.add))
                link(v.tensor_copy(cnti[:, :], cntf[:, :]))
                link(v.tensor_scalar(cnts[:, :], cnti[:, :], 7, None, ALU.logical_shift_right))
                link(v.tensor_copy(tilesf[:, :], cnts[:, :]))
                link(v.tensor_scalar(lag_rows[:, :], tilesf[:, :], float(-P), float(CAP), ALU.mult, ALU.add))

            def rows_of_tiles(n):
                link(v.tensor_tensor(over[:, 0:n, :], ends[0:1, :].unsqueeze(1).to_broadcast([1, n, EXPERTS]),
                                     tile_j[:, 0:n].unsqueeze(2).to_broadcast([1, n, EXPERTS]), ALU.is_le))
                link(v.tensor_reduce(expf[:, 0:n], over[:, 0:n, :], AX.X, ALU.add))
                link(v.tensor_tensor(over[:, 0:n, :], over[:, 0:n, :],
                                     lag_rows[0:1, :].unsqueeze(1).to_broadcast([1, n, EXPERTS]), ALU.mult))
                link(v.tensor_reduce(rowf[:, 0:n], over[:, 0:n, :], AX.X, ALU.add))
                link(v.scalar_tensor_tensor(rowg[:, 0:n], tile_j[:, 0:n], float(P), rowf[:, 0:n],
                                            ALU.mult, ALU.add))

            def first_table():
                whole_tiles(0)
                prefix(tilesf)
                link(v.tensor_copy(tile_j[:, :], iota_j[:, :]))
                rows_of_tiles(FIRST)
                v.tensor_copy(table[:, 0, 0:FIRST], expf[:, 0:FIRST])
                link(v.tensor_tensor(starts[:, :], ends[:, :], tilesf[:, :], ALU.subtract))
                v.tensor_scalar(starts[:, :], starts[:, :], float(FIRST), None, ALU.min)
                link(v.tensor_scalar(ends[:, :], ends[:, :], float(FIRST), None, ALU.min))
                link(v.tensor_tensor(done[:, :], ends[:, :], starts[:, :], ALU.subtract))
                v.memset(onward[:, :], 0.0)
                link(v.tensor_copy(table[:, 1, 0:FIRST], rowg[:, 0:FIRST]))
                v.tensor_tensor(onward[:, 0:EXPERTS - 1], done[:, 1:EXPERTS], done[:, 0:EXPERTS - 1], ALU.subtract
                                ).then_inc(table_ready, 1)
                dve.wait_ge(table_ready, 1)

            def pad_places():
                v.tensor_copy(padi[:, :], carry[0:1, 0, :]).then_inc(pad_ready, 1)
                whole_tiles(P - 1)

            def tiles_left():
                link(v.tensor_tensor(tilesf[:, :], tilesf[:, :], done[:, :], ALU.subtract))
                v.scalar_tensor_tensor(lag_rows[:, :], done[:, :], float(P), lag_rows[:, :], ALU.mult, ALU.add)
                prefix(tilesf)
                link(v.scalar_tensor_tensor(lag_rows[:, :], onward[:, :], float(P), lag_rows[:, :],
                                            ALU.mult, ALU.add))
                link(v.tensor_scalar(total1[:, :], ends[0:1, EXPERTS - 1:EXPERTS], -1.0, None, ALU.add))

            def second_table():
                v.tensor_scalar(past[:, 0:REST], iota_j[:, 0:REST], total1[:, 0:1], None, ALU.is_gt)
                link(v.tensor_scalar(tile_j[:, 0:REST], iota_j[:, 0:REST], total1[:, 0:1], None, ALU.min))
                rows_of_tiles(REST)
                v.tensor_copy(table[:, 0, FIRST:FT], expf[:, 0:REST])

            def second_rows():
                link(v.tensor_scalar(rowf[:, 0:1], done[0:1, 0:1], float(P), None, ALU.mult))
                link(v.tensor_scalar(rowg[:, 0:REST], rowg[:, 0:REST], rowf[:, 0:1], None, ALU.add))
                link(v.scalar_tensor_tensor(rowh[:, 0:REST], past[:, 0:REST], float(NOWHERE), rowg[:, 0:REST],
                                            ALU.mult, ALU.add))
                link(v.tensor_scalar(rowh[:, 0:REST], rowh[:, 0:REST], float(NOWHERE), None, ALU.min))
                v.tensor_copy(table[:, 1, FIRST:FT], rowh[:, 0:REST]).then_inc(table_ready, 1)

            turn(Turn(0))
            before = link.n
            turn(Turn(1))
            start = link.n
            assert start - before == LINKS, (start, before, LINKS)
            with dve.Fori(2, BATCHES - 1) as b:
                link.n = (b - 2) * LINKS + start
                turn(Turn(b))
            link.n = start + LINKS * (BATCHES - 3)
            turn(Turn(BATCHES - 1))

            last_turn = Turn(BATCHES)
            last_pair = BATCHES * PAIRS - 1
            raise_b(last_pair - 1, PAIRS - 2)
            invert(last_pair - 2, PAIRS - 3)
            raise_b(last_pair, PAIRS - 1)
            for back in (1, 0):
                invert(last_pair - back, PAIRS - 1 - back)
            for e, half in SPLITS[PAIRS - SPLIT_FROM:-4]:
                expert_lo(e, half)
            residual(last_turn, BATCHES - 1)
            for e, half in SPLITS[-4:]:
                expert_lo(e, half)

            def beside(j):
                if j in (AT_TRANSPOSES + 1, AT_TRANSPOSES + 2):
                    x2t_copy(last_turn, (j - AT_TRANSPOSES - 1,))
                if j == AT_LOGITS:
                    shift(last_turn, BATCHES - 1)
                if j == AT_LOGITS + 1:
                    choose(BATCHES - 1)
                if j == AT_SLOTS:
                    slots(last_turn, BATCHES - 1)

            def beside_late(j):
                for step, part in enumerate((pad_places, tiles_left, second_table, second_rows)):
                    if j == AT_SLOTS + step:
                        part()

            def fx_low(n, u):
                dve.wait_ge(fx_hi, n + 1)
                v.tensor_tensor(fxl[:, u % 2, :], ps[:, u % 2, 0:2 * P], fxh[:, u % 2, :].bitcast(F32),
                                ALU.subtract).then_inc(fx_lo, 1)

            def ft_low(n, u):
                for half, cols in enumerate(HALVES):
                    dve.wait_ge(ft_hi, n * 2 + (half + 1))
                    v.tensor_tensor(fhl[:, u % 2, cols], ps[:, 4 + half, 0:HID // 2], fhh[:, u % 2, cols].bitcast(F32),
                                    ALU.subtract).then_inc(ft_lo, 1)

            def gated(n, u, reuse):
                if reuse is not None:
                    dve.wait_ge(y_out[u], reuse)
                dve.wait_ge(fy_filled, n + 1)
                v.tensor_scalar(y_rows[:, u, :], ps[:, 6, 0:DM], xt_rows[:, u % UNROLL, DM + 1:ROW],
                                None, ALU.mult).then_inc(fy_done, 1)

            def six(i, base, head, more):
                for u in range(UNROLL):
                    j = base + u
                    if isinstance(j, int):
                        beside(j)
                    ft_low(j, u)
                    if more or u + 2 < UNROLL:
                        fx_low(j + 2, u + 2)
                    if isinstance(j, int):
                        beside_late(j)
                    gated(j, u, None if head else i * 16)

            fx_low(0, 0)
            fx_low(1, 1)
            back_xn(BATCHES - 1)
            six(0, 0, True, True)
            six(1, UNROLL, False, True)
            with dve.Fori(2, FT // UNROLL - 1) as i:
                six(i, i * UNROLL, False, True)
            six(FT // UNROLL - 1, FT - UNROLL, False, False)

            v.memset(fin_in[:, :, TT - 1, :], 0.0).then_inc(fin_clear, 1)
            dve.wait_ge(fin_clear, 1)
            for b in range(BATCHES):
                dve.wait_ge(fin_loaded[b], 32)
                o = fin_in[:, b, :, 0:DM]
                link(v.tensor_tensor(o, o, fin_in[:, b, :, DM:2 * DM], ALU.add))
                v.tensor_tensor(o, o, h_batch(b), ALU.add).then_inc(fin_ready, 1)

        @block.tensor
        def _(pe):
            t_ = nc.tensor

            def claim(tn, name):
                n = tn.before(name)
                if isinstance(n, int) and not tn.attention and tn.b == BATCHES and name not in WO:
                    if name not in ("l", "tot"):
                        pe.wait_ge(drained, n)
                    return
                if not isinstance(n, int):
                    pe.wait_ge(drained, n - 2)
                elif n >= 3:
                    pe.wait_ge(drained, n - 2)

            def three(out_ap, terms):
                steps = [(a, c) for ah, al, ch, cl in terms for a, c in ((ah, ch), (ah, cl), (al, ch))]
                for i, (a, c) in enumerate(steps):
                    last = t_.matmul(out_ap, a, c, start=(i == 0), stop=(i == len(steps) - 1))
                return last

            def transposes(tn):
                for t in range(TT):
                    claim(tn, XT[t])
                    dst = general(tn, XT[t])
                    for c in range(4):
                        last = t_.transpose(dst[:, c * P:(c + 1) * P], x_sb[:, t, c * P:(c + 1) * P], ident[:, :])
                    last.then_inc(filled, 1)

            def conv(tn):
                for t in range(TT):
                    claim(tn, CV[t])
                    if t == 0:
                        pe.wait_ge(drained, tn.upto(XT[TT - 1]))
                    three(general(tn, CV[t], DM),
                          [(xth[:, t, c * P:(c + 1) * P], xtl[:, t, c * P:(c + 1) * P], cwh[:, c, :], cwl[:, c, :])
                           for c in range(4)]).then_inc(filled, 1)

            def xn_transposes(tn, b):
                pe.wait_ge(xn_ready, b + 1)
                for c in range(2):
                    claim(tn, XNT[c])
                    dst = general(tn, XNT[c], TT * P)
                    for t in range(TT):
                        last = t_.transpose(dst[:, t * P:(t + 1) * P], xn[:, t, c * P:(c + 1) * P], ident[:, :])
                    last.then_inc(filled, 1)

            def project_query(tn, j):
                claim(tn, f"q{j}")
                three(general(tn, f"q{j}", QW),
                      [(wqh[:, c, j * P:(j + 1) * P], wql[:, c, j * P:(j + 1) * P],
                        xnh[:, c, 0:QW], xnl[:, c, 0:QW]) for c in range(2)]).then_inc(filled, 1)

            def project(tn):
                b = tn.b
                pe.wait_ge(drained, front_done(b))
                for j in range(2):
                    claim(tn, f"k{j}")
                    three(general(tn, f"k{j}", TT * P),
                          [(wkvh[:, 0, c, j * P:(j + 1) * P], wkvl[:, 0, c, j * P:(j + 1) * P],
                            xnh[:, c, :], xnl[:, c, :]) for c in range(2)]).then_inc(filled, 1)
                for j in range(EARLY_Q):
                    project_query(tn, j)
                    if j in LATE_PAIRS and not (isinstance(b, int) and b == 0):
                        pair = LATE_PAIRS[j]
                        values((b - 1) * PAIRS + pair, pair)

            def project_values(tn):
                for t in range(TT):
                    claim(tn, f"v{t}")
                    cols = slice(t * P, (t + 1) * P)
                    three(general(tn, f"v{t}", DM),
                          [(xnh[:, c, cols], xnl[:, c, cols], wkvh[:, 1, c, :], wkvl[:, 1, c, :])
                           for c in range(2)]).then_inc(filled, 1)

            def score(n, j):
                if not isinstance(n, int) or n >= 1:
                    pe.wait_ge(capped, n)
                for half in range(2):
                    g = 2 * (j // 4) + half
                    region = ps[:, S_BANK + half, :]
                    for kt, dst in ((0, region[:, 0:W0]), (2, region[:, W0:REG]),
                                    (1, ps[:, S_BANK + 2, half * W1:(half + 1) * W1])):
                        cols = slice(kt * P, (kt + 1) * P)
                        t_.matmul(dst, kh[:, g, cols], qs[:, half, j, kt * P:QW], start=True, stop=False)
                        last = t_.matmul(dst, kl[:, g, cols], qs[:, half, j, kt * P:QW], start=False, stop=True)
                last.then_inc(scores, 1)

            def values(n, p):
                pe.wait_ge(masked, n + 1)
                buf = prob[:, p % NP_, :]
                for half in range(2):
                    g = 2 * (p // 4) + half
                    if not isinstance(n, int) or n >= 1:
                        pe.wait_ge(raised[half], n)
                    dst = ps[:, O_BANK + half, :]
                    r = buf[:, half * REG:(half + 1) * REG]
                    mid = buf[:, 2 * REG + half * W1:2 * REG + (half + 1) * W1]
                    t_.matmul(dst[:, 0:QW], vo[:, 0, g, :], r[:, 0:W0], start=True, stop=False)
                    t_.matmul(dst[:, P:QW], vo[:, 1, g, :], mid, start=False, stop=False)
                    t_.matmul(dst[:, 2 * P:QW], vo[0:LAST, 2, g, :], r[0:LAST, W0:REG],
                              start=False, stop=True).then_inc(pv_done, 1)

            def output(tn, b):
                pe.wait_ge(normed, (b + 1) * PAIRS)
                for t in range(TT):
                    claim(tn, WO[t])
                    rows = P if t < TT - 1 else QW - t * P
                    for c in range(PAIRS):
                        last = t_.matmul(general(tn, WO[t], DM)[0:rows, :], ot[:, c, t * P:t * P + rows],
                                         wo_sb[:, c, :], start=(c == 0), stop=(c == PAIRS - 1))
                    last.then_inc(filled, 1)

            def last_output(tn):
                for pairs in ((0, 1, 2, 3), (4, 5), (6, 7)):
                    pe.wait_ge(normed, (BATCHES - 1) * PAIRS + (pairs[-1] + 1))
                    for t in range(TT):
                        if pairs[0] == 0:
                            claim(tn, WO[t])
                        rows = P if t < TT - 1 else QW - t * P
                        for c in pairs:
                            last = t_.matmul(general(tn, WO[t], DM)[0:rows, :], ot[:, c, t * P:t * P + rows],
                                             wo_sb[:, c, :], start=(c == 0), stop=(c == PAIRS - 1))
                        if pairs[-1] == PAIRS - 1:
                            last.then_inc(filled, 1)

            def x2_transposes(tn, b, parts=(0, 1)):
                pe.wait_ge(xn2_ready, b + 1)
                for c in parts:
                    claim(tn, X2T[c])
                    dst = general(tn, X2T[c], TT * P)
                    for t in range(TT):
                        last = t_.transpose(dst[:, t * P:(t + 1) * P], payload[:, 0, t, c * P:(c + 1) * P],
                                            ident[:, :])
                    last.then_inc(filled, 1)

            def router_hidden(tn, b):
                claim(tn, "g")
                pe.wait_ge(drained, tn.upto(X2T[1]))
                for c in range(2):
                    last = t_.matmul(general(tn, "g", TT * P)[0:GATE, :], wg1_sb[:, c, :], x2t[:, c, :],
                                     start=(c == 0), stop=(c == 1))
                last.then_inc(filled, 1)

            def router_logits(tn, b):
                claim(tn, "l")
                pe.wait_ge(gate_ready, b + 1)
                for t in range(TT):
                    last = t_.matmul(general(tn, "l")[:, t * EXPERTS:(t + 1) * EXPERTS],
                                     gate_t[:, t * P:(t + 1) * P], wg2_sb[:, :], start=True, stop=True)
                last.then_inc(filled, 1)

            def counts(tn, b):
                pe.wait_ge(chosen_ready, b + 1)
                for name, m in (("tri", before_m), ("tot", ones_m)):
                    claim(tn, name)
                    t_.matmul(general(tn, name, TT * EXPERTS), m[:, :],
                              chosen[:, :, :].rearrange("p t e -> p (t e)"), start=True, stop=True
                              ).then_inc(filled, 1)

            first = Turn(-1)
            pe.wait_ge(consts, 2)
            pe.wait_ge(x_in, 32)
            transposes(first)
            pe.wait_ge(split_lo, 1)
            conv(first)
            xn_transposes(first, 0)
            pe.wait_ge(split_lo, 3)
            pe.wait_ge(consts, 3)

            def turn(tn):
                b = tn.b
                project(tn)
                for p in range(PAIRS):
                    n = b * PAIRS + p
                    pe.wait_ge(drained, tn.upto(f"q{p}"))
                    score(n, p)
                    if p == 0:
                        project_values(tn)
                        if tn.front:
                            pe.wait_ge(x_in, 32 * (b + 2))
                            transposes(tn)
                    if p == 5 and tn.back:
                        router_hidden(tn, b - 1)
                    if p == LAG:
                        pe.wait_ge(drained, tn.upto("v2"))
                    if p >= LAG:
                        values(n - LAG, p - LAG)
                    if p == 1:
                        for j in range(EARLY_Q, PAIRS):
                            project_query(tn, j)
                        if tn.front:
                            conv(tn)
                    if p == 2 and tn.back:
                        pe.wait_ge(weights_in[2], 64)
                        output(tn, b - 1)
                    if p == 4 and tn.back:
                        x2_transposes(tn, b - 1)
                    if p == 5 and tn.back:
                        router_logits(tn, b - 1)
                    if p == 6 and tn.front:
                        xn_transposes(tn, b + 1)
                    if p == 7 and tn.back:
                        counts(tn, b - 1)

            turns(pe.Fori, turn)
            last_turn = Turn(BATCHES)
            for pair in (PAIRS - 2, PAIRS - 1):
                values((BATCHES - 1) * PAIRS + pair, pair)
            last_output(last_turn)

            def row_transposes(n, u, i):
                pe.wait_ge(rows_in[u % UNROLL], (i + 1) * 16)
                if not isinstance(n, int) or n >= 2:
                    pe.wait_ge(fx_lo, n - 1)
                for c in range(2):
                    last = t_.transpose(ps[:, u % 2, c * P:(c + 1) * P],
                                        xt_rows[:, u % UNROLL, c * P:(c + 1) * P], ident[:, :])
                last.then_inc(fx_filled, 1)

            def up(n, u, e):
                pe.wait_ge(fx_lo, n + 1)
                if not isinstance(n, int) or n >= 2:
                    pe.wait_ge(gelued, n - 1)
                three(ps[:, 2 + u % 2, :],
                      [(fxh[:, u % 2, c * P:(c + 1) * P], fxl[:, u % 2, c * P:(c + 1) * P],
                        ew[:, bass.ds(e * EW + c * HID, HID)], ew[:, bass.ds(e * EW + (2 + c) * HID, HID)])
                       for c in range(2)]).then_inc(fh_filled, 1)

            def h_transposes(n, u):
                pe.wait_ge(gelued, n + 1)
                for half in range(2):
                    if not isinstance(n, int) or n >= 1:
                        pe.wait_ge(ft_lo, n * 2 + (half - 1))
                    for c in (2 * half, 2 * half + 1):
                        last = t_.transpose(ps[:, 4 + half, c % 2 * P:(c % 2 + 1) * P],
                                            act_h[:, u % 2, c * P:(c + 1) * P], ident[:, :])
                    last.then_inc(ft_filled, 1)

            def down(n, u, e):
                if not isinstance(n, int) or n >= 1:
                    pe.wait_ge(fy_done, n)
                dst = ps[:, 6, 0:DM]
                for half in range(2):
                    pe.wait_ge(ft_lo, n * 2 + (half + 1))
                    for c in (2 * half, 2 * half + 1):
                        cols = slice(c * P, (c + 1) * P)
                        high = ew[:, bass.ds(e * EW + 4 * HID + c * DM, DM)]
                        low = ew[:, bass.ds(e * EW + 6 * HID + c * DM, DM)]
                        t_.matmul(dst, fhh[:, u % 2, cols], high, start=(c == 0), stop=False)
                        t_.matmul(dst, fhh[:, u % 2, cols], low, start=False, stop=False)
                        last = t_.matmul(dst, fhl[:, u % 2, cols], high, start=False, stop=(c == 3))
                last.then_inc(fy_filled, 1)

            def expert_of(j):
                e = pe.value_load(table[0:1, 0, bass.ds(j, 1)], min_val=0, max_val=EXPERTS - 1)
                pe.wait_ge(exp_lo, e * 2 + 2)
                return e

            def beside(j):
                if j in (AT_TRANSPOSES, AT_TRANSPOSES + 1):
                    x2_transposes(last_turn, BATCHES - 1, (j - AT_TRANSPOSES,))
                if j == AT_HIDDEN:
                    router_hidden(last_turn, BATCHES - 1)
                if j == AT_LOGITS:
                    router_logits(last_turn, BATCHES - 1)
                if j == AT_SLOTS:
                    counts(last_turn, BATCHES - 1)

            def six(i, base, more):
                e = expert_of(base)
                for u in range(UNROLL):
                    j = base + u
                    if isinstance(j, int):
                        beside(j)
                    h_transposes(j, u)
                    if more or u + 1 < UNROLL:
                        after = expert_of(j + 1)
                        up(j + 1, u + 1, after)
                    if more or u + 2 < UNROLL:
                        row_transposes(j + 2, u + 2, i if u + 2 < UNROLL else i + 1)
                    down(j, u, e)
                    e = after

            pe.wait_ge(table_ready, 1)
            row_transposes(0, 0, 0)
            row_transposes(1, 1, 0)
            up(0, 0, expert_of(0))
            pe.wait_ge(drained, last_turn.upto("w2"))
            six(0, 0, True)
            six(1, UNROLL, True)
            pe.wait_ge(table_ready, 2)
            with pe.Fori(2, FT // UNROLL - 1) as i:
                six(i, i * UNROLL, True)
            six(FT // UNROLL - 1, FT - UNROLL, False)


LINKS = 19


def kernel(x, L0_tok_conv_w, L0_tok_conv_b, L0_tok_ln_gamma, L0_tok_ln_beta, L0_attn_Wq, L0_attn_Wk, L0_attn_Wv,
           L0_attn_Wo, L0_ffn_wg1, L0_ffn_bg1, L0_ffn_wg2, L0_ffn_w_in, L0_ffn_w_out):
    import numpy as np
    import concourse.bacc as bacc
    from concourse.bass_utils import run_bass_kernel_spmd

    def paired(w):
        w = np.asarray(w).reshape(2, 2, HEADS // KV, HD, -1)
        return w.transpose(0, 2, 1, 3, 4).reshape(HEADS * HD, -1)

    arrays = {
        "x": np.asarray(x).reshape(BATCHES, SEQ, 2 * DM),
        "conv_w": np.asarray(L0_tok_conv_w).transpose(2, 1, 0).reshape(2 * DM, DM),
        "conv_b": np.asarray(L0_tok_conv_b),
        "gamma": np.asarray(L0_tok_ln_gamma),
        "beta": np.asarray(L0_tok_ln_beta),
        "wq": paired(L0_attn_Wq).T,
        "wk": np.asarray(L0_attn_Wk).T,
        "wv": np.asarray(L0_attn_Wv).T,
        "wo": paired(np.asarray(L0_attn_Wo).T),
        "wg1": np.asarray(L0_ffn_wg1),
        "bg1": np.asarray(L0_ffn_bg1),
        "wg2": np.asarray(L0_ffn_wg2),
        "w_in": np.asarray(L0_ffn_w_in),
        "w_out": np.asarray(L0_ffn_w_out),
    }
    arrays = {n: np.ascontiguousarray(a) for n, a in arrays.items()}
    nc = bacc.Bacc("TRN2", target_bir_lowering=False, num_devices=1, dynamic_dma_scratch_size=8192)
    args = [nc.dram_tensor(n, a.shape, mybir.dt.from_np(a.dtype), kind="ExternalInput").ap()
            for n, a in arrays.items()]
    xs = nc.dram_tensor("expert_rows", (NOWHERE + P, ROW), F32).ap()
    ys = nc.dram_tensor("gated_rows", (TOK, TOPK * DM), F32).ap()
    out = nc.dram_tensor("out", (BATCHES, SEQ, DM), F32, kind="ExternalOutput").ap()
    rs_dram = nc.dram_tensor("sum_reciprocals", (NR, 2, QW), F32).ap()
    build(nc, *args, xs, ys, rs_dram, out)
    result = run_bass_kernel_spmd(nc, [arrays], core_ids=[0])
    return result.results[0]["out"]
```
